# Optimizing a Trainium2 kernel written in Bass

```python
import numpy as np
import jax
import jax.numpy as jnp

def _softmax(x, axis=-1):
    return jax.nn.softmax(x, axis=axis)

def _gelu(x):
    return jax.nn.gelu(x, approximate=True)

def _silu(x):
    return jax.nn.silu(x)

def _sigmoid(x):
    return jax.nn.sigmoid(x)

def _layernorm(x, axis=-1, eps=1e-05):
    m = jnp.mean(x, axis=axis, keepdims=True)
    v = jnp.var(x, axis=axis, keepdims=True)
    return (x - m) / jnp.sqrt(v + eps)

def _scatter_add(tgt, idx, src, axis=0):
    return tgt.at[idx].add(src)

def _segment_sum(src, seg, n):
    return jax.ops.segment_sum(src, seg, n)
kernel_name = 'mk_adaln_d4_jaxref_r8_7a2975'

def setup_inputs(seed: int=0):
    np.random.seed(seed)
    _w = jnp.asarray

    def _L0_attn_setup():
        import jax, jax.numpy as jnp
        import numpy as np
        import math
        D_MODEL = 128
        N_HEADS = 16
        HEAD_DIM = D_MODEL // N_HEADS
        BATCH = 2
        SEQ = 256

        def _get_slopes(n_heads):

            def p2(n):
                start = 2.0 ** (-8.0 / n)
                return [start * start ** i for i in range(n)]
            if math.log2(n_heads).is_integer():
                return jnp.asarray(p2(n_heads), dtype=jnp.float32)
            cp = 2 ** math.floor(math.log2(n_heads))
            extra = p2(2 * cp)[::2][:n_heads - cp]
            return jnp.asarray(p2(cp) + extra, dtype=jnp.float32)
        key = jax.random.key(seed)
        k1, k2, k3 = jax.random.split(key, 3)
        x = jax.random.normal(k1, (BATCH, SEQ, D_MODEL), dtype=jnp.float32)
        W_qkv = jax.random.normal(k2, (D_MODEL, 3 * D_MODEL), dtype=jnp.float32) * D_MODEL ** (-0.5)
        b_qkv = jnp.zeros((3 * D_MODEL,), dtype=jnp.float32)
        W_out = jax.random.normal(k3, (D_MODEL, D_MODEL), dtype=jnp.float32) * D_MODEL ** (-0.5)
        b_out = jnp.zeros((D_MODEL,), dtype=jnp.float32)
        return {'x': x, 'W_qkv': W_qkv, 'b_qkv': b_qkv, 'W_out': W_out, 'b_out': b_out}
    _L0_attn_in = _L0_attn_setup()

    def _L0_ffn_setup():
        import jax, jax.numpy as jnp
        import numpy as np
        D_MODEL = 128
        N_HEADS = 16
        HEAD_DIM = D_MODEL // N_HEADS
        KV_LATENT = 64
        N_EXPERTS = 4
        D_HIDDEN = 4 * D_MODEL
        B, T = (2, 128)

        def rmsnorm(x, w, eps=1e-06):
            return w * (x * jax.lax.rsqrt(jnp.mean(x * x, axis=-1, keepdims=True) + eps))

        def layernorm(x, g, b, eps=1e-05):
            mu = jnp.mean(x, axis=-1, keepdims=True)
            var = jnp.mean((x - mu) ** 2, axis=-1, keepdims=True)
            return (x - mu) * jax.lax.rsqrt(var + eps) * g + b

        def apply_rope(x):
            t, d = (x.shape[2], x.shape[3])
            half = d // 2
            pos = jnp.arange(t, dtype=x.dtype)[:, None]
            inv_freq = 1.0 / 10000.0 ** (jnp.arange(half, dtype=x.dtype) / half)
            ang = pos * inv_freq[None, :]
            sin, cos = (jnp.sin(ang), jnp.cos(ang))
            x1, x2 = (x[..., :half], x[..., half:])
            return jnp.concatenate([x1 * cos - x2 * sin, x1 * sin + x2 * cos], axis=-1)

        def mla_attention(x, Wq, Wdkv, Wuk, Wuv, Wo, ln_g, ln_b):
            b, t, _ = x.shape
            q = (x @ Wq.T).reshape(b, t, N_HEADS, HEAD_DIM).transpose(0, 2, 1, 3)
            latent = layernorm(x @ Wdkv.T, ln_g, ln_b)
            k = (latent @ Wuk.T).reshape(b, t, N_HEADS, HEAD_DIM).transpose(0, 2, 1, 3)
            v = (latent @ Wuv.T).reshape(b, t, N_HEADS, HEAD_DIM).transpose(0, 2, 1, 3)
            q = apply_rope(q)
            k = apply_rope(k)
            scores = jnp.einsum('bhqd,bhkd->bhqk', q, k) / np.sqrt(HEAD_DIM)
            causal = jnp.tril(jnp.ones((t, t), dtype=bool))
            scores = jnp.where(causal, scores, -jnp.inf)
            attn = jax.nn.softmax(scores, axis=-1)
            out = jnp.einsum('bhqk,bhkd->bhqd', attn, v).transpose(0, 2, 1, 3).reshape(b, t, D_MODEL)
            return out @ Wo.T

        def moe(x, gate_w, gate_b, W1, b1, W2, b2):
            logits = x @ gate_w.T + gate_b
            top = jnp.argmax(logits, axis=-1)
            onehot = jax.nn.one_hot(top, N_EXPERTS, dtype=x.dtype)
            h = jax.nn.relu(jnp.einsum('btd,ehd->bteh', x, W1) + b1)
            y = jnp.einsum('bteh,edh->bted', h, W2) + b2
            return jnp.einsum('bted,bte->btd', y, onehot)
        key = jax.random.key(seed)
        ks = jax.random.split(key, 16)
        s = lambda fan_in: 1.0 / np.sqrt(fan_in)
        return {'x': jax.random.normal(ks[0], (B, T, D_MODEL), jnp.float32), 'norm1_w': jnp.ones((D_MODEL,), jnp.float32), 'norm2_w': jnp.ones((D_MODEL,), jnp.float32), 'Wq': jax.random.normal(ks[1], (D_MODEL, D_MODEL), jnp.float32) * s(D_MODEL), 'Wdkv': jax.random.normal(ks[2], (KV_LATENT, D_MODEL), jnp.float32) * s(D_MODEL), 'Wuk': jax.random.normal(ks[3], (D_MODEL, KV_LATENT), jnp.float32) * s(KV_LATENT), 'Wuv': jax.random.normal(ks[4], (D_MODEL, KV_LATENT), jnp.float32) * s(KV_LATENT), 'Wo': jax.random.normal(ks[5], (D_MODEL, D_MODEL), jnp.float32) * s(D_MODEL), 'ln_g': jnp.ones((KV_LATENT,), jnp.float32), 'ln_b': jnp.zeros((KV_LATENT,), jnp.float32), 'gate_w': jax.random.normal(ks[6], (N_EXPERTS, D_MODEL), jnp.float32) * s(D_MODEL), 'gate_b': jnp.zeros((N_EXPERTS,), jnp.float32), 'W1': jax.random.normal(ks[7], (N_EXPERTS, D_HIDDEN, D_MODEL), jnp.float32) * s(D_MODEL), 'b1': jnp.zeros((N_EXPERTS, D_HIDDEN), jnp.float32), 'W2': jax.random.normal(ks[8], (N_EXPERTS, D_MODEL, D_HIDDEN), jnp.float32) * s(D_HIDDEN), 'b2': jnp.zeros((N_EXPERTS, D_MODEL), jnp.float32)}
    _L0_ffn_in = _L0_ffn_setup()
    _L0_c = _w((lambda *s: np.random.randn(*s).astype(np.float32) * 0.05)(8, 128))
    _L0_wmod = _w((lambda *s: np.random.randn(*s).astype(np.float32) * 0.05)(128, 6 * 128) * 128 ** (-0.5))

    def _L1_attn_setup():
        import jax, jax.numpy as jnp
        import numpy as np
        D_MODEL = 128
        N_HEADS = 16
        D_HEAD = D_MODEL // N_HEADS
        MIN_SPARSITY = 0.1
        key = jax.random.key(seed)
        ks = jax.random.split(key, 6)
        B, L, D = (1, 256, D_MODEL)
        w_scale = 0.02
        x = jax.random.normal(ks[0], (B, L, D), dtype=jnp.float32)
        Wq = jax.random.normal(ks[1], (D, D), dtype=jnp.float32) * w_scale
        Wk = jax.random.normal(ks[2], (D, D), dtype=jnp.float32) * w_scale
        Wv = jax.random.normal(ks[3], (D, D), dtype=jnp.float32) * w_scale
        Wo = jax.random.normal(ks[4], (D, D), dtype=jnp.float32) * w_scale
        bq = jnp.zeros((D,), jnp.float32)
        bk = jnp.zeros((D,), jnp.float32)
        bv = jnp.zeros((D,), jnp.float32)
        bo = jnp.zeros((D,), jnp.float32)
        entropy_ema = jnp.ones((N_HEADS,), jnp.float32)
        entropy_threshold = jnp.full((N_HEADS,), 2.0, jnp.float32)
        return {'x': x, 'Wq': Wq, 'bq': bq, 'Wk': Wk, 'bk': bk, 'Wv': Wv, 'bv': bv, 'Wo': Wo, 'bo': bo, 'entropy_ema': entropy_ema, 'entropy_threshold': entropy_threshold}
    _L1_attn_in = _L1_attn_setup()

    def _L1_ffn_setup():
        import jax, jax.numpy as jnp
        import numpy as np
        TOPK = 4
        key = jax.random.key(seed)
        ks = jax.random.split(key, 9)
        B, T, D = (4, 256, 128)
        E, H = (32, 128)
        HS = H * TOPK
        s = lambda k, shape, fan: jax.random.normal(k, shape, dtype=jnp.float32) / np.sqrt(fan)
        return {'x': jax.random.normal(ks[0], (B, T, D), dtype=jnp.float32), 'router_w': s(ks[1], (E, D), D), 'router_bias': jnp.zeros((E,), dtype=jnp.float32), 'gate_w': s(ks[2], (E, H, D), D), 'up_w': s(ks[3], (E, H, D), D), 'down_w': s(ks[4], (E, D, H), H), 'sgate_w': s(ks[5], (HS, D), D), 'sup_w': s(ks[6], (HS, D), D), 'sdown_w': s(ks[7], (D, HS), HS)}
    _L1_ffn_in = _L1_ffn_setup()
    _L1_c = _w((lambda *s: np.random.randn(*s).astype(np.float32) * 0.05)(8, 128))
    _L1_wmod = _w((lambda *s: np.random.randn(*s).astype(np.float32) * 0.05)(128, 6 * 128) * 128 ** (-0.5))

    def _L2_attn_setup():
        import jax, jax.numpy as jnp
        import numpy as np
        B, T, D, H = (4, 256, 128, 16)
        HD = D // H
        NEG = -np.finfo(np.float32).max
        key = jax.random.key(seed)
        ks = jax.random.split(key, 9)
        s = 1.0 / np.sqrt(D)
        return {'x': jax.random.normal(ks[0], (B, T, D), jnp.float32), 'wq': jax.random.normal(ks[1], (D, D), jnp.float32) * s, 'bq': jax.random.normal(ks[2], (D,), jnp.float32) * 0.02, 'wk': jax.random.normal(ks[3], (D, D), jnp.float32) * s, 'bk': jax.random.normal(ks[4], (D,), jnp.float32) * 0.02, 'wv': jax.random.normal(ks[5], (D, D), jnp.float32) * s, 'bv': jax.random.normal(ks[6], (D,), jnp.float32) * 0.02, 'wo': jax.random.normal(ks[7], (D, D), jnp.float32) * s, 'bo': jax.random.normal(ks[8], (D,), jnp.float32) * 0.02}
    _L2_attn_in = _L2_attn_setup()

    def _L2_ffn_setup():
        import jax, jax.numpy as jnp
        import numpy as np
        LN_EPS = 1e-05

        def entmax15(z):
            z = z / 2.0
            z = z - jnp.max(z, axis=-1, keepdims=True)
            zs = -jnp.sort(-z, axis=-1)
            k = jnp.arange(1, z.shape[-1] + 1, dtype=z.dtype)
            mean = jnp.cumsum(zs, axis=-1) / k
            meansq = jnp.cumsum(zs * zs, axis=-1) / k
            ss = k * (meansq - jnp.square(mean))
            delta = (1.0 - ss) / k
            tau = mean - jnp.sqrt(jnp.clip(delta, 0.0))
            support = jnp.sum((tau <= zs).astype(jnp.int32), axis=-1, keepdims=True)
            tau_star = jnp.take_along_axis(tau, support - 1, axis=-1)
            return jnp.square(jnp.clip(z - tau_star, 0.0))

        def layernorm_noaffine(v):
            m = jnp.mean(v, axis=-1, keepdims=True)
            var = jnp.mean(jnp.square(v - m), axis=-1, keepdims=True)
            return (v - m) / jnp.sqrt(var + LN_EPS)

        def cp_mumoe(x, gate, Win, Wout):
            ones = jnp.ones(x.shape[:-1] + (1,), x.dtype)
            xb = jnp.concatenate([x, ones], axis=-1)
            z = jnp.einsum('btd,dr->btr', xb, Win) * gate
            return jnp.einsum('btr,or->bto', z, Wout)
        key = jax.random.key(seed)
        ks = jax.random.split(key, 8)
        B, T, D, O, D2, E, R = (8, 256, 128, 512, 128, 16, 64)
        s = lambda k, shape, scale: jax.random.normal(k, shape, jnp.float32) * scale
        return {'x': s(ks[0], (B, T, D), 1.0), 'proj': s(ks[1], (D, E), D ** (-0.5)), 'C1': s(ks[2], (E, R), E ** (-0.5)), 'Win1': s(ks[3], (D + 1, R), D ** (-0.5)), 'Wout1': s(ks[4], (O, R), R ** (-0.5)), 'C2': s(ks[5], (E, R), E ** (-0.5)), 'Win2': s(ks[6], (O + 1, R), O ** (-0.5)), 'Wout2': s(ks[7], (D2, R), R ** (-0.5))}
    _L2_ffn_in = _L2_ffn_setup()
    _L2_c = _w((lambda *s: np.random.randn(*s).astype(np.float32) * 0.05)(8, 128))
    _L2_wmod = _w((lambda *s: np.random.randn(*s).astype(np.float32) * 0.05)(128, 6 * 128) * 128 ** (-0.5))

    def _L3_attn_setup():
        import jax, jax.numpy as jnp
        import numpy as np
        NUM_HEADS = 16
        DIM_HEAD = 64
        SCALE = DIM_HEAD ** (-0.5)
        ROPE_BASE = 10000.0

        def _rope(t):
            n, d = (t.shape[2], t.shape[3])
            inv_freq = 1.0 / ROPE_BASE ** (jnp.arange(0, d, 2, dtype=jnp.float32) / d)
            freqs = jnp.arange(n, dtype=jnp.float32)[:, None] * inv_freq[None, :]
            cos = jnp.concatenate([jnp.cos(freqs), jnp.cos(freqs)], axis=-1)
            sin = jnp.concatenate([jnp.sin(freqs), jnp.sin(freqs)], axis=-1)
            t1, t2 = jnp.split(t, 2, axis=-1)
            rot = jnp.concatenate([-t2, t1], axis=-1)
            return t * cos + rot * sin
        key = jax.random.key(seed)
        k1, k2, k3 = jax.random.split(key, 3)
        B, N, D = (2, 2049, 128)
        x = jax.random.normal(k1, (B, N, D), dtype=jnp.float32)
        ln_gamma = jnp.ones((D,), dtype=jnp.float32)
        ln_beta = jnp.zeros((D,), dtype=jnp.float32)
        w_qkv = jax.random.normal(k2, (D, 3 * NUM_HEADS * DIM_HEAD), dtype=jnp.float32) * 0.02
        w_out = jax.random.normal(k3, (NUM_HEADS * DIM_HEAD, D), dtype=jnp.float32) * 0.02
        return {'x': x, 'ln_gamma': ln_gamma, 'ln_beta': ln_beta, 'w_qkv': w_qkv, 'w_out': w_out}
    _L3_attn_in = _L3_attn_setup()

    def _L3_ffn_setup():
        import jax, jax.numpy as jnp
        import numpy as np
        from jax.scipy.special import logsumexp
        EPS = 1e-06
        SINKHORN_ITERS = 8
        TEMPERATURE = 1.0

        def sinkhorn(logits):
            t = jnp.log(jnp.clip(logits, EPS)) / TEMPERATURE
            for _ in range(SINKHORN_ITERS):
                t = t - logsumexp(t, axis=-2, keepdims=True)
                t = t - logsumexp(t, axis=-1, keepdims=True)
            return jnp.exp(t)
        key = jax.random.key(seed)
        k1, k2, k3 = jax.random.split(key, 3)
        b, n, d, e, h = (4, 512, 128, 8, 1)
        x = jax.random.normal(k1, (b, n, d), dtype=jnp.float32)
        gate_w = jax.random.normal(k2, (h, d, e), dtype=jnp.float32)
        experts = jax.random.normal(k3, (e, d, d), dtype=jnp.float32) * 0.02
        return {'x': x, 'gate_w': gate_w, 'experts': experts}
    _L3_ffn_in = _L3_ffn_setup()
    _L3_c = _w((lambda *s: np.random.randn(*s).astype(np.float32) * 0.05)(8, 128))
    _L3_wmod = _w((lambda *s: np.random.randn(*s).astype(np.float32) * 0.05)(128, 6 * 128) * 128 ** (-0.5))
    _d = {'L0_attn_x': _L0_attn_in['x'], 'L0_attn_W_qkv': _L0_attn_in['W_qkv'], 'L0_attn_b_qkv': _L0_attn_in['b_qkv'], 'L0_attn_W_out': _L0_attn_in['W_out'], 'L0_attn_b_out': _L0_attn_in['b_out'], 'L0_ffn_norm1_w': _L0_ffn_in['norm1_w'], 'L0_ffn_norm2_w': _L0_ffn_in['norm2_w'], 'L0_ffn_Wq': _L0_ffn_in['Wq'], 'L0_ffn_Wdkv': _L0_ffn_in['Wdkv'], 'L0_ffn_Wuk': _L0_ffn_in['Wuk'], 'L0_ffn_Wuv': _L0_ffn_in['Wuv'], 'L0_ffn_Wo': _L0_ffn_in['Wo'], 'L0_ffn_ln_g': _L0_ffn_in['ln_g'], 'L0_ffn_ln_b': _L0_ffn_in['ln_b'], 'L0_ffn_gate_w': _L0_ffn_in['gate_w'], 'L0_ffn_gate_b': _L0_ffn_in['gate_b'], 'L0_ffn_W1': _L0_ffn_in['W1'], 'L0_ffn_b1': _L0_ffn_in['b1'], 'L0_ffn_W2': _L0_ffn_in['W2'], 'L0_ffn_b2': _L0_ffn_in['b2'], 'L0_c': _L0_c, 'L0_wmod': _L0_wmod, 'L1_attn_Wq': _L1_attn_in['Wq'], 'L1_attn_bq': _L1_attn_in['bq'], 'L1_attn_Wk': _L1_attn_in['Wk'], 'L1_attn_bk': _L1_attn_in['bk'], 'L1_attn_Wv': _L1_attn_in['Wv'], 'L1_attn_bv': _L1_attn_in['bv'], 'L1_attn_Wo': _L1_attn_in['Wo'], 'L1_attn_bo': _L1_attn_in['bo'], 'L1_attn_entropy_ema': _L1_attn_in['entropy_ema'], 'L1_attn_entropy_threshold': _L1_attn_in['entropy_threshold'], 'L1_ffn_router_w': _L1_ffn_in['router_w'], 'L1_ffn_router_bias': _L1_ffn_in['router_bias'], 'L1_ffn_gate_w': _L1_ffn_in['gate_w'], 'L1_ffn_up_w': _L1_ffn_in['up_w'], 'L1_ffn_down_w': _L1_ffn_in['down_w'], 'L1_ffn_sgate_w': _L1_ffn_in['sgate_w'], 'L1_ffn_sup_w': _L1_ffn_in['sup_w'], 'L1_ffn_sdown_w': _L1_ffn_in['sdown_w'], 'L1_c': _L1_c, 'L1_wmod': _L1_wmod, 'L2_attn_wq': _L2_attn_in['wq'], 'L2_attn_bq': _L2_attn_in['bq'], 'L2_attn_wk': _L2_attn_in['wk'], 'L2_attn_bk': _L2_attn_in['bk'], 'L2_attn_wv': _L2_attn_in['wv'], 'L2_attn_bv': _L2_attn_in['bv'], 'L2_attn_wo': _L2_attn_in['wo'], 'L2_attn_bo': _L2_attn_in['bo'], 'L2_ffn_proj': _L2_ffn_in['proj'], 'L2_ffn_C1': _L2_ffn_in['C1'], 'L2_ffn_Win1': _L2_ffn_in['Win1'], 'L2_ffn_Wout1': _L2_ffn_in['Wout1'], 'L2_ffn_C2': _L2_ffn_in['C2'], 'L2_ffn_Win2': _L2_ffn_in['Win2'], 'L2_ffn_Wout2': _L2_ffn_in['Wout2'], 'L2_c': _L2_c, 'L2_wmod': _L2_wmod, 'L3_attn_ln_gamma': _L3_attn_in['ln_gamma'], 'L3_attn_ln_beta': _L3_attn_in['ln_beta'], 'L3_attn_w_qkv': _L3_attn_in['w_qkv'], 'L3_attn_w_out': _L3_attn_in['w_out'], 'L3_ffn_gate_w': _L3_ffn_in['gate_w'], 'L3_ffn_experts': _L3_ffn_in['experts'], 'L3_c': _L3_c, 'L3_wmod': _L3_wmod}
    _x0 = _d['L0_attn_x']
    _d['L0_attn_x'] = jax.random.normal(jax.random.fold_in(jax.random.key(seed), 1), (8, 256, 128), dtype=_x0.dtype)
    del _x0
    return _d

def reference(L0_attn_x, L0_attn_W_qkv, L0_attn_b_qkv, L0_attn_W_out, L0_attn_b_out, L0_ffn_norm1_w, L0_ffn_norm2_w, L0_ffn_Wq, L0_ffn_Wdkv, L0_ffn_Wuk, L0_ffn_Wuv, L0_ffn_Wo, L0_ffn_ln_g, L0_ffn_ln_b, L0_ffn_gate_w, L0_ffn_gate_b, L0_ffn_W1, L0_ffn_b1, L0_ffn_W2, L0_ffn_b2, L0_c, L0_wmod, L1_attn_Wq, L1_attn_bq, L1_attn_Wk, L1_attn_bk, L1_attn_Wv, L1_attn_bv, L1_attn_Wo, L1_attn_bo, L1_attn_entropy_ema, L1_attn_entropy_threshold, L1_ffn_router_w, L1_ffn_router_bias, L1_ffn_gate_w, L1_ffn_up_w, L1_ffn_down_w, L1_ffn_sgate_w, L1_ffn_sup_w, L1_ffn_sdown_w, L1_c, L1_wmod, L2_attn_wq, L2_attn_bq, L2_attn_wk, L2_attn_bk, L2_attn_wv, L2_attn_bv, L2_attn_wo, L2_attn_bo, L2_ffn_proj, L2_ffn_C1, L2_ffn_Win1, L2_ffn_Wout1, L2_ffn_C2, L2_ffn_Win2, L2_ffn_Wout2, L2_c, L2_wmod, L3_attn_ln_gamma, L3_attn_ln_beta, L3_attn_w_qkv, L3_attn_w_out, L3_ffn_gate_w, L3_ffn_experts, L3_c, L3_wmod):

    def _L0_attn_ref(x, W_qkv, b_qkv, W_out, b_out):
        import jax, jax.numpy as jnp
        import numpy as np
        import math
        D_MODEL = 128
        N_HEADS = 16
        HEAD_DIM = D_MODEL // N_HEADS
        BATCH = 2
        SEQ = 256

        def _get_slopes(n_heads):

            def p2(n):
                start = 2.0 ** (-8.0 / n)
                return [start * start ** i for i in range(n)]
            if math.log2(n_heads).is_integer():
                return jnp.asarray(p2(n_heads), dtype=jnp.float32)
            cp = 2 ** math.floor(math.log2(n_heads))
            extra = p2(2 * cp)[::2][:n_heads - cp]
            return jnp.asarray(p2(cp) + extra, dtype=jnp.float32)
        B, S, D = x.shape
        H, hd = (N_HEADS, HEAD_DIM)
        qkv = x @ W_qkv + b_qkv
        qkv = qkv.reshape(B, S, 3, H, hd).transpose(2, 0, 3, 1, 4)
        Q, K, V = (qkv[0], qkv[1], qkv[2])
        scores = jnp.einsum('bhqd,bhkd->bhqk', Q, K) / math.sqrt(hd)
        pos = jnp.arange(S)
        rel = pos[None, :] - pos[:, None]
        slopes = _get_slopes(H)
        alibi = slopes[:, None, None] * rel.astype(jnp.float32)
        scores = scores + alibi[None]
        causal = rel <= 0
        scores = jnp.where(causal[None, None], scores, -jnp.inf)
        attn = jax.nn.softmax(scores, axis=-1)
        out = jnp.einsum('bhqk,bhkd->bqhd', attn, V).reshape(B, S, D)
        return out @ W_out + b_out

    def _L0_ffn_ref(x, norm1_w, norm2_w, Wq, Wdkv, Wuk, Wuv, Wo, ln_g, ln_b, gate_w, gate_b, W1, b1, W2, b2):
        import jax, jax.numpy as jnp
        import numpy as np
        D_MODEL = 128
        N_HEADS = 16
        HEAD_DIM = D_MODEL // N_HEADS
        KV_LATENT = 64
        N_EXPERTS = 4
        D_HIDDEN = 4 * D_MODEL
        B, T = (2, 128)

        def rmsnorm(x, w, eps=1e-06):
            return w * (x * jax.lax.rsqrt(jnp.mean(x * x, axis=-1, keepdims=True) + eps))

        def layernorm(x, g, b, eps=1e-05):
            mu = jnp.mean(x, axis=-1, keepdims=True)
            var = jnp.mean((x - mu) ** 2, axis=-1, keepdims=True)
            return (x - mu) * jax.lax.rsqrt(var + eps) * g + b

        def apply_rope(x):
            t, d = (x.shape[2], x.shape[3])
            half = d // 2
            pos = jnp.arange(t, dtype=x.dtype)[:, None]
            inv_freq = 1.0 / 10000.0 ** (jnp.arange(half, dtype=x.dtype) / half)
            ang = pos * inv_freq[None, :]
            sin, cos = (jnp.sin(ang), jnp.cos(ang))
            x1, x2 = (x[..., :half], x[..., half:])
            return jnp.concatenate([x1 * cos - x2 * sin, x1 * sin + x2 * cos], axis=-1)

        def mla_attention(x, Wq, Wdkv, Wuk, Wuv, Wo, ln_g, ln_b):
            b, t, _ = x.shape
            q = (x @ Wq.T).reshape(b, t, N_HEADS, HEAD_DIM).transpose(0, 2, 1, 3)
            latent = layernorm(x @ Wdkv.T, ln_g, ln_b)
            k = (latent @ Wuk.T).reshape(b, t, N_HEADS, HEAD_DIM).transpose(0, 2, 1, 3)
            v = (latent @ Wuv.T).reshape(b, t, N_HEADS, HEAD_DIM).transpose(0, 2, 1, 3)
            q = apply_rope(q)
            k = apply_rope(k)
            scores = jnp.einsum('bhqd,bhkd->bhqk', q, k) / np.sqrt(HEAD_DIM)
            causal = jnp.tril(jnp.ones((t, t), dtype=bool))
            scores = jnp.where(causal, scores, -jnp.inf)
            attn = jax.nn.softmax(scores, axis=-1)
            out = jnp.einsum('bhqk,bhkd->bhqd', attn, v).transpose(0, 2, 1, 3).reshape(b, t, D_MODEL)
            return out @ Wo.T

        def moe(x, gate_w, gate_b, W1, b1, W2, b2):
            logits = x @ gate_w.T + gate_b
            top = jnp.argmax(logits, axis=-1)
            onehot = jax.nn.one_hot(top, N_EXPERTS, dtype=x.dtype)
            h = jax.nn.relu(jnp.einsum('btd,ehd->bteh', x, W1) + b1)
            y = jnp.einsum('bteh,edh->bted', h, W2) + b2
            return jnp.einsum('bted,bte->btd', y, onehot)
        x = x + mla_attention(rmsnorm(x, norm1_w), Wq, Wdkv, Wuk, Wuv, Wo, ln_g, ln_b)
        x = x + moe(rmsnorm(x, norm2_w), gate_w, gate_b, W1, b1, W2, b2)
        return x

    def _L1_attn_ref(x, Wq, bq, Wk, bk, Wv, bv, Wo, bo, entropy_ema, entropy_threshold):
        import jax, jax.numpy as jnp
        import numpy as np
        D_MODEL = 128
        N_HEADS = 16
        D_HEAD = D_MODEL // N_HEADS
        MIN_SPARSITY = 0.1
        B, L, D = x.shape
        H, dh = (N_HEADS, D_HEAD)

        def proj(W, b):
            return (x @ W.T + b).reshape(B, L, H, dh).transpose(0, 2, 1, 3)
        q, k, v = (proj(Wq, bq), proj(Wk, bk), proj(Wv, bv))
        scores = jnp.einsum('bhqd,bhkd->bhqk', q, k) / jnp.float32(np.sqrt(dh))
        attn = jax.nn.softmax(scores, axis=-1)
        sr = MIN_SPARSITY + (1.0 - MIN_SPARSITY) * jax.nn.sigmoid(entropy_ema - entropy_threshold)
        k_keep = jnp.maximum(1, (L * (1.0 - sr)).astype(jnp.int32))
        order = jnp.argsort(-attn, axis=-1)
        rank = jnp.argsort(order, axis=-1)
        keep = rank < k_keep[None, :, None, None]
        w = jnp.where(keep, attn, jnp.float32(0.0))
        w = w / (jnp.sum(w, axis=-1, keepdims=True) + 1e-10)
        out = jnp.einsum('bhqk,bhkd->bhqd', w, v)
        out = out.transpose(0, 2, 1, 3).reshape(B, L, D)
        return out @ Wo.T + bo

    def _L1_ffn_ref(x, router_w, router_bias, gate_w, up_w, down_w, sgate_w, sup_w, sdown_w):
        import jax, jax.numpy as jnp
        import numpy as np
        TOPK = 4
        B, T, D = x.shape
        flat = x.reshape(B * T, D)
        logits = flat.astype(jnp.float32) @ router_w.T + router_bias
        scores = jax.nn.softmax(logits, axis=-1)
        topk_scores, topk_idx = jax.lax.top_k(scores, TOPK)
        topk_scores = topk_scores / jnp.clip(topk_scores.sum(axis=-1, keepdims=True), 1e-12, None)
        h = jax.nn.silu(jnp.einsum('nd,ehd->neh', flat, gate_w)) * jnp.einsum('nd,ehd->neh', flat, up_w)
        expert_out = jnp.einsum('neh,edh->ned', h, down_w)
        sel = jnp.take_along_axis(expert_out, topk_idx[:, :, None], axis=1)
        out = (sel * topk_scores.astype(flat.dtype)[:, :, None]).sum(axis=1)
        out = out + jax.nn.silu(flat @ sgate_w.T) * (flat @ sup_w.T) @ sdown_w.T
        return out.reshape(B, T, D)

    def _L2_attn_ref(x, wq, bq, wk, bk, wv, bv, wo, bo):
        import jax, jax.numpy as jnp
        import numpy as np
        B, T, D, H = (4, 256, 128, 16)
        HD = D // H
        NEG = -np.finfo(np.float32).max
        b, t, d = x.shape

        def proj(w, bias):
            y = x @ w + bias
            return y.reshape(b, t, H, HD).transpose(0, 2, 1, 3)
        q = proj(wq, bq)
        k = proj(wk, bk)
        v = proj(wv, bv)
        scale = 1.0 / np.sqrt(HD).astype(np.float32)
        scores = jnp.einsum('bhqd,bhkd->bhqk', q, k) * scale
        mask = jnp.triu(jnp.full((t, t), NEG, jnp.float32), k=1)
        attn = jax.nn.softmax(scores + mask, axis=-1)
        out = jnp.einsum('bhqk,bhkd->bhqd', attn, v)
        out = out.transpose(0, 2, 1, 3).reshape(b, t, d)
        return out @ wo + bo

    def _L2_ffn_ref(x, proj, C1, Win1, Wout1, C2, Win2, Wout2):
        import jax, jax.numpy as jnp
        import numpy as np
        LN_EPS = 1e-05

        def entmax15(z):
            z = z / 2.0
            z = z - jnp.max(z, axis=-1, keepdims=True)
            zs = -jnp.sort(-z, axis=-1)
            k = jnp.arange(1, z.shape[-1] + 1, dtype=z.dtype)
            mean = jnp.cumsum(zs, axis=-1) / k
            meansq = jnp.cumsum(zs * zs, axis=-1) / k
            ss = k * (meansq - jnp.square(mean))
            delta = (1.0 - ss) / k
            tau = mean - jnp.sqrt(jnp.clip(delta, 0.0))
            support = jnp.sum((tau <= zs).astype(jnp.int32), axis=-1, keepdims=True)
            tau_star = jnp.take_along_axis(tau, support - 1, axis=-1)
            return jnp.square(jnp.clip(z - tau_star, 0.0))

        def layernorm_noaffine(v):
            m = jnp.mean(v, axis=-1, keepdims=True)
            var = jnp.mean(jnp.square(v - m), axis=-1, keepdims=True)
            return (v - m) / jnp.sqrt(var + LN_EPS)

        def cp_mumoe(x, gate, Win, Wout):
            ones = jnp.ones(x.shape[:-1] + (1,), x.dtype)
            xb = jnp.concatenate([x, ones], axis=-1)
            z = jnp.einsum('btd,dr->btr', xb, Win) * gate
            return jnp.einsum('btr,or->bto', z, Wout)
        a = entmax15(layernorm_noaffine(jnp.einsum('btd,de->bte', x, proj)))
        g1 = jnp.einsum('bte,er->btr', a, C1)
        h = cp_mumoe(x, g1, Win1, Wout1)
        h = jax.nn.gelu(h, approximate=False)
        g2 = jnp.einsum('bte,er->btr', a, C2)
        return cp_mumoe(h, g2, Win2, Wout2)

    def _L3_attn_ref(x, ln_gamma, ln_beta, w_qkv, w_out):
        import jax, jax.numpy as jnp
        import numpy as np
        NUM_HEADS = 16
        DIM_HEAD = 64
        SCALE = DIM_HEAD ** (-0.5)
        ROPE_BASE = 10000.0

        def _rope(t):
            n, d = (t.shape[2], t.shape[3])
            inv_freq = 1.0 / ROPE_BASE ** (jnp.arange(0, d, 2, dtype=jnp.float32) / d)
            freqs = jnp.arange(n, dtype=jnp.float32)[:, None] * inv_freq[None, :]
            cos = jnp.concatenate([jnp.cos(freqs), jnp.cos(freqs)], axis=-1)
            sin = jnp.concatenate([jnp.sin(freqs), jnp.sin(freqs)], axis=-1)
            t1, t2 = jnp.split(t, 2, axis=-1)
            rot = jnp.concatenate([-t2, t1], axis=-1)
            return t * cos + rot * sin
        B, N, D = x.shape
        mu = jnp.mean(x, axis=-1, keepdims=True)
        var = jnp.mean(jnp.square(x - mu), axis=-1, keepdims=True)
        xn = (x - mu) * jax.lax.rsqrt(var + 1e-05) * ln_gamma + ln_beta
        qkv = xn @ w_qkv
        q, k, v = jnp.split(qkv, 3, axis=-1)

        def to_heads(t):
            return t.reshape(B, N, NUM_HEADS, DIM_HEAD).transpose(0, 2, 1, 3)
        q, k, v = (to_heads(q), to_heads(k), to_heads(v))
        q = jnp.concatenate([q[:, :, :1, :], _rope(q[:, :, 1:, :])], axis=2)
        k = jnp.concatenate([k[:, :, :1, :], _rope(k[:, :, 1:, :])], axis=2)
        dots = jnp.einsum('bhqd,bhkd->bhqk', q, k) * SCALE
        attn = jax.nn.softmax(dots, axis=-1)
        out = jnp.einsum('bhqk,bhkd->bhqd', attn, v)
        out = out.transpose(0, 2, 1, 3).reshape(B, N, NUM_HEADS * DIM_HEAD)
        return out @ w_out

    def _L3_ffn_ref(x, gate_w, experts):
        import jax, jax.numpy as jnp
        import numpy as np
        from jax.scipy.special import logsumexp
        EPS = 1e-06
        SINKHORN_ITERS = 8
        TEMPERATURE = 1.0

        def sinkhorn(logits):
            t = jnp.log(jnp.clip(logits, EPS)) / TEMPERATURE
            for _ in range(SINKHORN_ITERS):
                t = t - logsumexp(t, axis=-2, keepdims=True)
                t = t - logsumexp(t, axis=-1, keepdims=True)
            return jnp.exp(t)
        b, n, d = x.shape
        h, _, e = gate_w.shape
        m = n // e
        xh = x[:, None]
        gate_logits = jnp.einsum('bhnd,hde->bhne', xh, gate_w)
        gates = sinkhorn(gate_logits)
        g = jnp.swapaxes(gates, -1, -2)
        gv, idx = jax.lax.top_k(g, m)
        gate_values = jnp.swapaxes(gv, -1, -2)
        routed_indices = jnp.swapaxes(idx, -1, -2)
        hard_gates = (gate_values > 0.5).astype(x.dtype)
        bi = jnp.arange(b)[:, None, None, None]
        hi = jnp.arange(h)[None, :, None, None]
        routed = xh[bi, hi, routed_indices]
        experts4 = experts[:, None, :, :]
        out = jnp.einsum('bhmei,ehio->bhmeo', routed, experts4)
        out = out * hard_gates[..., None]
        y = jnp.zeros_like(xh).at[bi, hi, routed_indices].set(out)
        return y[:, 0]
    x = L0_attn_x
    mod = (_silu(L0_c) @ L0_wmod).reshape(L0_c.shape[0], 6, 1, -1)
    sa, ca, ga, sb, cb, gb = (mod[:, 0], mod[:, 1], mod[:, 2], mod[:, 3], mod[:, 4], mod[:, 5])
    ga = (2 * (ga >= 0) - 1) * jnp.maximum(jnp.abs(ga), 0.25)
    gb = (2 * (gb >= 0) - 1) * jnp.maximum(jnp.abs(gb), 0.25)
    h = _layernorm(x, axis=-1) * (1 + ca) + sa
    x = x + ga * _L0_attn_ref(h, L0_attn_W_qkv, L0_attn_b_qkv, L0_attn_W_out, L0_attn_b_out)
    h = _layernorm(x, axis=-1) * (1 + cb) + sb
    x = x + gb * _L0_ffn_ref(h, L0_ffn_norm1_w, L0_ffn_norm2_w, L0_ffn_Wq, L0_ffn_Wdkv, L0_ffn_Wuk, L0_ffn_Wuv, L0_ffn_Wo, L0_ffn_ln_g, L0_ffn_ln_b, L0_ffn_gate_w, L0_ffn_gate_b, L0_ffn_W1, L0_ffn_b1, L0_ffn_W2, L0_ffn_b2)
    mod = (_silu(L1_c) @ L1_wmod).reshape(L1_c.shape[0], 6, 1, -1)
    sa, ca, ga, sb, cb, gb = (mod[:, 0], mod[:, 1], mod[:, 2], mod[:, 3], mod[:, 4], mod[:, 5])
    ga = (2 * (ga >= 0) - 1) * jnp.maximum(jnp.abs(ga), 0.25)
    gb = (2 * (gb >= 0) - 1) * jnp.maximum(jnp.abs(gb), 0.25)
    h = _layernorm(x, axis=-1) * (1 + ca) + sa
    x = x + ga * _L1_attn_ref(h, L1_attn_Wq, L1_attn_bq, L1_attn_Wk, L1_attn_bk, L1_attn_Wv, L1_attn_bv, L1_attn_Wo, L1_attn_bo, L1_attn_entropy_ema, L1_attn_entropy_threshold)
    h = _layernorm(x, axis=-1) * (1 + cb) + sb
    x = x + gb * _L1_ffn_ref(h, L1_ffn_router_w, L1_ffn_router_bias, L1_ffn_gate_w, L1_ffn_up_w, L1_ffn_down_w, L1_ffn_sgate_w, L1_ffn_sup_w, L1_ffn_sdown_w)
    mod = (_silu(L2_c) @ L2_wmod).reshape(L2_c.shape[0], 6, 1, -1)
    sa, ca, ga, sb, cb, gb = (mod[:, 0], mod[:, 1], mod[:, 2], mod[:, 3], mod[:, 4], mod[:, 5])
    ga = (2 * (ga >= 0) - 1) * jnp.maximum(jnp.abs(ga), 0.25)
    gb = (2 * (gb >= 0) - 1) * jnp.maximum(jnp.abs(gb), 0.25)
    h = _layernorm(x, axis=-1) * (1 + ca) + sa
    x = x + ga * _L2_attn_ref(h, L2_attn_wq, L2_attn_bq, L2_attn_wk, L2_attn_bk, L2_attn_wv, L2_attn_bv, L2_attn_wo, L2_attn_bo)
    h = _layernorm(x, axis=-1) * (1 + cb) + sb
    x = x + gb * _L2_ffn_ref(h, L2_ffn_proj, L2_ffn_C1, L2_ffn_Win1, L2_ffn_Wout1, L2_ffn_C2, L2_ffn_Win2, L2_ffn_Wout2)
    mod = (_silu(L3_c) @ L3_wmod).reshape(L3_c.shape[0], 6, 1, -1)
    sa, ca, ga, sb, cb, gb = (mod[:, 0], mod[:, 1], mod[:, 2], mod[:, 3], mod[:, 4], mod[:, 5])
    ga = (2 * (ga >= 0) - 1) * jnp.maximum(jnp.abs(ga), 0.25)
    gb = (2 * (gb >= 0) - 1) * jnp.maximum(jnp.abs(gb), 0.25)
    h = _layernorm(x, axis=-1) * (1 + ca) + sa
    x = x + ga * _L3_attn_ref(h, L3_attn_ln_gamma, L3_attn_ln_beta, L3_attn_w_qkv, L3_attn_w_out)
    h = _layernorm(x, axis=-1) * (1 + cb) + sb
    x = x + gb * _L3_ffn_ref(h, L3_ffn_gate_w, L3_ffn_experts)
    return x

_drawn_inputs = setup_inputs


def setup_inputs(seed=0):
    import zlib

    import numpy as np

    out = dict(_drawn_inputs(seed))
    spreads = {'L0_attn_b_qkv': (0.0, 0.1),
     'L0_attn_b_out': (0.0, 0.1),
     'L0_ffn_norm1_w': (1.0, 0.2),
     'L0_ffn_norm2_w': (1.0, 0.2),
     'L0_ffn_ln_g': (1.0, 0.2),
     'L0_ffn_ln_b': (0.0, 0.1),
     'L0_ffn_gate_b': (0.0, 0.1),
     'L0_ffn_b1': (0.0, 0.1),
     'L0_ffn_b2': (0.0, 0.1),
     'L1_attn_bq': (0.0, 0.1),
     'L1_attn_bk': (0.0, 0.1),
     'L1_attn_bv': (0.0, 0.1),
     'L1_attn_bo': (0.0, 0.1),
     'L1_attn_entropy_ema': (1.0, 0.2),
     'L1_attn_entropy_threshold': (2.0, 0.2),
     'L1_ffn_router_bias': (0.0, 0.1),
     'L3_attn_ln_gamma': (1.0, 0.2),
     'L3_attn_ln_beta': (0.0, 0.1)}
    factors = {}
    for name, (base, spread) in spreads.items():
        noise = np.random.default_rng([zlib.crc32(name.encode()), seed]).standard_normal(out[name].shape)
        drawn = base * np.exp(spread * noise) if base else spread * noise
        out[name] = jnp.asarray(drawn.astype(out[name].dtype))
    for name, factor in factors.items():
        out[name] = (out[name] * factor).astype(out[name].dtype)
    return out
```

```python
import numpy as np
from contextlib import ExitStack

import concourse.bass as bass
from concourse import mybir

F32 = mybir.dt.float32
BF16 = mybir.dt.bfloat16
I32 = mybir.dt.int32
ALU = mybir.AluOpType
ACT = mybir.ActivationFunctionType
AX = mybir.AxisListType

P = 128
B, S, D = 8, 256, 128
T = S // P
H = 16
HD = D // H
HPG = 4
NG = H // HPG
HD3 = 64
NG3 = H // 2
E0, C0 = 4, 4
E1, TOP1, SH1 = 32, 4, 4
EA = E1 + SH1
E2, R2, O2 = 16, 64, 4
E3 = 8
M3 = S // E3
ROUNDS3 = 8
LN_EPS, RMS_EPS = 1e-5, 1e-6
CLIP3 = 1e-6
MASKED = -1e30

SEARCH_LO = -2.0 ** -6
SEARCH_SPAN = 1.0 + 2.0 ** -5
SEARCH_STEPS = 24
LAST_STEP = SEARCH_SPAN * 2.0 ** -SEARCH_STEPS
ROWS1 = H * T
ROWS_DVE = 18
QUICK_STEPS = 6
QUICK_LO, QUICK_HI = 0.6, 0.8
UNSEEN = -10.0
LEFT = 8
QUICK_RAISES = 9
BISECT_RAISES = 5

PHASES = ["l0_attn", "l0_ffn", "l1_attn", "l1_ffn", "l2_attn", "l2_ffn", "l3_attn", "l3_ffn", "l3_out"]
WEIGHED = PHASES[:-1]

ATTN = [("wmod", 3 * D), ("wq", NG * P), ("wk", NG * P), ("wv", D), ("bq", NG), ("bk", NG),
        ("bv", D), ("wo", D), ("bo", D)]
ROPE = [("cosq", S), ("sinq", S), ("cosk", S), ("sink", S)]
COLUMNS = {
    "l0_attn": ATTN,
    "l0_ffn": [("wmod", 3 * D), ("n1", D), ("n2", D), ("wq", NG * P), ("wqr", NG * P), ("wdkv", 64),
               ("lng", 64), ("lnb", 64), ("wuk", NG * P), ("wukr", NG * P), ("wuv", D), ("wo", D),
               ("gate", E0), ("gateb", E0), ("w1", E0 * C0 * P), ("b1", E0 * C0), ("w2", E0 * C0 * D), ("b2", E0 * D)] + ROPE,
    "l1_attn": ATTN + [("ema", H), ("thr", H)],
    "l1_ffn": [("wmod", 3 * D), ("router", E1), ("routerb", E1), ("gate", EA * P), ("up", EA * P), ("down", EA * D)],
    "l2_attn": ATTN,
    "l2_ffn": [("wmod", 3 * D), ("proj", E2), ("c1", R2), ("c2", R2), ("win1", R2), ("win1b", 1),
               ("wout1", O2 * P), ("win2", O2 * R2), ("win2b", 1), ("wout2", D)],
    "l3_attn": [("wmod", 3 * D), ("gamma", D), ("beta", D), ("wqk", NG3 * 4 * P), ("wv", H * HD3), ("wo", NG3 * D)] + ROPE,
    "l3_ffn": [("wmod", 3 * D), ("gate", E3), ("experts", E3 * D)],
}
CONSTS = [("ident", P), ("qscale", 1), ("aliq", NG * P), ("alik", P), ("alipos", S),
          ("first", E0), ("order8", LEFT), ("karange", E2), ("kinv", E2), ("restart", T * E2), ("expert1", 1)]



def offsets(cols):
    at, out = 0, {}
    for name, n in cols:
        out[name] = (at, n)
        at += n
    return out, at


class Signal:

    def __init__(self, sem, per):
        self.sem, self.per = sem, per
        self.base = {}
        total = 0
        for ph in PHASES:
            self.base[ph] = total
            total += per.get(ph, 0) * B

    def __call__(self, ph, b, n):
        return b * self.per[ph] + (self.base[ph] + n)


DVE_STEPS = {"l0_attn": 20, "l0_ffn": 74, "l1_attn": 197, "l1_ffn": 40, "l2_attn": 20, "l2_ffn": 57, "l3_attn": 72, "l3_ffn": 19, "l3_out": 23}
SELECT_STEPS = 150


def adaln_program(nc, x_in, c_in, const_in, weights_in, out):
    ctx = ExitStack()
    with ctx:
        def sb(name, shape, dt=F32):
            return ctx.enter_context(nc.sbuf_tensor(name, shape, dt))

        def signal(name, **per):
            return Signal(ctx.enter_context(nc.semaphore(name)), per)

        def once(name):
            return ctx.enter_context(nc.semaphore(name))

        x = sb("x", [P, B * T, D])
        consts_at, n_const = offsets(CONSTS)
        const = sb("const", [P, n_const])

        def C(name, rows=P):
            at, n = consts_at[name]
            return const[0:rows, at:at + n]

        places = {ph: offsets(COLUMNS[ph]) for ph in WEIGHED}
        region = [sb(f"weights{i}", [P, max(places[ph][1] for ph in WEIGHED[i::2])]) for i in range(2)]

        def W(ph, name, rows=P):
            at, n = places[ph][0][name]
            return region[WEIGHED.index(ph) % 2][0:rows, at:at + n]

        silu_c = sb("silu_c", [P, 4 * B])
        silu_b = sb("silu_b", [P, P])
        ones = sb("ones", [P, P])
        identb = sb("identb", [P, P], BF16)
        future = sb("future", [P, P], BF16)
        minus_half = sb("minus_half", [P, T])
        half = sb("half", [P, T * E2])

        xb = sb("xb", [P, T, D])
        hb = sb("hb", [P, T, D])
        nb = sb("nb", [P, T, D])
        sum_b = sb("sum_b", [P, T, D])
        gate_b = sb("gate_b", [P, D])
        scale_b = sb("scale_b", [P, D])
        stats = sb("stats", [P, T, 6])
        moments = sb("moments", [P, T, 2])
        square = sb("square", [P, T])
        var = sb("var", [P, T])
        rstd = sb("rstd", [P, T])
        gap = sb("gap", [P, 1])
        feat = sb("feat", [P, T * P])
        feat_o = sb("feat_o", [P, NG3, T * P])
        qT = sb("qT", [P, NG3, S])
        kT = sb("kT", [P, NG3, S])
        rope_c = sb("rope_c", [P, S])
        rope_s = sb("rope_s", [P, S])
        V = sb("V", [P, T, H * HD3])
        nmax = sb("nmax", [P, H, T])
        rowsum = sb("rowsum", [P, H, T])
        rinv = sb("rinv", [P, H, T])
        probs = sb("probs", [P, 3, T * S])
        probsT = sb("probsT", [P, 2, T * S])
        O = sb("O", [P, T, H * HD3])
        big = sb("big", [P, ROWS1, S])
        small = [sb(f"small{i}", [P, T * E1]) for i in range(10)]
        hid = sb("hid", [P, 2, C0, T * P])
        keep, aim, low, mid, neg_mid, above, counts = (
            sb(n, [P, ROWS1]) for n in ("keep", "aim", "low", "mid", "neg_mid", "above", "counts"))
        tried, under, over = (small[i][:, 0:2 * ROWS1].rearrange("p (u j) -> p u j", u=2) for i in range(3))
        enough, short = (small[3][:, i * ROWS1:(i + 1) * ROWS1] for i in range(2))
        part, span = (small[4][:, i * ROWS1:(i + 1) * ROWS1] for i in range(2))
        left, doubt = (small[5][:, i * ROWS1:(i + 1) * ROWS1] for i in range(2))
        largest = small[6][:].rearrange("p (j e) -> p j e", e=LEFT)
        past = small[7][:].rearrange("p (j e) -> p j e", e=LEFT)
        doubts = small[8][:, 0:1]
        doubts_i = sb("doubts_i", [1, 1], I32)
        width = sb("width", [P, 1])
        keep_i = sb("keep_i", [P, H], I32)
        ones_e = sb("ones_e", [P, E1])

        def halves(buffer):
            axes = " ".join("abc"[:len(buffer.shape) - 1])
            return buffer.rearrange(f"p {axes} -> p ({axes})").bitcast(BF16).rearrange("p (j k) -> p j k", k=S)

        masks = halves(hid[:])
        spare = halves(feat_o[:])
        flags = [masks[:, j, :] for j in range(16)] + [halves(probs[:])[:, 8 + j, :] for j in range(ROWS_DVE - 16)]
        signs = [spare[:, j, :] for j in range(ROWS1 - ROWS_DVE)]
        bisect_flags = [masks[:, j, :] for j in range(16)] + [spare[:, j, :] for j in range(16)]
        candidates = hid[:].rearrange("p u c n -> p (u c) n")
        marked = feat_o[:]
        within = halves(probs[:])[:, 0:8, :]
        place = halves(O[:, 1:2, :])
        restart = halves(qT[:, NG:2 * NG, :])
        routes = sb("routes", [P, T, B, E3])
        masks3 = sb("masks3", [P, T, B, E3])
        gates_all = V[:, 0, :].rearrange("p (b d) -> p b d", b=B)
        colmax = sb("colmax", [P, T * B * E3])
        colsum = sb("colsum", [P, B, E3])
        rowsum3 = sb("rowsum3", [P, T * B])
        best = sb("best", [P, T * B])
        pb = [ctx.enter_context(nc.psum_tensor(f"bank{i}", [P, 512], F32)) for i in range(8)]

        every = dict.fromkeys(PHASES, 1)
        attn = ("l0_attn", "l0_ffn", "l1_attn", "l2_attn", "l3_attn")
        heads = dict.fromkeys(attn, H)
        n_norm = {"l0_attn": 1, "l0_ffn": 4, "l1_attn": 1, "l1_ffn": 1, "l2_attn": 1, "l2_ffn": 2, "l3_attn": 2, "l3_ffn": 1}
        n_turn = {"l0_attn": 2, "l0_ffn": 4, "l1_attn": 2, "l1_ffn": 1, "l2_attn": 2, "l2_ffn": 2, "l3_attn": 1, "l3_ffn": 1}
        n_proj = {"l0_attn": NG + 1, "l0_ffn": 2 * NG + 2, "l1_attn": NG + 1, "l2_attn": NG + 1, "l3_attn": NG3}
        x_loaded, c_loaded, const_loaded, silu_done, masks_ready, stored = map(
            once, ("x_loaded", "c_loaded", "const_loaded", "silu_done", "masks_ready", "stored"))
        fixed_ready = once("fixed_ready")
        loaded = [once(f"weights_loaded_{ph}") for ph in WEIGHED]
        pass_done = signal("pass_done", **every)
        silu_ready = signal("silu_ready", **every)
        mod_psum = signal("mod_psum", **every)
        var_ready = signal("var_ready", **n_norm)
        rstd_ready = signal("rstd_ready", **n_norm)
        tok_ready = signal("tok_ready", **n_turn)
        turned = signal("turned", **n_turn)
        feat_ready = signal("feat_ready", **n_turn)
        proj_psum = signal("proj_psum", **n_proj)
        qkv_ready = signal("qkv_ready", **n_proj)
        scores_psum = signal("scores_psum", **heads)
        max_ready = signal("max_ready", **heads)
        probs_ready = signal("probs_ready", **heads)
        probsT_psum = signal("probsT_psum", **heads)
        probsT_ready = signal("probsT_ready", **heads)
        pv_done = signal("pv_done", **heads)
        out_psum = signal("out_psum", l0_attn=1, l0_ffn=1, l1_attn=1, l2_attn=1, l2_ffn=1, l3_attn=1)
        dve_step = signal("dve_step", **DVE_STEPS)
        gate_psum = signal("gate_psum", l0_ffn=1, l1_ffn=1, l2_ffn=1, l3_ffn=1)
        gated = signal("gated", l2_ffn=1)
        hid_psum = signal("hid_psum", l0_ffn=E0 * 2, l1_ffn=EA, l2_ffn=2)
        hid_ready = signal("hid_ready", l0_ffn=E0 * 2, l1_ffn=EA, l2_ffn=2)
        silu_g = signal("silu_g", l1_ffn=EA)
        expert_psum = signal("expert_psum", l0_ffn=E0, l1_ffn=EA, l3_out=T)
        expert_used = signal("expert_used", l0_ffn=E0, l1_ffn=EA)
        keep_exp, keep_exped, keep_count = once("keep_exp"), once("keep_exped"), once("keep_count")
        mid_ready = signal("mid_ready", l1_attn=QUICK_STEPS)
        counts_act = signal("counts_act", l1_attn=QUICK_STEPS)
        quick_step = signal("quick_step", l1_attn=QUICK_STEPS * QUICK_RAISES)
        bisect_step = signal("bisect_step", l1_attn=SEARCH_STEPS * BISECT_RAISES)
        doubts_ready = signal("doubts_ready", l1_attn=1)
        doubts_psum = signal("doubts_psum", l1_attn=1)
        kept_ready = signal("kept_ready", l1_attn=4)
        max_route = signal("max_route", l1_ffn=1)
        exp_route = signal("exp_route", l1_ffn=1)
        delta_ready = signal("delta_ready", l2_ffn=1)
        root_ready = signal("root_ready", l2_ffn=1)
        z_psum = signal("z_psum", l2_ffn=2)
        z_ready = signal("z_ready", l2_ffn=2)
        v_psum = signal("v_psum", l3_attn=2)
        v_ready = signal("v_ready", l3_attn=2)
        row_ready = signal("row_ready", l3_out=1)
        sink_max, sink_next, sink_sum, sink_step = map(once, ("sink_max", "sink_next", "sink_sum", "sink_step"))
        o_ready = signal("o_ready", l3_attn=4)
        o_turned = signal("o_turned", l3_attn=4)
        o_feat = signal("o_feat", l3_attn=4)

        block = ctx.enter_context(nc.Block())

        def tiles(flat):
            return flat.rearrange("p (t n) -> p t n", t=T)

        def both(row):
            return row.unsqueeze(1).to_broadcast([P, T, row.shape[1]])

        CAUSAL = [(0, 0, 128), (1, 128, 256)]
        FULL = [(0, 0, 256), (1, 256, 256)]

        def narrow(h):
            return slice(32 * (h % HPG), 32 * (h % HPG) + 32), h // HPG

        def wide(h):
            return slice(64 * (h % 2), 64 * (h % 2) + 64), h // 2

        @block.sync
        def _(sp):
            sp.dma_start(x[:], x_in.rearrange("b (t p) d -> p (b t) d", p=P)).then_inc(x_loaded, 16)
            sp.dma_start(silu_c[:], c_in).then_inc(c_loaded, 16)
            sp.dma_start(const[:], const_in).then_inc(const_loaded, 16)
            for i, ph in enumerate(WEIGHED):
                if i >= 2:
                    sp.wait_ge(pass_done.sem, (i - 1) * B + 1)
                n = places[ph][1]
                sp.dma_start(region[i % 2][:, 0:n], weights_in[ph]).then_inc(loaded[i], 16)
            sp.wait_ge(pass_done.sem, len(PHASES) * B + 1)
            sp.dma_start(out.rearrange("b (t p) d -> p (b t) d", p=P), x[:]).then_inc(stored, 16)
            sp.wait_ge(stored, 16)

        @block.gpsimd
        def _(pool):
            nc.gpsimd.memset(identb[:], 0.0).then_inc(masks_ready, 1)
            nc.gpsimd.memset(future[:], 0.0).then_inc(masks_ready, 1)
            pool.wait_ge(masks_ready, 2)
            nc.gpsimd.affine_select(out=identb[:], in_=identb[:], compare_op=ALU.not_equal, fill=1.0, base=0,
                                    pattern=[[-1, P]], channel_multiplier=1).then_inc(masks_ready, 1)
            nc.gpsimd.affine_select(out=future[:], in_=future[:], compare_op=ALU.is_ge, fill=MASKED, base=0,
                                    pattern=[[-1, P]], channel_multiplier=1).then_inc(masks_ready, 1)
            pool.wait_ge(fixed_ready, 4)
            for ph in WEIGHED:
                with pool.Fori(0, B) as b:
                    for n in range(n_norm[ph]):
                        pool.wait_ge(var_ready.sem, var_ready(ph, b, n + 1))
                        nc.gpsimd.tensor_tensor(rstd[:], var[:], minus_half[:], ALU.pow).then_inc(rstd_ready.sem, 1)
                    if ph == "l2_ffn":
                        pool.wait_ge(delta_ready.sem, delta_ready(ph, b, 1))
                        nc.gpsimd.tensor_tensor(small[5][:, 0:T * E2], small[4][:, 0:T * E2], half[:],
                                                ALU.pow).then_inc(root_ready.sem, 1)
                if ph == "l3_ffn":
                    pool.wait_ge(pass_done.sem, pass_done("l3_out", 0, 1))
                    nc.gpsimd.partition_all_reduce(colmax[:], routes[:].rearrange("p t b e -> p (t b e)"), P,
                                                   bass.bass_isa.ReduceOp.max).then_inc(sink_max, 1)

        @block.tensor
        def _(pe):
            mm = nc.tensor.matmul

            def start_pass(ph, b):
                pe.wait_ge(pass_done.sem, pass_done(ph, b, 1))
                pe.wait_ge(silu_ready.sem, silu_ready(ph, b, 1))
                mm(pb[7][:, 0:3 * D], silu_b[:], W(ph, "wmod"), start=True, stop=True).then_inc(mod_psum.sem, 1)

            def turn(ph, b, n, src, width=P):
                pe.wait_ge(tok_ready.sem, tok_ready(ph, b, n))
                for t in range(T):
                    last = nc.tensor.transpose(pb[0][0:width, t * P:(t + 1) * P], src[:, t, :], C("ident"))
                last.then_inc(turned.sem, 1)
                pe.wait_ge(feat_ready.sem, feat_ready(ph, b, n))

            def project_narrow(ph, b):
                f = feat[:]
                for g in range(NG):
                    q = pb[2 + g][:, 0:S]
                    k = pb[2 + g][:, S:2 * S]
                    ali = ph == "l0_attn"
                    mm(q, W(ph, "wq")[:, g * P:(g + 1) * P], f, start=True, stop=not ali)
                    if ali:
                        mm(q, C("aliq", 2)[:, g * P:(g + 1) * P], C("alipos", 2), start=False, stop=True)
                    last = mm(k, W(ph, "wk")[:, g * P:(g + 1) * P], f, start=True, stop=not ali)
                    if ali:
                        last = mm(k, C("alik", 2), C("alipos", 2), start=False, stop=True)
                    last.then_inc(proj_psum.sem, 1)
                for t in range(T):
                    last = mm(pb[0][:, t * D:(t + 1) * D], f[:, t * P:(t + 1) * P], W(ph, "wv"), start=True, stop=True)
                last.then_inc(proj_psum.sem, 1)

            def scores(ph, b, h, head, blocks):
                rows, g = head(h)
                bank = pb[2 + h % 4]
                if h < 4:
                    pe.wait_ge(qkv_ready.sem, qkv_ready(ph, b, n_proj[ph]))
                else:
                    pe.wait_ge(probs_ready.sem, probs_ready(ph, b, h - 3))
                for t, at, n in blocks:
                    causal = blocks is CAUSAL
                    last = mm(bank[:, at:at + n], qT[rows, g, t * P:(t + 1) * P], kT[rows, g, 0:n],
                              start=True, stop=not causal)
                    if causal:
                        last = mm(bank[:, at + t * P:at + n], identb[:], future[:], start=False, stop=True)
                last.then_inc(scores_psum.sem, 1)

            def turn_probs(ph, b, h, src, blocks):
                if h >= 2:
                    pe.wait_ge(probsT_ready.sem, probsT_ready(ph, b, h - 1))
                for _, at, n in blocks:
                    for k in range(n // P):
                        cols = slice(at + k * P, at + (k + 1) * P)
                        last = nc.tensor.transpose(pb[6 + h % 2][:, cols], src[:, cols], C("ident"))
                last.then_inc(probsT_psum.sem, 1)

            def weigh(ph, b, h, o, v, blocks):
                pe.wait_ge(probsT_ready.sem, probsT_ready(ph, b, h + 1))
                for t, at, n in blocks:
                    for k in range(n // P):
                        last = mm(o(t), probsT[:, h % 2, at + k * P:at + (k + 1) * P], v(k),
                                  start=k == 0, stop=k == n // P - 1)
                last.then_inc(pv_done.sem, 1)

            def narrow_attention(ph, b, blocks, width=HD):
                def o(h):
                    return lambda t: pb[1][:, (t * H + h) * width:(t * H + h + 1) * width]

                def v(h):
                    return lambda k: V[:, k, h * width:(h + 1) * width]

                for s in range(H + 3):
                    if s < H:
                        scores(ph, b, s, narrow, blocks)
                    if 2 <= s < H + 2:
                        pe.wait_ge(probs_ready.sem, probs_ready(ph, b, s - 1))
                        turn_probs(ph, b, s - 2, probs[:, (s - 2) % 3, :], blocks)
                    if s >= 3:
                        weigh(ph, b, s - 3, o(s - 3), v(s - 3), blocks)

            def project_out(ph, b):
                for t in range(T):
                    last = mm(pb[0][:, t * D:(t + 1) * D], feat[:, t * P:(t + 1) * P], W(ph, "wo"), start=True, stop=True)
                last.then_inc(out_psum.sem, 1)

            def plain_attn(b, ph):
                start_pass(ph, b)
                turn(ph, b, 1, hb)
                project_narrow(ph, b)
                narrow_attention(ph, b, CAUSAL)
                turn(ph, b, 2, O[:, :, 0:D])
                project_out(ph, b)

            def l0_ffn(b, ph="l0_ffn"):
                start_pass(ph, b)
                turn(ph, b, 1, nb)
                for g in range(NG):
                    cols = slice(g * P, (g + 1) * P)
                    mm(pb[2 + g][:, 0:S], W(ph, "wq")[:, cols], feat[:], start=True, stop=True)
                    mm(pb[2 + g][:, S:2 * S], W(ph, "wqr")[:, cols], feat[:], start=True, stop=True).then_inc(proj_psum.sem, 1)
                for t in range(T):
                    last = mm(pb[1][:, t * 64:(t + 1) * 64], feat[:, t * P:(t + 1) * P], W(ph, "wdkv"), start=True, stop=True)
                last.then_inc(proj_psum.sem, 1)
                turn(ph, b, 2, nb)
                for g in range(NG):
                    pe.wait_ge(qkv_ready.sem, qkv_ready(ph, b, g + 1))
                    cols = slice(g * P, (g + 1) * P)
                    mm(pb[2 + g][:, 0:S], W(ph, "wuk", 64)[:, cols], feat[0:64, :], start=True, stop=True)
                    mm(pb[2 + g][:, S:2 * S], W(ph, "wukr", 64)[:, cols], feat[0:64, :], start=True, stop=True).then_inc(proj_psum.sem, 1)
                for t in range(T):
                    last = mm(pb[0][:, t * D:(t + 1) * D], feat[0:64, t * P:(t + 1) * P], W(ph, "wuv", 64), start=True, stop=True)
                last.then_inc(proj_psum.sem, 1)
                narrow_attention(ph, b, CAUSAL)
                turn(ph, b, 3, O[:, :, 0:D])
                project_out(ph, b)
                turn(ph, b, 4, nb)
                for t in range(T):
                    last = mm(pb[1][:, t * E0:(t + 1) * E0], feat[:, t * P:(t + 1) * P], W(ph, "gate"), start=True, stop=True)
                last.then_inc(gate_psum.sem, 1)

                def rise(e):
                    for u in range(2):
                        n = 2 * e + u
                        if n >= 4:
                            pe.wait_ge(hid_ready.sem, hid_ready(ph, b, n - 3))
                        for c in range(2):
                            at = (e * C0 + 2 * u + c) * P
                            last = mm(pb[2 + n % 4][:, c * S:(c + 1) * S], W(ph, "w1")[:, at:at + P], feat[:], start=True, stop=True)
                        last.then_inc(hid_psum.sem, 1)

                def fall(e):
                    pe.wait_ge(hid_ready.sem, hid_ready(ph, b, 2 * e + 2))
                    if e >= 2:
                        pe.wait_ge(expert_used.sem, expert_used(ph, b, e - 1))
                    for t in range(T):
                        o = pb[6 + e % 2][:, t * D:(t + 1) * D]
                        for c in range(C0):
                            at = (e * C0 + c) * D
                            mm(o, hid[:, e % 2, c, t * P:(t + 1) * P], W(ph, "w2")[:, at:at + D], start=c == 0, stop=False)
                        last = mm(o, ones[0:1, :], W(ph, "b2", 1)[:, e * D:(e + 1) * D], start=False, stop=True)
                    last.then_inc(expert_psum.sem, 1)

                for e in range(E0 + 1):
                    if e < E0:
                        rise(e)
                    if e >= 1:
                        fall(e - 1)

            def l1_attn(b, ph="l1_attn"):
                start_pass(ph, b)
                turn(ph, b, 1, hb)
                project_narrow(ph, b)
                for h in range(H):
                    scores(ph, b, h, narrow, FULL)
                pe.wait_ge(doubts_ready.sem, doubts_ready(ph, b, 1))
                mm(pb[0][0:1, 0:1], ones[:, 0:1], doubts, start=True, stop=True).then_inc(doubts_psum.sem, 1)
                width = HD + 1
                for s in range(H + 1):
                    if s < H:
                        pe.wait_ge(kept_ready.sem, kept_ready(ph, b, s // 4 + 1))
                        turn_probs(ph, b, s, big[:, 2 * s:2 * s + 2, :].rearrange("p t k -> p (t k)"), FULL)
                    if s >= 1:
                        h = s - 1
                        weigh(ph, b, h, lambda t: pb[1][:, t * 256 + h * width:t * 256 + (h + 1) * width],
                              lambda k: V[:, k, h * width:(h + 1) * width], FULL)
                turn(ph, b, 2, O[:, :, 0:D])
                project_out(ph, b)

            def l1_ffn(b, ph="l1_ffn"):
                start_pass(ph, b)
                turn(ph, b, 1, hb)
                for t in range(T):
                    last = mm(pb[1][:, t * E1:(t + 1) * E1], feat[:, t * P:(t + 1) * P], W(ph, "router"), start=True, stop=True)
                last.then_inc(gate_psum.sem, 1)

                def rise(e):
                    if e >= 4:
                        pe.wait_ge(hid_ready.sem, hid_ready(ph, b, e - 3))
                    cols = slice(e * P, (e + 1) * P)
                    mm(pb[2 + e % 4][:, 0:S], W(ph, "gate")[:, cols], feat[:], start=True, stop=True)
                    mm(pb[2 + e % 4][:, S:2 * S], W(ph, "up")[:, cols], feat[:], start=True, stop=True).then_inc(hid_psum.sem, 1)

                def fall(e):
                    pe.wait_ge(hid_ready.sem, hid_ready(ph, b, e + 1))
                    if e >= 2:
                        pe.wait_ge(expert_used.sem, expert_used(ph, b, e - 1))
                    for t in range(T):
                        last = mm(pb[6 + e % 2][:, t * D:(t + 1) * D], hid[:, e % 2, 0, t * P:(t + 1) * P],
                                  W(ph, "down")[:, e * D:(e + 1) * D], start=True, stop=True)
                    last.then_inc(expert_psum.sem, 1)

                for e in range(EA + 2):
                    if e < EA:
                        rise(e)
                    if e >= 2:
                        fall(e - 2)

            def l2_ffn(b, ph="l2_ffn"):
                start_pass(ph, b)
                turn(ph, b, 1, hb)
                for t in range(T):
                    last = mm(pb[1][:, t * E2:(t + 1) * E2], feat[:, t * P:(t + 1) * P], W(ph, "proj"), start=True, stop=True)
                last.then_inc(gate_psum.sem, 1)
                mm(pb[2][0:R2, 0:S], W(ph, "win1"), feat[:], start=True, stop=True)
                pe.wait_ge(tok_ready.sem, tok_ready(ph, b, 2))
                for t in range(T):
                    last = nc.tensor.transpose(pb[0][0:E2, t * P:(t + 1) * P], nb[:, t, 0:E2], C("ident"))
                last.then_inc(turned.sem, 1)
                pe.wait_ge(feat_ready.sem, feat_ready(ph, b, 2))
                mm(pb[3][0:R2, 0:S], W(ph, "c1", E2), feat_o[0:E2, 0, :], start=True, stop=True)
                mm(pb[3][0:R2, S:2 * S], W(ph, "c2", E2), feat_o[0:E2, 0, :], start=True, stop=True).then_inc(z_psum.sem, 1)
                pe.wait_ge(z_ready.sem, z_ready(ph, b, 1))
                for u in range(2):
                    for c in range(2):
                        at = (2 * u + c) * P
                        last = mm(pb[4 + u][:, c * S:(c + 1) * S], W(ph, "wout1", R2)[:, at:at + P], rope_c[0:R2, :], start=True, stop=True)
                    last.then_inc(hid_psum.sem, 1)
                for c in range(O2):
                    pe.wait_ge(hid_ready.sem, hid_ready(ph, b, c // 2 + 1))
                    last = mm(pb[2][0:R2, 0:S], W(ph, "win2")[:, c * R2:(c + 1) * R2], hid[:, 0, c, :], start=c == 0, stop=c == O2 - 1)
                last.then_inc(z_psum.sem, 1)
                pe.wait_ge(z_ready.sem, z_ready(ph, b, 2))
                for t in range(T):
                    last = mm(pb[0][:, t * D:(t + 1) * D], rope_s[0:R2, t * P:(t + 1) * P], W(ph, "wout2", R2), start=True, stop=True)
                last.then_inc(out_psum.sem, 1)

            def l3_attn(b, ph="l3_attn"):
                start_pass(ph, b)
                turn(ph, b, 1, nb)
                for g in range(NG3):
                    two = 2 + 2 * (g % 2)
                    if g >= 2:
                        pe.wait_ge(qkv_ready.sem, qkv_ready(ph, b, g - 1))
                    for j in range(4):
                        at = (g * 4 + j) * P
                        last = mm(pb[two + j // 2][:, (j % 2) * S:(j % 2 + 1) * S], W(ph, "wqk")[:, at:at + P], feat[:], start=True, stop=True)
                    last.then_inc(proj_psum.sem, 1)
                    if g in (1, 3):
                        t = g // 2
                        if t:
                            pe.wait_ge(v_ready.sem, v_ready(ph, b, 1))
                        for j in range(2):
                            last = mm(pb[6 + j][:], feat[:, t * P:(t + 1) * P], W(ph, "wv")[:, j * 512:(j + 1) * 512], start=True, stop=True)
                        last.then_inc(v_psum.sem, 1)
                pe.wait_ge(v_ready.sem, v_ready(ph, b, 2))
                for s in range(H + 3):
                    if s < H:
                        scores(ph, b, s, wide, FULL)
                    if 2 <= s < H + 2:
                        pe.wait_ge(probs_ready.sem, probs_ready(ph, b, s - 1))
                        turn_probs(ph, b, s - 2, probs[:, (s - 2) % 3, :], FULL)
                    if s >= 3:
                        h = s - 3
                        if h >= 8 and h % 4 == 0:
                            pe.wait_ge(o_ready.sem, o_ready(ph, b, h // 4 - 1))
                        weigh(ph, b, h, lambda t: pb[h // 4 % 2][:, (t * 4 + h % 4) * HD3:(t * 4 + h % 4 + 1) * HD3],
                              lambda k: V[:, k, h * HD3:(h + 1) * HD3], FULL)
                for u in range(4):
                    pe.wait_ge(o_ready.sem, o_ready(ph, b, u + 1))
                    for j in range(2):
                        for t in range(T):
                            g = 2 * u + j
                            last = nc.tensor.transpose(pb[2 + u][:, j * S + t * P:j * S + (t + 1) * P], O[:, t, g * P:(g + 1) * P], C("ident"))
                    last.then_inc(o_turned.sem, 1)
                pe.wait_ge(o_feat.sem, o_feat(ph, b, 4))
                for t in range(T):
                    for g in range(NG3):
                        last = mm(pb[0][:, t * D:(t + 1) * D], feat_o[:, g, t * P:(t + 1) * P], W(ph, "wo")[:, g * D:(g + 1) * D],
                                  start=g == 0, stop=g == NG3 - 1)
                last.then_inc(out_psum.sem, 1)

            def l3_ffn(b, ph="l3_ffn"):
                start_pass(ph, b)
                turn(ph, b, 1, hb)
                for t in range(T):
                    last = mm(pb[1][:, t * E3:(t + 1) * E3], feat[:, t * P:(t + 1) * P], W(ph, "gate"), start=True, stop=True)
                last.then_inc(gate_psum.sem, 1)

            def l3_route():
                for r in range(ROUNDS3):
                    pe.wait_ge(sink_next, r + 1)
                    for t in range(T):
                        last = mm(pb[0][:, 0:B * E3], ones[:], routes[:, t].rearrange("p b e -> p (b e)"), start=t == 0, stop=t == T - 1)
                    last.then_inc(sink_sum, 1)
                pe.wait_ge(sink_next, ROUNDS3 + 1)
                for t in range(T):
                    last = nc.tensor.transpose(pb[1][0:B * E3, t * P:(t + 1) * P], routes[:, t].rearrange("p b e -> p (b e)"), C("ident"))
                last.then_inc(sink_sum, 1)
                pe.wait_ge(sink_next, ROUNDS3 + 2)
                n = B * E3
                for t in range(T):
                    last = nc.tensor.transpose(pb[0][:, t * n:(t + 1) * n], qT[0:n, 2, t * P:(t + 1) * P], C("ident", n)[:, 0:n])
                last.then_inc(sink_sum, 1)

            def l3_out(b, ph="l3_out"):
                pe.wait_ge(row_ready.sem, row_ready(ph, b, 1))
                for t in range(T):
                    for j in range(2):
                        last = mm(pb[2 + 2 * t + j][:], feat[:, t * P:(t + 1) * P], W("l3_ffn", "experts")[:, j * 512:(j + 1) * 512], start=True, stop=True)
                    last.then_inc(expert_psum.sem, 1)

            pe.wait_ge(masks_ready, 4)
            pe.wait_ge(const_loaded, 16)
            pe.wait_ge(fixed_ready, 4)
            pe.wait_ge(loaded[0], 16)
            with pe.Fori(0, B) as b:
                plain_attn(b, "l0_attn")
            pe.wait_ge(loaded[1], 16)
            with pe.Fori(0, B) as b:
                l0_ffn(b)
            pe.wait_ge(loaded[2], 16)
            with pe.Fori(0, B) as b:
                l1_attn(b)
            pe.wait_ge(loaded[3], 16)
            with pe.Fori(0, B) as b:
                l1_ffn(b)
            pe.wait_ge(loaded[4], 16)
            with pe.Fori(0, B) as b:
                plain_attn(b, "l2_attn")
            pe.wait_ge(loaded[5], 16)
            with pe.Fori(0, B) as b:
                l2_ffn(b)
            pe.wait_ge(loaded[6], 16)
            with pe.Fori(0, B) as b:
                l3_attn(b)
            pe.wait_ge(loaded[7], 16)
            with pe.Fori(0, B) as b:
                l3_ffn(b)
            l3_route()
            with pe.Fori(0, B) as b:
                l3_out(b)

        @block.vector
        def _(dve):
            V_ = nc.vector
            count = [0]

            def step(ins):
                count[0] += 1
                ins.then_inc(dve_step.sem, 1)

            def settle(ph, b):
                dve.wait_ge(dve_step.sem, dve_step(ph, b, count[0]))

            def settle_apart(ph, b):
                settle(ph, b)
                step(V_.memset(gap[:], 0.0))

            def take_row(ph, b):
                count[0] = 0
                dve.wait_ge(pass_done.sem, pass_done(ph, b, 1))
                step(V_.memset(gap[:], 0.0))
                step(V_.tensor_copy(xb[:], x[:, bass.ds(b * T, T), :]))
                layer = PHASES.index(ph) // 2
                V_.tensor_copy(silu_b[:], silu_c[:, bass.ds(b + layer * B, 1)].to_broadcast([P, P])).then_inc(silu_ready.sem, 1)
                settle(ph, b)

            def put_row(ph, b):
                settle_apart(ph, b)
                V_.tensor_copy(x[:, bass.ds(b * T, T), :], xb[:]).then_inc(pass_done.sem, 1)
                assert count[0] == DVE_STEPS[ph], f"NSTEPS {ph} {count[0]}"

            def norm(ph, b, n, dst, src, eps, mean=True):
                w = src.shape[2]
                for t in range(T):
                    step(V_.bn_stats(stats[:, t, :], src[:, t, :]))
                settle_apart(ph, b)
                for t in range(T):
                    step(V_.bn_aggr(moments[:, t, :], stats[:, t, :]))
                settle(ph, b)
                spread = moments[:, :, 1]
                if not mean:
                    step(V_.tensor_tensor(square[:], moments[:, :, 0], moments[:, :, 0], ALU.mult))
                    settle(ph, b)
                    step(V_.tensor_tensor(square[:], square[:], moments[:, :, 1], ALU.add))
                    settle(ph, b)
                    spread = square[:]
                V_.tensor_scalar(var[:], spread, eps, None, ALU.add).then_inc(var_ready.sem, 1)
                dve.wait_ge(rstd_ready.sem, rstd_ready(ph, b, n))
                for t in range(T):
                    if mean:
                        step(V_.tensor_scalar(dst[:, t, 0:w], src[:, t, :], moments[:, t, 0:1], rstd[:, t:t + 1], ALU.subtract, ALU.mult))
                    else:
                        step(V_.tensor_scalar(dst[:, t, 0:w], src[:, t, :], rstd[:, t:t + 1], None, ALU.mult))
                settle(ph, b)

            def adaln(ph, b):
                norm(ph, b, 1, nb[:], xb[:], LN_EPS)
                dve.wait_ge(mod_psum.sem, mod_psum(ph, b, 1))
                shift, scale, gate = (pb[7][:, j * D:(j + 1) * D] for j in range(3))
                step(V_.tensor_scalar(scale_b[:], scale, 1.0, None, ALU.add))
                step(V_.tensor_scalar(gate_b[:], gate, -1.0, 0.25, ALU.mult, ALU.max))
                step(V_.tensor_scalar(sum_b[:, 0, :], gate, 0.0, 2.0, ALU.is_ge, ALU.mult))
                settle(ph, b)
                step(V_.tensor_tensor(gate_b[:], gate, gate_b[:], ALU.max))
                settle(ph, b)
                step(V_.scalar_tensor_tensor(gate_b[:], sum_b[:, 0, :], 1.0, gate_b[:], ALU.subtract, ALU.mult))
                step(V_.tensor_tensor(nb[:], nb[:], both(scale_b[:]), ALU.mult))
                settle(ph, b)
                return V_.tensor_tensor(hb[:], nb[:], both(shift), ALU.add)

            def add_gated(ph, b):
                settle(ph, b)
                step(V_.tensor_tensor(sum_b[:], sum_b[:], both(gate_b[:]), ALU.mult))
                settle(ph, b)
                step(V_.tensor_tensor(xb[:], xb[:], sum_b[:], ALU.add))

            def row_max(ph, b, h, blocks):
                dve.wait_ge(scores_psum.sem, scores_psum(ph, b, h + 1))
                bank = pb[2 + h % 4]
                if blocks is CAUSAL:
                    for t, at, n in blocks:
                        last = V_.tensor_reduce(nmax[:, h, t:t + 1], bank[:, at:at + n], AX.X, ALU.max, negate=True)
                else:
                    last = V_.tensor_reduce(nmax[:, h, :], tiles(bank[:]), AX.X, ALU.max, negate=True)
                last.then_inc(max_ready.sem, 1)

            def take_probsT(ph, b, h, blocks):
                n = blocks[-1][1] + blocks[-1][2]
                dve.wait_ge(probsT_psum.sem, probsT_psum(ph, b, h + 1))
                if h >= 2:
                    dve.wait_ge(pv_done.sem, pv_done(ph, b, h - 1))
                V_.tensor_copy(probsT[:, h % 2, 0:n], pb[6 + h % 2][:, 0:n]).then_inc(probsT_ready.sem, 1)

            def narrow_softmax(ph, b, blocks):
                for s in range(H + 2):
                    if s < H:
                        row_max(ph, b, s, blocks)
                    if s >= 2:
                        take_probsT(ph, b, s - 2, blocks)
                dve.wait_ge(probs_ready.sem, probs_ready(ph, b, H))
                step(V_.reciprocal(rinv[:], rowsum[:]))
                settle(ph, b)
                dve.wait_ge(pv_done.sem, pv_done(ph, b, H))
                for t in range(T):
                    last = V_.tensor_tensor(O[:, t, 0:D].rearrange("p (h d) -> p h d", h=H),
                                            pb[1][:, t * D:(t + 1) * D].rearrange("p (h d) -> p h d", h=H),
                                            rinv[:, :, t].unsqueeze(2).to_broadcast([P, H, HD]), ALU.mult)
                last.then_inc(tok_ready.sem, 1)

            def take_qk(ph, b):
                for g in range(NG):
                    dve.wait_ge(proj_psum.sem, proj_psum(ph, b, g + 1))
                    V_.tensor_scalar(qT[:, g, :], pb[2 + g][:, 0:S], W(ph, "bq")[:, g:g + 1], C("qscale"), ALU.add, ALU.mult)
                    V_.tensor_scalar(kT[:, g, :], pb[2 + g][:, S:2 * S], W(ph, "bk")[:, g:g + 1], None, ALU.add).then_inc(qkv_ready.sem, 1)
                dve.wait_ge(proj_psum.sem, proj_psum(ph, b, NG + 1))

            def plain_attn(b, ph):
                take_row(ph, b)
                adaln(ph, b).then_inc(tok_ready.sem, 1)
                take_qk(ph, b)
                V_.tensor_tensor(V[:, :, 0:D], tiles(pb[0][:, 0:T * D]), both(W(ph, "bv")), ALU.add).then_inc(qkv_ready.sem, 1)
                narrow_softmax(ph, b, CAUSAL)
                dve.wait_ge(out_psum.sem, out_psum(ph, b, 1))
                step(V_.tensor_tensor(sum_b[:], tiles(pb[0][:, 0:T * D]), both(W(ph, "bo")), ALU.add))
                add_gated(ph, b)
                put_row(ph, b)

            def rope(dst, bank, cos, sin, ph, b):
                step(V_.tensor_tensor(rope_c[:], bank[:, 0:S], W(ph, cos), ALU.mult))
                step(V_.tensor_tensor(rope_s[:], bank[:, S:2 * S], W(ph, sin), ALU.mult))
                settle(ph, b)
                return V_.tensor_tensor(dst, rope_c[:], rope_s[:], ALU.add)

            def l0_ffn(b, ph="l0_ffn"):
                take_row(ph, b)
                step(adaln(ph, b))
                settle(ph, b)
                norm(ph, b, 2, nb[:], hb[:], RMS_EPS, mean=False)
                V_.tensor_tensor(nb[:], nb[:], both(W(ph, "n1")), ALU.mult).then_inc(tok_ready.sem, 1)
                for g in range(NG):
                    dve.wait_ge(proj_psum.sem, proj_psum(ph, b, g + 1))
                    if g:
                        dve.wait_ge(qkv_ready.sem, qkv_ready(ph, b, g))
                    rope(qT[:, g, :], pb[2 + g], "cosq", "sinq", ph, b).then_inc(qkv_ready.sem, 1)
                dve.wait_ge(proj_psum.sem, proj_psum(ph, b, NG + 1))
                V_.tensor_copy(O[:, :, 0:64], pb[1][:, 0:T * 64].rearrange("p (t n) -> p t n", t=T)).then_inc(qkv_ready.sem, 1)
                dve.wait_ge(qkv_ready.sem, qkv_ready(ph, b, NG + 1))
                norm(ph, b, 3, nb[:], O[:, :, 0:64], LN_EPS)
                step(V_.tensor_tensor(nb[:, :, 0:64], nb[:, :, 0:64], both(W(ph, "lng")), ALU.mult))
                settle(ph, b)
                V_.tensor_tensor(nb[:, :, 0:64], nb[:, :, 0:64], both(W(ph, "lnb")), ALU.add).then_inc(tok_ready.sem, 1)
                for g in range(NG):
                    dve.wait_ge(proj_psum.sem, proj_psum(ph, b, NG + 2 + g))
                    if g:
                        dve.wait_ge(qkv_ready.sem, qkv_ready(ph, b, NG + 1 + g))
                    rope(kT[:, g, :], pb[2 + g], "cosk", "sink", ph, b).then_inc(qkv_ready.sem, 1)
                dve.wait_ge(proj_psum.sem, proj_psum(ph, b, 2 * NG + 2))
                V_.tensor_copy(V[:, :, 0:D], tiles(pb[0][:, 0:T * D])).then_inc(qkv_ready.sem, 1)
                narrow_softmax(ph, b, CAUSAL)
                dve.wait_ge(out_psum.sem, out_psum(ph, b, 1))
                step(V_.tensor_tensor(hb[:], hb[:], tiles(pb[0][:, 0:T * D]), ALU.add))
                settle(ph, b)
                norm(ph, b, 4, nb[:], hb[:], RMS_EPS, mean=False)
                V_.tensor_tensor(nb[:], nb[:], both(W(ph, "n2")), ALU.mult).then_inc(tok_ready.sem, 1)
                logit, order, top, pick = (small[i][:, 0:T * E0].rearrange("p (t e) -> p t e", t=T) for i in range(4))
                top1 = small[4][:, 0:T]
                every_e = top1.unsqueeze(2).to_broadcast([P, T, E0])
                dve.wait_ge(gate_psum.sem, gate_psum(ph, b, 1))
                step(V_.tensor_tensor(logit, pb[1][:, 0:T * E0].rearrange("p (t e) -> p t e", t=T), both(W(ph, "gateb")), ALU.add))
                settle(ph, b)
                step(V_.tensor_reduce(top1, logit, AX.X, ALU.max))
                settle(ph, b)
                step(V_.tensor_tensor(order, logit, every_e, ALU.is_equal))
                settle(ph, b)
                step(V_.tensor_tensor(order, order, both(C("first")), ALU.mult))
                settle(ph, b)
                step(V_.tensor_reduce(top1, order, AX.X, ALU.max))
                settle(ph, b)
                step(V_.tensor_tensor(pick, order, every_e, ALU.is_equal))
                step(V_.tensor_copy(sum_b[:], hb[:]))
                for e in range(E0):
                    dve.wait_ge(expert_psum.sem, expert_psum(ph, b, e + 1))
                    settle(ph, b)
                    for t in range(T):
                        ins = V_.scalar_tensor_tensor(sum_b[:, t, :], pb[6 + e % 2][:, t * D:(t + 1) * D], pick[:, t, e:e + 1],
                                                      sum_b[:, t, :], ALU.mult, ALU.add)
                        if t < T - 1:
                            step(ins)
                    ins.then_inc(expert_used.sem, 1)
                    dve.wait_ge(expert_used.sem, expert_used(ph, b, e + 1))
                add_gated(ph, b)
                put_row(ph, b)

            def l1_keep_counts(ph="l1_attn"):
                z, e, q, f, kf = (small[i][:, 0:H] for i in range(5))
                n = [0]

                def then(ins):
                    n[0] += 1
                    ins.then_inc(keep_count, 1)
                    dve.wait_ge(keep_count, n[0])

                then(V_.memset(restart, 1.0))
                then(V_.memset(restart[:, :, 0:1], 0.0))
                V_.tensor_tensor(z, W(ph, "ema"), W(ph, "thr"), ALU.subtract).then_inc(keep_exp, 1)
                dve.wait_ge(keep_exped, 1)
                then(V_.tensor_scalar(e, e, 1.0, None, ALU.add))
                then(V_.reciprocal(q, e))
                then(V_.tensor_scalar(q, q, 0.9, 0.1, ALU.mult, ALU.add))
                then(V_.tensor_scalar(q, q, -1.0, 1.0, ALU.mult, ALU.add))
                then(V_.tensor_scalar(q, q, float(S), None, ALU.mult))
                then(V_.tensor_copy(keep_i[:], q))
                then(V_.tensor_copy(f, keep_i[:]))
                then(V_.tensor_tensor(kf, f, q, ALU.is_gt))
                then(V_.tensor_tensor(f, f, kf, ALU.subtract))
                then(V_.tensor_scalar(f, f, 1.0, None, ALU.max))
                then(V_.tensor_copy(keep[:].rearrange("p (h t) -> p h t", t=T), f.unsqueeze(2).to_broadcast([P, H, T])))
                then(V_.tensor_scalar(aim[:], keep[:], -(LEFT + 1) / 2, None, ALU.add))

            def quick_search(ph, b):
                raised = [0]

                def then(ins, b, it):
                    raised[0] += 1
                    ins.then_inc(quick_step.sem, 1)
                    dve.wait_ge(quick_step.sem, quick_step(ph, b, raised[0]) + it * QUICK_RAISES)

                mean = rowsum[:].rearrange("p h t -> p (h t)")
                step(V_.tensor_scalar(under[:, 0, :], mean, (1 + QUICK_LO) / S, -QUICK_LO, ALU.mult, ALU.add))
                step(V_.tensor_scalar(over[:, 0, :], mean, (1 - QUICK_HI) / S, QUICK_HI, ALU.mult, ALU.add))
                step(V_.memset(under[:, 1, :], float(S)))
                step(V_.memset(over[:, 1, :], UNSEEN))
                settle_apart(ph, b)
                with dve.Fori(0, QUICK_STEPS) as it:
                    V_.tensor_tensor(span, over[:, 0, :], under[:, 0, :], ALU.subtract)
                    V_.tensor_tensor(enough, under[:, 1, :], aim[:], ALU.subtract)
                    then(V_.tensor_tensor(part, under[:, 1, :], over[:, 1, :], ALU.subtract), b, it)
                    then(V_.reciprocal(short, part), b, it)
                    then(V_.tensor_tensor(part, enough, short, ALU.mult), b, it)
                    then(V_.tensor_scalar(part, part, 0.01, 0.99, ALU.max, ALU.min), b, it)
                    then(V_.tensor_tensor(part, part, span, ALU.mult), b, it)
                    then(V_.tensor_tensor(tried[:, 0, :], under[:, 0, :], part, ALU.add), b, it)
                    V_.tensor_scalar(neg_mid[:], tried[:, 0, :], -1.0, None, ALU.mult).then_inc(mid_ready.sem, 1)
                    for j in range(ROWS_DVE):
                        last = V_.tensor_scalar(flags[j], big[:, j, :], tried[:, 0, j:j + 1], 0.0, ALU.is_gt, ALU.add,
                                                accum_out=tried[:, 1, j:j + 1])
                    dve.wait_ge(counts_act.sem, counts_act(ph, b, 1) + it)
                    then(V_.tensor_scalar(tried[:, 1, ROWS_DVE:], tried[:, 1, ROWS_DVE:], 0.5, S / 2, ALU.mult, ALU.add), b, it)
                    V_.tensor_tensor(enough, tried[:, 1, :], keep[:], ALU.is_ge)
                    then(V_.tensor_tensor(short, tried[:, 1, :], keep[:], ALU.is_lt), b, it)
                    V_.memset(gap[:], 0.0)
                    two = [P, 2, ROWS1]
                    V_.copy_predicated(under, enough.bitcast(I32).unsqueeze(1).to_broadcast(two), tried)
                    then(V_.copy_predicated(over, short.bitcast(I32).unsqueeze(1).to_broadcast(two), tried), b, it)
                assert raised[0] == QUICK_RAISES, f"QUICK {raised[0]}"
                for j in range(ROWS_DVE, ROWS1):
                    step(V_.tensor_scalar(signs[j - ROWS_DVE], big[:, j, :], over[:, 0, j:j + 1], 0.0, ALU.is_gt, ALU.add,
                                          accum_out=over[:, 1, j:j + 1]))
                settle(ph, b)
                step(V_.tensor_tensor(left, keep[:], over[:, 1, :], ALU.subtract))
                settle(ph, b)
                step(V_.tensor_scalar(doubt, left, -(LEFT + 1) / 2, None, ALU.add))
                settle(ph, b)
                step(V_.tensor_tensor(doubt, doubt, doubt, ALU.mult))
                settle(ph, b)
                V_.tensor_scalar(part, doubt, (LEFT / 2) ** 2, 0.0, ALU.is_gt, ALU.add, accum_out=doubts).then_inc(doubts_ready.sem, 1)
                dve.wait_ge(doubts_ready.sem, doubts_ready(ph, b, 1))

            def choose(ph, b):
                for u in range(4):
                    js = range(8 * u, 8 * u + 8)
                    for j in js:
                        step(V_.scalar_tensor_tensor(candidates[:, j % 8, :], big[:, j, :], over[:, 0, j:j + 1], big[:, j, :],
                                                     ALU.is_le, ALU.mult))
                    step(V_.tensor_tensor(past, C("order8").unsqueeze(1).to_broadcast([P, 8, LEFT]),
                                          left[:, 8 * u:8 * u + 8].unsqueeze(2).to_broadcast([P, 8, LEFT]), ALU.is_ge))
                    settle_apart(ph, b)
                    for j in js:
                        step(V_.max(largest[:, j % 8, :], candidates[:, j % 8, :]))
                    settle(ph, b)
                    step(V_.scalar_tensor_tensor(largest, past, 2.0, largest, ALU.mult, ALU.max))
                    settle_apart(ph, b)
                    for j in js:
                        step(V_.match_replace(marked[:, j % 8, :], largest[:, j % 8, :], candidates[:, j % 8, :], -1.0))
                    settle(ph, b)
                    for j in js:
                        last = V_.scalar_tensor_tensor(big[:, j, :], marked[:, j % 8, :], 0.0, big[:, j, :], ALU.is_le, ALU.mult)
                    last.then_inc(kept_ready.sem, 1)
                    dve.wait_ge(kept_ready.sem, kept_ready(ph, b, u + 1))

            def bisect(ph, b):
                step(V_.memset(low[:], SEARCH_LO))
                step(V_.memset(width[:], SEARCH_SPAN / 2))
                step(V_.memset(mid[:], SEARCH_LO + SEARCH_SPAN / 2))
                settle_apart(ph, b)
                raised = [0]

                def then(ins, b, it):
                    raised[0] += 1
                    ins.then_inc(bisect_step.sem, 1)
                    dve.wait_ge(bisect_step.sem, bisect_step(ph, b, raised[0]) + it * BISECT_RAISES)

                with dve.Fori(0, SEARCH_STEPS) as it:
                    for j in range(ROWS1):
                        last = V_.tensor_scalar(bisect_flags[j], big[:, j, :], mid[:, j:j + 1], 0.0, ALU.is_gt, ALU.add,
                                                accum_out=counts[:, j:j + 1])
                    then(last, b, it)
                    then(V_.tensor_tensor(above[:], counts[:], keep[:], ALU.is_ge), b, it)
                    then(V_.scalar_tensor_tensor(low[:], above[:], width[:, 0:1], low[:], ALU.mult, ALU.add), b, it)
                    then(V_.tensor_scalar(width[:], width[:], 0.5, None, ALU.mult), b, it)
                    then(V_.tensor_scalar(mid[:], low[:], width[:, 0:1], None, ALU.add), b, it)
                assert raised[0] == BISECT_RAISES, f"BISECT {raised[0]}"
                step(V_.tensor_scalar(mid[:], low[:], 2 * LAST_STEP, None, ALU.add))
                settle(ph, b)
                step(V_.tensor_scalar(low[:], low[:], -LAST_STEP, None, ALU.add))
                settle(ph, b)
                for u in range(4):
                    js = range(8 * u, 8 * u + 8)
                    for j in js:
                        step(V_.tensor_scalar(masks[:, j % 8, :], big[:, j, :], mid[:, j:j + 1], 0.0, ALU.is_gt, ALU.add,
                                              accum_out=counts[:, j:j + 1]))
                        step(V_.tensor_scalar(within[:, j % 8, :], big[:, j, :], low[:, j:j + 1], None, ALU.is_gt))
                    settle(ph, b)
                    step(V_.tensor_tensor(within, within, masks[:, 0:8, :], ALU.subtract))
                    step(V_.tensor_tensor(counts[:, 8 * u:8 * u + 8], keep[:, 8 * u:8 * u + 8], counts[:, 8 * u:8 * u + 8], ALU.subtract))
                    settle(ph, b)
                    step(V_.tensor_tensor_scan(place.rearrange("p j k -> p (j k)"), restart.rearrange("p j k -> p (j k)"),
                                               within.rearrange("p j k -> p (j k)"), 0.0, ALU.mult, ALU.add))
                    settle(ph, b)
                    for j in js:
                        step(V_.scalar_tensor_tensor(place[:, j % 8, :], place[:, j % 8, :], counts[:, j:j + 1], within[:, j % 8, :],
                                                     ALU.is_le, ALU.mult))
                    settle(ph, b)
                    step(V_.tensor_tensor(masks[:, 0:8, :], masks[:, 0:8, :], place, ALU.add))
                    settle(ph, b)
                    V_.tensor_tensor(big[:, 8 * u:8 * u + 8, :], big[:, 8 * u:8 * u + 8, :], masks[:, 0:8, :], ALU.mult).then_inc(kept_ready.sem, 1)
                    dve.wait_ge(kept_ready.sem, kept_ready(ph, b, u + 1))

            def l1_attn(b, ph="l1_attn"):
                take_row(ph, b)
                adaln(ph, b).then_inc(tok_ready.sem, 1)
                take_qk(ph, b)
                v1 = V[:, :, 0:H * (HD + 1)].rearrange("p t (h d) -> p t h d", h=H)
                step(V_.memset(V[:, :, 0:H * (HD + 1)], 1.0))
                settle(ph, b)
                for t in range(T):
                    last = V_.tensor_tensor(v1[:, t, :, 0:HD], pb[0][:, t * D:(t + 1) * D].rearrange("p (h d) -> p h d", h=H),
                                            W(ph, "bv").rearrange("p (h d) -> p h d", h=H), ALU.add)
                last.then_inc(qkv_ready.sem, 1)
                for h in range(H):
                    row_max(ph, b, h, FULL)
                dve.wait_ge(probs_ready.sem, probs_ready(ph, b, H))
                quick_search(ph, b)
                dve.wait_ge(doubts_psum.sem, doubts_psum(ph, b, 1))
                step(V_.tensor_copy(doubts_i[:], pb[0][0:1, 0:1]))
                settle_apart(ph, b)
                found = dve.value_load(doubts_i[:], min_val=0, max_val=P * ROWS1)
                start = count[0]
                with dve.If(found > 0):
                    bisect(ph, b)
                    dve.sem_inc(dve_step.sem, start + SELECT_STEPS - count[0])
                slow = count[0]
                count[0] = start
                with dve.Else():
                    choose(ph, b)
                    dve.sem_inc(dve_step.sem, start + SELECT_STEPS - count[0])
                    dve.sem_inc(bisect_step.sem, SEARCH_STEPS * BISECT_RAISES)
                assert max(slow, count[0]) < start + SELECT_STEPS, f"SELECT {slow - start} {count[0] - start}"
                count[0] = start + SELECT_STEPS
                dve.wait_ge(pv_done.sem, pv_done(ph, b, H))
                for t in range(T):
                    o1 = pb[1][:, t * 256:t * 256 + H * (HD + 1)].rearrange("p (h d) -> p h d", h=H)
                    step(V_.scalar_tensor_tensor(rinv[:, :, t], rowsum[:, :, t], 1e-10, o1[:, :, HD], ALU.mult, ALU.add))
                settle(ph, b)
                step(V_.reciprocal(nmax[:], rinv[:]))
                settle(ph, b)
                for t in range(T):
                    o1 = pb[1][:, t * 256:t * 256 + H * (HD + 1)].rearrange("p (h d) -> p h d", h=H)
                    last = V_.tensor_tensor(O[:, t, 0:D].rearrange("p (h d) -> p h d", h=H), o1[:, :, 0:HD],
                                            nmax[:, :, t].unsqueeze(2).to_broadcast([P, H, HD]), ALU.mult)
                last.then_inc(tok_ready.sem, 1)
                dve.wait_ge(out_psum.sem, out_psum(ph, b, 1))
                step(V_.tensor_tensor(sum_b[:], tiles(pb[0][:, 0:T * D]), both(W(ph, "bo")), ALU.add))
                add_gated(ph, b)
                put_row(ph, b)

            def l1_ffn(b, ph="l1_ffn"):
                take_row(ph, b)
                adaln(ph, b).then_inc(tok_ready.sem, 1)
                score, prob, most, tied = (small[i][:, 0:T * E1].rearrange("p (t e) -> p t e", t=T) for i in range(4))
                rank = small[4][:, 0:T * E1].rearrange("p (t e) -> p t e", t=T)
                one, total, top8 = small[5][:, 0:T], small[6][:, 0:T], small[7][:, 0:T * 8].rearrange("p (t e) -> p t e", t=T)
                weight = small[8][:].rearrange("p (t e) -> p t e", t=T)
                spread = lambda v: v.unsqueeze(2).to_broadcast([P, T, E1])
                dve.wait_ge(gate_psum.sem, gate_psum(ph, b, 1))
                step(V_.tensor_tensor(score, pb[1][:, 0:T * E1].rearrange("p (t e) -> p t e", t=T), both(W(ph, "routerb")), ALU.add))
                settle(ph, b)
                step(V_.tensor_reduce(one, score, AX.X, ALU.max))
                settle(ph, b)
                V_.tensor_tensor(score, score, spread(one), ALU.subtract).then_inc(max_route.sem, 1)
                dve.wait_ge(exp_route.sem, exp_route(ph, b, 1))
                step(V_.tensor_reduce(one, prob, AX.X, ALU.add))
                settle(ph, b)
                step(V_.reciprocal(total, one))
                settle(ph, b)
                step(V_.tensor_tensor(score, prob, spread(total), ALU.mult))
                settle_apart(ph, b)
                for t in range(T):
                    step(V_.max(top8[:, t, :], score[:, t, :]))
                settle(ph, b)
                fourth = top8[:, :, TOP1 - 1:TOP1].to_broadcast([P, T, E1])
                step(V_.tensor_tensor(most, score, fourth, ALU.is_gt))
                step(V_.tensor_tensor(tied, score, fourth, ALU.is_equal))
                settle(ph, b)
                step(V_.tensor_reduce(one, most, AX.X, ALU.add))
                for t in range(T):
                    step(V_.tensor_tensor_scan(rank[:, t, :], ones_e[:], tied[:, t, :], 0.0, ALU.mult, ALU.add))
                settle(ph, b)
                step(V_.tensor_scalar(one, one, -1.0, float(TOP1), ALU.mult, ALU.add))
                settle(ph, b)
                step(V_.tensor_tensor(rank, rank, spread(one), ALU.is_le))
                settle(ph, b)
                step(V_.tensor_tensor(tied, tied, rank, ALU.mult))
                settle(ph, b)
                step(V_.tensor_tensor(most, most, tied, ALU.add))
                settle(ph, b)
                step(V_.tensor_tensor(score, score, most, ALU.mult))
                settle(ph, b)
                step(V_.tensor_reduce(one, score, AX.X, ALU.add))
                settle(ph, b)
                step(V_.tensor_scalar(one, one, 1e-12, None, ALU.max))
                settle(ph, b)
                step(V_.reciprocal(total, one))
                settle(ph, b)
                step(V_.tensor_tensor(weight, score, spread(total), ALU.mult))
                settle(ph, b)

                def rise(e):
                    dve.wait_ge(silu_g.sem, silu_g(ph, b, e + 1))
                    if e >= 2:
                        dve.wait_ge(expert_psum.sem, expert_psum(ph, b, e - 1))
                    V_.tensor_tensor(hid[:, e % 2, 0, :], hid[:, e % 2, 1, :], pb[2 + e % 4][:, S:2 * S], ALU.mult).then_inc(hid_ready.sem, 1)

                def fall(e):
                    dve.wait_ge(expert_psum.sem, expert_psum(ph, b, e + 1))
                    if e:
                        dve.wait_ge(expert_used.sem, expert_used(ph, b, e))
                    down = pb[6 + e % 2]
                    if e == 0:
                        for t in range(T):
                            last = V_.tensor_scalar(sum_b[:, t, :], down[:, t * D:(t + 1) * D], weight[:, t, e:e + 1], None, ALU.mult)
                    elif e < E1:
                        for t in range(T):
                            last = V_.scalar_tensor_tensor(sum_b[:, t, :], down[:, t * D:(t + 1) * D], weight[:, t, e:e + 1],
                                                           sum_b[:, t, :], ALU.mult, ALU.add)
                    else:
                        last = V_.tensor_tensor(sum_b[:], sum_b[:], tiles(down[:, 0:T * D]), ALU.add)
                    last.then_inc(expert_used.sem, 1)

                for e in range(EA + 2):
                    if e < EA:
                        rise(e)
                    if e >= 2:
                        fall(e - 2)
                dve.wait_ge(expert_used.sem, expert_used(ph, b, EA))
                add_gated(ph, b)
                put_row(ph, b)

            def l2_ffn(b, ph="l2_ffn"):
                take_row(ph, b)
                adaln(ph, b).then_inc(tok_ready.sem, 1)
                view = lambda i: small[i][:, 0:T * E2].rearrange("p (t e) -> p t e", t=T)
                z, zs, rest, mean, tau, a = view(0), view(1), view(2), view(3), view(6), view(7)
                flat = lambda i: small[i][:, 0:T * E2]
                one = small[8][:, 0:T]
                spread = one.unsqueeze(2).to_broadcast([P, T, E2])
                dve.wait_ge(gate_psum.sem, gate_psum(ph, b, 1))
                step(V_.tensor_copy(a, pb[1][:, 0:T * E2].rearrange("p (t e) -> p t e", t=T)))
                settle(ph, b)
                norm(ph, b, 2, z, a, LN_EPS)
                step(V_.tensor_scalar(z, z, 0.5, None, ALU.mult))
                settle(ph, b)
                step(V_.tensor_reduce(one, z, AX.X, ALU.max))
                settle(ph, b)
                step(V_.tensor_tensor(z, z, spread, ALU.subtract))
                settle_apart(ph, b)
                for t in range(T):
                    step(V_.max(zs[:, t, 0:8], z[:, t, :]))
                settle_apart(ph, b)
                for t in range(T):
                    step(V_.match_replace(rest[:, t, :], zs[:, t, 0:8], z[:, t, :], MASKED))
                settle_apart(ph, b)
                for t in range(T):
                    step(V_.max(zs[:, t, 8:16], rest[:, t, :]))
                settle(ph, b)
                step(V_.tensor_tensor_scan(flat(3), C("restart"), flat(1), 0.0, ALU.mult, ALU.add))
                step(V_.tensor_tensor(rest, zs, zs, ALU.mult))
                settle(ph, b)
                step(V_.tensor_tensor_scan(flat(4), C("restart"), flat(2), 0.0, ALU.mult, ALU.add))
                step(V_.tensor_tensor(mean, mean, both(C("kinv")), ALU.mult))
                settle(ph, b)
                meansq = view(4)
                step(V_.tensor_tensor(meansq, meansq, both(C("kinv")), ALU.mult))
                step(V_.tensor_tensor(rest, mean, mean, ALU.mult))
                settle(ph, b)
                step(V_.tensor_tensor(meansq, meansq, rest, ALU.subtract))
                settle(ph, b)
                step(V_.tensor_tensor(meansq, meansq, both(C("karange")), ALU.mult))
                settle(ph, b)
                step(V_.tensor_scalar(meansq, meansq, -1.0, 1.0, ALU.mult, ALU.add))
                settle(ph, b)
                step(V_.tensor_tensor(meansq, meansq, both(C("kinv")), ALU.mult))
                settle(ph, b)
                V_.tensor_scalar(meansq, meansq, 0.0, None, ALU.max).then_inc(delta_ready.sem, 1)
                dve.wait_ge(root_ready.sem, root_ready(ph, b, 1))
                step(V_.tensor_tensor(tau, mean, view(5), ALU.subtract))
                settle(ph, b)
                step(V_.tensor_tensor(rest, tau, zs, ALU.is_le))
                settle(ph, b)
                step(V_.tensor_reduce(one, rest, AX.X, ALU.add))
                settle(ph, b)
                step(V_.tensor_tensor(rest, both(C("karange")), spread, ALU.is_equal))
                settle(ph, b)
                step(V_.tensor_tensor(rest, rest, tau, ALU.mult))
                settle(ph, b)
                step(V_.tensor_reduce(one, rest, AX.X, ALU.add))
                settle(ph, b)
                step(V_.tensor_tensor(z, z, spread, ALU.subtract))
                settle(ph, b)
                step(V_.tensor_scalar(z, z, 0.0, None, ALU.max))
                settle(ph, b)
                V_.tensor_tensor(nb[:, :, 0:E2], z, z, ALU.mult).then_inc(tok_ready.sem, 1)
                dve.wait_ge(gated.sem, gated(ph, b, 1))
                V_.scalar_tensor_tensor(rope_c[0:R2, :], pb[2][0:R2, 0:S], W(ph, "win1b", R2), feat_o[0:R2, 1, :], ALU.add, ALU.mult).then_inc(z_ready.sem, 1)
                dve.wait_ge(z_psum.sem, z_psum(ph, b, 2))
                V_.scalar_tensor_tensor(rope_s[0:R2, :], pb[2][0:R2, 0:S], W(ph, "win2b", R2), feat_o[0:R2, 2, :], ALU.add, ALU.mult).then_inc(z_ready.sem, 1)
                dve.wait_ge(out_psum.sem, out_psum(ph, b, 1))
                step(V_.tensor_copy(sum_b[:], tiles(pb[0][:, 0:T * D])))
                add_gated(ph, b)
                put_row(ph, b)

            def l3_attn(b, ph="l3_attn"):
                take_row(ph, b)
                step(adaln(ph, b))
                settle(ph, b)
                norm(ph, b, 2, nb[:], hb[:], LN_EPS)
                step(V_.tensor_tensor(nb[:], nb[:], both(W(ph, "gamma")), ALU.mult))
                settle(ph, b)
                V_.tensor_tensor(nb[:], nb[:], both(W(ph, "beta")), ALU.add).then_inc(tok_ready.sem, 1)
                for g in range(NG3):
                    dve.wait_ge(proj_psum.sem, proj_psum(ph, b, g + 1))
                    two = 2 + 2 * (g % 2)
                    if g:
                        dve.wait_ge(qkv_ready.sem, qkv_ready(ph, b, g))
                    step(rope(qT[:, g, :], pb[two], "cosq", "sinq", ph, b))
                    settle(ph, b)
                    rope(kT[:, g, :], pb[two + 1], "cosk", "sink", ph, b).then_inc(qkv_ready.sem, 1)
                for s in range(H + 3):
                    if s < H:
                        row_max(ph, b, s, FULL)
                    if 2 <= s < H + 2:
                        take_probsT(ph, b, s - 2, FULL)
                    if s >= 3 and (s - 3) % 4 == 3:
                        u = (s - 3) // 4
                        hs = slice(4 * u, 4 * u + 4)
                        dve.wait_ge(pv_done.sem, pv_done(ph, b, 4 * u + 4))
                        step(V_.reciprocal(rinv[:, hs, :], rowsum[:, hs, :]))
                        settle(ph, b)
                        for t in range(T):
                            last = V_.tensor_tensor(O[:, t, 4 * u * HD3:(4 * u + 4) * HD3].rearrange("p (h d) -> p h d", h=4),
                                                    pb[u % 2][:, t * 256:(t + 1) * 256].rearrange("p (h d) -> p h d", h=4),
                                                    rinv[:, hs, t].unsqueeze(2).to_broadcast([P, 4, HD3]), ALU.mult)
                        last.then_inc(o_ready.sem, 1)
                dve.wait_ge(out_psum.sem, out_psum(ph, b, 1))
                step(V_.tensor_copy(sum_b[:], tiles(pb[0][:, 0:T * D])))
                add_gated(ph, b)
                put_row(ph, b)

            def l3_ffn(b, ph="l3_ffn"):
                take_row(ph, b)
                adaln(ph, b).then_inc(tok_ready.sem, 1)
                dve.wait_ge(gate_psum.sem, gate_psum(ph, b, 1))
                step(V_.tensor_scalar(small[0][:, 0:T * E3], pb[1][:, 0:T * E3], CLIP3, None, ALU.max))
                settle(ph, b)
                step(V_.memset(gap[:], 0.0))
                step(V_.tensor_copy(routes[:, :, bass.ds(b, 1), :], small[0][:, 0:T * E3].rearrange("p (t o e) -> p t o e", t=T, o=1)))
                step(V_.tensor_copy(big[:, bass.ds(b, 1), :], feat[:].unsqueeze(1)))
                V_.tensor_copy(gates_all[:, bass.ds(b, 1), :], gate_b[:].unsqueeze(1)).then_inc(pass_done.sem, 1)
                assert count[0] == DVE_STEPS[ph], f"NSTEPS {ph} {count[0]}"

            def l3_route():
                n = [0]

                def then(ins):
                    n[0] += 1
                    ins.then_inc(sink_step, 1)
                    dve.wait_ge(sink_step, n[0])

                over_t = lambda v: v.unsqueeze(1).to_broadcast([P, T, B * E3])
                cols = routes[:].rearrange("p t b e -> p t (b e)")
                rows = routes[:].rearrange("p t b e -> p (t b) e")
                cs = colsum[:].rearrange("p b e -> p (b e)")
                over_e = lambda v: v.unsqueeze(2).to_broadcast([P, T * B, E3])
                dve.wait_ge(sink_max, 1)
                then(V_.tensor_tensor(cs, colmax[:, 0:B * E3], colmax[:, B * E3:], ALU.max))
                then(V_.reciprocal(colmax[:, 0:B * E3], cs))
                V_.tensor_tensor(cols, cols, over_t(colmax[:, 0:B * E3]), ALU.mult).then_inc(sink_next, 1)
                for r in range(ROUNDS3):
                    dve.wait_ge(sink_sum, r + 1)
                    then(V_.reciprocal(cs, pb[0][:, 0:B * E3]))
                    then(V_.tensor_tensor(cols, cols, over_t(cs), ALU.mult))
                    then(V_.tensor_reduce(rowsum3[:], rows, AX.X, ALU.add))
                    then(V_.reciprocal(best[:], rowsum3[:]))
                    V_.tensor_tensor(rows, rows, over_e(best[:]), ALU.mult).then_inc(sink_next, 1)
                R = B * E3
                gate, work, key, strict, seen, same, run, one = (qT[0:R, i, :] for i in range(8))
                top = small[9][0:R, 0:M3]
                dve.wait_ge(sink_sum, ROUNDS3 + 1)
                then(V_.tensor_copy(gate, pb[1][0:R, 0:S]))
                then(V_.memset(one, 1.0))
                then(V_.memset(strict, 0.0))
                then(V_.memset(seen, 0.0))
                src, other = gate, [work, key]
                for i in range(M3 // 8):
                    then(V_.max(top[:, 8 * i:8 * i + 8], src))
                    then(V_.match_replace(other[i % 2], top[:, 8 * i:8 * i + 8], src, -1.0))
                    src = other[i % 2]
                for m in range(M3):
                    v = top[:, m:m + 1]
                    then(V_.scalar_tensor_tensor(strict, gate, v, strict, ALU.is_lt, ALU.add))
                    then(V_.tensor_scalar(same, gate, v, None, ALU.is_equal))
                    then(V_.tensor_tensor_scan(run, one, same, 0.0, ALU.mult, ALU.add))
                    then(V_.tensor_tensor(run, run, same, ALU.mult))
                    then(V_.tensor_tensor(seen, seen, run, ALU.max))
                then(V_.tensor_tensor(strict, strict, seen, ALU.add))
                then(V_.tensor_scalar(same, src, 0.0, None, ALU.is_lt))
                then(V_.tensor_scalar(strict, strict, float(E3), -float(E3), ALU.mult, ALU.add))
                V_.scalar_tensor_tensor(key, strict, C("expert1", R), same, ALU.add, ALU.mult).then_inc(sink_next, 1)
                dve.wait_ge(sink_sum, ROUNDS3 + 2)
                keys = masks3[:].rearrange("p t b e -> p (t b) e")
                won = colmax[:].rearrange("p (r e) -> p r e", e=E3)
                then(V_.tensor_copy(masks3[:].rearrange("p t b e -> p (t b e)"), pb[0][:, 0:T * R]))
                then(V_.tensor_reduce(best[:], keys, AX.X, ALU.max))
                then(V_.tensor_tensor(won, keys, over_e(best[:]), ALU.is_equal))
                then(V_.tensor_scalar(keys, keys, 0.0, None, ALU.is_gt))
                then(V_.tensor_tensor(won, won, keys, ALU.mult))
                then(V_.tensor_scalar(rows, rows, 0.5, None, ALU.is_gt))
                then(V_.tensor_tensor(keys, won, rows, ALU.mult))

            def l3_out(b, ph="l3_out"):
                count[0] = 0
                dve.wait_ge(pass_done.sem, pass_done(ph, b, 1))
                step(V_.memset(gap[:], 0.0))
                step(V_.tensor_copy(xb[:], x[:, bass.ds(b * T, T), :]))
                step(V_.tensor_copy(gate_b[:].unsqueeze(1), gates_all[:, bass.ds(b, 1), :]))
                step(V_.tensor_copy(small[0][:, 0:T * E3].rearrange("p (t o e) -> p t o e", t=T, o=1), masks3[:, :, bass.ds(b, 1), :]))
                V_.tensor_copy(feat[:].unsqueeze(1), big[:, bass.ds(b, 1), :]).then_inc(row_ready.sem, 1)
                settle(ph, b)
                for t in range(T):
                    dve.wait_ge(expert_psum.sem, expert_psum(ph, b, t + 1))
                for e in range(E3):
                    for t in range(T):
                        o = pb[2 + 2 * t + e // 4][:, e % 4 * D:(e % 4 + 1) * D]
                        w = small[0][:, t * E3 + e:t * E3 + e + 1]
                        if e == 0:
                            step(V_.tensor_scalar(sum_b[:, t, :], o, w, None, ALU.mult))
                        else:
                            step(V_.scalar_tensor_tensor(sum_b[:, t, :], o, w, sum_b[:, t, :], ALU.mult, ALU.add))
                    settle(ph, b)
                add_gated(ph, b)
                put_row(ph, b)

            V_.memset(ones[:], 1.0).then_inc(fixed_ready, 1)
            V_.memset(ones_e[:], 1.0).then_inc(fixed_ready, 1)
            V_.memset(minus_half[:], -0.5).then_inc(fixed_ready, 1)
            V_.memset(half[:], 0.5).then_inc(fixed_ready, 1)
            dve.wait_ge(fixed_ready, 4)
            dve.wait_ge(x_loaded, 16)
            dve.wait_ge(silu_done, 1)
            dve.wait_ge(const_loaded, 16)
            V_.memset(gap[:], 0.0).then_inc(pass_done.sem, 1)
            dve.wait_ge(loaded[0], 16)
            with dve.Fori(0, B) as b:
                plain_attn(b, "l0_attn")
            dve.wait_ge(loaded[1], 16)
            with dve.Fori(0, B) as b:
                l0_ffn(b)
            dve.wait_ge(loaded[2], 16)
            l1_keep_counts()
            with dve.Fori(0, B) as b:
                l1_attn(b)
            dve.wait_ge(loaded[3], 16)
            with dve.Fori(0, B) as b:
                l1_ffn(b)
            dve.wait_ge(loaded[4], 16)
            with dve.Fori(0, B) as b:
                plain_attn(b, "l2_attn")
            dve.wait_ge(loaded[5], 16)
            with dve.Fori(0, B) as b:
                l2_ffn(b)
            dve.wait_ge(loaded[6], 16)
            with dve.Fori(0, B) as b:
                l3_attn(b)
            dve.wait_ge(loaded[7], 16)
            with dve.Fori(0, B) as b:
                l3_ffn(b)
            l3_route()
            with dve.Fori(0, B) as b:
                l3_out(b)

        @block.scalar
        def _(act):
            def take_turn(ph, b, n, width=P, dst=None):
                act.wait_ge(turned.sem, turned(ph, b, n))
                nc.scalar.activation(feat[0:width, :] if dst is None else dst, pb[0][0:width, 0:T * P], ACT.Copy).then_inc(feat_ready.sem, 1)

            def exps(ph, b, blocks):
                for h in range(H):
                    act.wait_ge(max_ready.sem, max_ready(ph, b, h + 1))
                    if h >= 3:
                        act.wait_ge(probsT_psum.sem, probsT_psum(ph, b, h - 2))
                    for t, at, n in blocks:
                        last = nc.scalar.activation(probs[:, h % 3, at:at + n], pb[2 + h % 4][:, at:at + n], ACT.Exp,
                                                    bias=nmax[:, h, t:t + 1], accum_out=rowsum[:, h, t:t + 1])
                    last.then_inc(probs_ready.sem, 1)

            def plain_attn(b, ph):
                take_turn(ph, b, 1)
                exps(ph, b, CAUSAL)
                take_turn(ph, b, 2)

            def l0_ffn(b, ph="l0_ffn"):
                take_turn(ph, b, 1)
                take_turn(ph, b, 2, 64)
                exps(ph, b, CAUSAL)
                take_turn(ph, b, 3)
                take_turn(ph, b, 4)
                for n in range(2 * E0):
                    e, u = n // 2, n % 2
                    act.wait_ge(hid_psum.sem, hid_psum(ph, b, n + 1))
                    if e >= 2:
                        act.wait_ge(expert_psum.sem, expert_psum(ph, b, e - 1))
                    for c in range(2):
                        at = e * C0 + 2 * u + c
                        last = nc.scalar.activation(hid[:, e % 2, 2 * u + c, :], pb[2 + n % 4][:, c * S:(c + 1) * S], ACT.Relu,
                                                    bias=W(ph, "b1")[:, at:at + 1])
                    last.then_inc(hid_ready.sem, 1)

            def l1_attn(b, ph="l1_attn"):
                take_turn(ph, b, 1)
                for h in range(H):
                    act.wait_ge(max_ready.sem, max_ready(ph, b, h + 1))
                    for t in range(T):
                        last = nc.scalar.activation(big[:, h * T + t, :], pb[2 + h % 4][:, t * S:(t + 1) * S], ACT.Exp,
                                                    bias=nmax[:, h, t:t + 1], accum_out=rowsum[:, h, t:t + 1])
                    last.then_inc(probs_ready.sem, 1)
                with act.Fori(0, QUICK_STEPS) as it:
                    act.wait_ge(mid_ready.sem, mid_ready(ph, b, 1) + it)
                    for j in range(ROWS_DVE, ROWS1):
                        last = nc.scalar.activation(signs[j - ROWS_DVE], big[:, j, :], ACT.Sign, bias=neg_mid[:, j:j + 1],
                                                    accum_out=tried[:, 1, j:j + 1])
                    last.then_inc(counts_act.sem, 1)
                for h in range(H):
                    act.wait_ge(probsT_psum.sem, probsT_psum(ph, b, h + 1))
                    if h >= 2:
                        act.wait_ge(pv_done.sem, pv_done(ph, b, h - 1))
                    nc.scalar.activation(probsT[:, h % 2, :], pb[6 + h % 2][:], ACT.Copy).then_inc(probsT_ready.sem, 1)
                take_turn(ph, b, 2)

            def l1_ffn(b, ph="l1_ffn"):
                take_turn(ph, b, 1)
                act.wait_ge(max_route.sem, max_route(ph, b, 1))
                nc.scalar.activation(small[1][:, 0:T * E1], small[0][:, 0:T * E1], ACT.Exp).then_inc(exp_route.sem, 1)
                for e in range(EA):
                    act.wait_ge(hid_psum.sem, hid_psum(ph, b, e + 1))
                    if e >= 2:
                        act.wait_ge(hid_ready.sem, hid_ready(ph, b, e - 1))
                    nc.scalar.activation(hid[:, e % 2, 1, :], pb[2 + e % 4][:, 0:S], ACT.Silu).then_inc(silu_g.sem, 1)

            def l2_ffn(b, ph="l2_ffn"):
                take_turn(ph, b, 1)
                take_turn(ph, b, 2, E2, feat_o[0:E2, 0, :])
                act.wait_ge(z_psum.sem, z_psum(ph, b, 1))
                nc.scalar.activation(feat_o[0:R2, 1:3, :], pb[3][0:R2, :].rearrange("p (u n) -> p u n", u=2), ACT.Copy).then_inc(gated.sem, 1)
                for u in range(2):
                    act.wait_ge(hid_psum.sem, hid_psum(ph, b, u + 1))
                    nc.scalar.activation(hid[:, 0, 2 * u:2 * u + 2, :], pb[4 + u][:].rearrange("p (c n) -> p c n", c=2), ACT.Gelu).then_inc(hid_ready.sem, 1)

            def l3_attn(b, ph="l3_attn"):
                take_turn(ph, b, 1)
                for t in range(T):
                    act.wait_ge(v_psum.sem, v_psum(ph, b, t + 1))
                    for j in range(2):
                        last = nc.scalar.activation(V[:, t, j * 512:(j + 1) * 512], pb[6 + j][:], ACT.Copy)
                    last.then_inc(v_ready.sem, 1)
                exps(ph, b, FULL)
                for u in range(4):
                    act.wait_ge(o_turned.sem, o_turned(ph, b, u + 1))
                    nc.scalar.activation(feat_o[:, 2 * u:2 * u + 2, :], pb[2 + u][:].rearrange("p (c n) -> p c n", c=2), ACT.Copy).then_inc(o_feat.sem, 1)

            act.wait_ge(c_loaded, 16)
            nc.scalar.activation(silu_c[:], silu_c[:], ACT.Silu).then_inc(silu_done, 1)
            with act.Fori(0, B) as b:
                plain_attn(b, "l0_attn")
            act.wait_ge(loaded[1], 16)
            with act.Fori(0, B) as b:
                l0_ffn(b)
            act.wait_ge(keep_exp, 1)
            nc.scalar.activation(small[1][:, 0:H], small[0][:, 0:H], ACT.Exp, scale=-1.0).then_inc(keep_exped, 1)
            with act.Fori(0, B) as b:
                l1_attn(b)
            with act.Fori(0, B) as b:
                l1_ffn(b)
            with act.Fori(0, B) as b:
                plain_attn(b, "l2_attn")
            with act.Fori(0, B) as b:
                l2_ffn(b)
            with act.Fori(0, B) as b:
                l3_attn(b)
            with act.Fori(0, B) as b:
                take_turn("l3_ffn", b, 1)


def shape_constants():
    out = {"ident": np.eye(P)}
    row = np.arange(P)
    dim = row % 32
    out["qscale"] = np.where(dim < HD, HD ** -0.5, 1.0)[:, None]
    slopes = 2.0 ** (-8.0 / H * (np.arange(H) + 1))
    aliq, alik, alipos = np.zeros((P, NG, HPG, 32)), np.zeros((P, HPG, 32)), np.zeros((P, S))
    aliq[0, :, :, HD] = slopes.reshape(NG, HPG)
    aliq[1, :, :, HD + 1] = -slopes.reshape(NG, HPG)
    alipos[0], alipos[1] = 1.0, np.arange(S)
    alik[1, :, HD], alik[0, :, HD + 1] = 1.0, 1.0
    out["aliq"], out["alik"], out["alipos"] = aliq.reshape(P, -1), alik.reshape(P, -1), alipos
    out["first"] = np.tile(np.arange(E0, 0, -1.0), (P, 1))
    out["order8"] = np.tile(np.arange(LEFT), (P, 1))
    k = np.arange(1, E2 + 1)
    out["karange"], out["kinv"] = np.tile(k, (P, 1)), np.tile(1.0 / k, (P, 1))
    out["restart"] = np.tile(k > 1, (P, T))
    out["expert1"] = (row % E3 + 1)[:, None]
    return out


def rope_tables(angle, dim, half, scale):
    inside = dim >= 0
    sign = np.where(dim % (2 * half) < half, -1.0, 1.0)[:, None]
    cos, sin = np.cos(angle) * inside[:, None], np.sin(angle) * sign * inside[:, None]
    return {"cosq": cos * scale, "sinq": sin * scale, "cosk": cos, "sink": sin}


def rope_small():
    dim = np.arange(P) % 32
    inv = (1.0 / 10000.0 ** (np.arange(HD // 2, dtype=np.float32) / np.float32(HD // 2))).astype(np.float32)
    angle = (np.arange(S, dtype=np.float32)[None, :] * inv[dim % (HD // 2)][:, None]).astype(np.float64)
    return rope_tables(angle, np.where(dim < HD, dim, -1), HD // 2, HD ** -0.5)


def rope_wide():
    dim = np.arange(P) % HD3
    inv = (1.0 / np.float32(10000.0) ** (np.arange(0, HD3, 2, dtype=np.float32) / HD3)).astype(np.float32)
    pos = np.maximum(np.arange(S) - 1, 0).astype(np.float32)
    angle = (pos[None, :] * inv[dim % (HD3 // 2)][:, None]).astype(np.float64)
    return rope_tables(angle, dim, HD3 // 2, HD3 ** -0.5)


def blocks_of_32(w):
    out = np.zeros((w.shape[0], H, 32), np.float32)
    out[:, :, :HD] = w.reshape(-1, H, HD)
    return out.reshape(w.shape[0], -1)


def columns(v):
    return blocks_of_32(v[None, :]).reshape(NG, P).T


def swap_halves(w, width):
    n = w.shape[0]
    return w.reshape(n, -1, 2, width // 2)[:, :, ::-1].reshape(n, -1)


def everywhere(v):
    return np.broadcast_to(v[None, :], (P, v.shape[0]))


def laid_out(a):
    attn0 = lambda wq, wk, wv, bq, bk, bv, wo, bo: {
        "wq": blocks_of_32(wq), "wk": blocks_of_32(wk), "wv": wv, "bq": columns(bq), "bk": columns(bk),
        "bv": everywhere(bv), "wo": wo, "bo": everywhere(bo)}
    w, b = a["L0_attn_W_qkv"], a["L0_attn_b_qkv"]
    out = {"l0_attn": attn0(w[:, :D], w[:, D:2 * D], w[:, 2 * D:], b[:D], b[D:2 * D], b[2 * D:], a["L0_attn_W_out"], a["L0_attn_b_out"])}
    f = lambda n: a["L0_ffn_" + n]
    out["l0_ffn"] = {
        "n1": everywhere(f("norm1_w")), "n2": everywhere(f("norm2_w")),
        "wq": blocks_of_32(f("Wq").T), "wqr": blocks_of_32(swap_halves(f("Wq").T, HD)), "wdkv": f("Wdkv").T,
        "lng": everywhere(f("ln_g")), "lnb": everywhere(f("ln_b")),
        "wuk": blocks_of_32(f("Wuk").T), "wukr": blocks_of_32(swap_halves(f("Wuk").T, HD)), "wuv": f("Wuv").T, "wo": f("Wo").T,
        "gate": f("gate_w").T, "gateb": everywhere(f("gate_b")),
        "w1": f("W1").transpose(2, 0, 1).reshape(D, -1), "b1": f("b1").reshape(E0 * C0, P).T,
        "w2": f("W2").reshape(E0, D, C0, P).transpose(3, 0, 2, 1).reshape(P, -1), "b2": f("b2").reshape(1, -1)}
    f = lambda n: a["L1_attn_" + n]
    out["l1_attn"] = attn0(f("Wq").T, f("Wk").T, f("Wv").T, f("bq"), f("bk"), f("bv"), f("Wo").T, f("bo"))
    out["l1_attn"].update(ema=everywhere(f("entropy_ema")), thr=everywhere(f("entropy_threshold")))
    f = lambda n: a["L1_ffn_" + n]
    out["l1_ffn"] = {
        "router": f("router_w").T, "routerb": everywhere(f("router_bias")),
        "gate": np.concatenate([f("gate_w").transpose(2, 0, 1).reshape(D, -1), f("sgate_w").T], 1),
        "up": np.concatenate([f("up_w").transpose(2, 0, 1).reshape(D, -1), f("sup_w").T], 1),
        "down": np.concatenate([f("down_w").transpose(2, 0, 1).reshape(P, -1),
                                f("sdown_w").reshape(D, SH1, P).transpose(2, 1, 0).reshape(P, -1)], 1)}
    f = lambda n: a["L2_attn_" + n]
    out["l2_attn"] = attn0(f("wq"), f("wk"), f("wv"), f("bq"), f("bk"), f("bv"), f("wo"), f("bo"))
    f = lambda n: a["L2_ffn_" + n]
    out["l2_ffn"] = {
        "proj": f("proj"), "c1": f("C1"), "c2": f("C2"), "win1": f("Win1")[:D], "win1b": f("Win1")[D:].T,
        "wout1": f("Wout1").T, "win2": f("Win2")[:O2 * P].reshape(O2, P, R2).transpose(1, 0, 2).reshape(P, -1),
        "win2b": f("Win2")[O2 * P:].T, "wout2": f("Wout2").T}
    w = a["L3_attn_w_qkv"]
    n = H * HD3
    four = [w[:, :n], swap_halves(w[:, :n], HD3), w[:, n:2 * n], swap_halves(w[:, n:2 * n], HD3)]
    out["l3_attn"] = {
        "gamma": everywhere(a["L3_attn_ln_gamma"]), "beta": everywhere(a["L3_attn_ln_beta"]),
        "wqk": np.stack([v.reshape(D, NG3, P) for v in four], 2).reshape(D, -1), "wv": w[:, 2 * n:],
        "wo": a["L3_attn_w_out"].reshape(NG3, P, D).transpose(1, 0, 2).reshape(P, -1)}
    out["l3_ffn"] = {"gate": a["L3_ffn_gate_w"][0], "experts": a["L3_ffn_experts"].transpose(1, 0, 2).reshape(D, -1)}
    for i, ph in enumerate(WEIGHED):
        half = a[f"L{i // 2}_wmod"]
        out[ph]["wmod"] = half[:, :3 * D] if i % 2 == 0 else half[:, 3 * D:]
    out["l0_ffn"].update(rope_small())
    out["l3_attn"].update(rope_wide())
    return out


def side_by_side(cols, parts):
    at, n = offsets(cols)
    out = np.zeros((P, n), np.float32)
    for name, (first, width) in at.items():
        part = parts[name]
        assert part.shape[1] == width, (name, part.shape, width)
        out[:part.shape[0], first:first + width] = part
    return out


def kernel(**inputs):
    import concourse.bacc as bacc
    from concourse.bass_utils import run_bass_kernel_spmd

    a = {k: np.asarray(v) for k, v in inputs.items()}
    arrays = {"x": np.ascontiguousarray(a["L0_attn_x"]),
              "c": np.ascontiguousarray(np.stack([a[f"L{i}_c"] for i in range(4)]).reshape(4 * B, D).T),
              "const": side_by_side(CONSTS, shape_constants())}
    weights = laid_out(a)
    for ph in WEIGHED:
        arrays["weights_" + ph] = side_by_side(COLUMNS[ph], weights[ph])
    nc = bacc.Bacc("TRN2", target_bir_lowering=False, num_devices=1)
    dram = {k: nc.dram_tensor("in_" + k, v.shape, F32, kind="ExternalInput").ap() for k, v in arrays.items()}
    out = nc.dram_tensor("out", (B, S, D), F32, kind="ExternalOutput").ap()
    adaln_program(nc, dram["x"], dram["c"], dram["const"], {ph: dram["weights_" + ph] for ph in WEIGHED}, out)
    r = run_bass_kernel_spmd(nc, [{"in_" + k: v for k, v in arrays.items()}], core_ids=[0])
    return r.results[0]["out"]
```

```python
import numpy as np
from contextlib import ExitStack

import concourse.bass as bass
from concourse import mybir

F32 = mybir.dt.float32
BF16 = mybir.dt.bfloat16
I32 = mybir.dt.int32
ALU = mybir.AluOpType
ACT = mybir.ActivationFunctionType
AX = mybir.AxisListType

P = 128
B, S, D = 8, 256, 128
T = S // P
H = 16
HD = D // H
HPG = 2
NG = H // HPG
PARTS = 3
SLOTS = [(0, 0), (1, 0), (2, 0), (0, 1), (1, 1), (0, 2)]
ALI_ROWS = 2 * PARTS
HALF = NG // 2
EXPANDS = HPG * len(SLOTS)
HD3 = 64
NG3 = H // 2
E0, C0 = 4, 4
E1, TOP1, SH1 = 32, 4, 4
EA = E1 + SH1
E2, R2, O2 = 16, 64, 4
E3 = 8
M3 = S // E3
ROUNDS3 = 8
LN_EPS, RMS_EPS = 1e-5, 1e-6
CLIP3 = 1e-6
MASKED = -1e30

SEARCH_LO = -2.0 ** -6
SEARCH_SPAN = 1.0 + 2.0 ** -5
SEARCH_STEPS = 24
LAST_STEP = SEARCH_SPAN * 2.0 ** -SEARCH_STEPS
ROWS1 = H * T
ROWS_DVE = 18
QUICK_STEPS = 5
QUICK_LO, QUICK_HI = 0.5, 0.6
UNSEEN = -10.0
LEFT = 8
QUICK_RAISES = 8
BISECT_RAISES = 5

PHASES = ["l0_attn", "l0_ffn", "l1_attn", "l1_ffn", "l2_attn", "l2_ffn", "l3_attn", "l3_ffn", "l3_out"]
WEIGHED = PHASES[:-1]

ATTN = [("wmod", 3 * D), ("wq", D), ("wk", D), ("wv", D), ("bq", 1), ("bk", 1),
        ("bv", D), ("wo", D), ("bo", D)]
ROPE = [("cosq", S), ("sinq", S), ("cosk", S), ("sink", S)]
COLUMNS = {
    "l0_attn": ATTN,
    "l0_ffn": [("wmod", 3 * D), ("n1", D), ("n2", D), ("wq", D), ("wqr", D), ("wdkv", 64),
               ("lng", 64), ("lnb", 64), ("wuk", D), ("wukr", D), ("wuv", D), ("wo", D),
               ("gate", E0), ("gateb", E0), ("w1", E0 * C0 * P), ("b1", E0 * C0), ("w2", E0 * C0 * D), ("b2", E0 * D)] + ROPE,
    "l1_attn": ATTN + [("ema", H), ("thr", H)],
    "l1_ffn": [("wmod", 3 * D), ("router", E1), ("routerb", E1), ("gate", EA * P), ("up", EA * P), ("down", EA * D)],
    "l2_attn": ATTN,
    "l2_ffn": [("wmod", 3 * D), ("proj", E2), ("c1", R2), ("c2", R2), ("win1", R2), ("win1b", 1),
               ("wout1", O2 * P), ("win2", O2 * R2), ("win2b", 1), ("wout2", D)],
    "l3_attn": [("wmod", 3 * D), ("gamma", D), ("beta", D), ("wqk", NG3 * 4 * P), ("wv", H * HD3), ("wo", NG3 * D)] + ROPE,
    "l3_ffn": [("wmod", 3 * D), ("gate", E3), ("experts", E3 * D)],
}
CONSTS = [("ident", P), 
          ("first", E0), ("order8", LEFT), ("karange", E2), ("kinv", E2), ("restart", T * E2), ("expert1", 1)]



def offsets(cols):
    at, out = 0, {}
    for name, n in cols:
        out[name] = (at, n)
        at += n
    return out, at


class Signal:

    def __init__(self, sem, per):
        self.sem, self.per = sem, per
        self.base = {}
        total = 0
        for ph in PHASES:
            self.base[ph] = total
            total += per.get(ph, 0) * B

    def __call__(self, ph, b, n):
        return b * self.per[ph] + (self.base[ph] + n)


DVE_STEPS = {"l0_attn": 4, "l0_ffn": 25, "l1_attn": 181, "l1_ffn": 40, "l2_attn": 4, "l2_ffn": 57, "l3_attn": 7, "l3_ffn": 19, "l3_out": 23}
FRONT_STEPS = {"l0_attn": 20, "l0_ffn": 41, "l1_attn": 20, "l2_attn": 20, "l3_attn": 64}
SELECT_STEPS = 150


def adaln_program(nc, x_in, c_in, const_in, ali_in, weights_in, out):
    ctx = ExitStack()
    with ctx:
        def sb(name, shape, dt=F32):
            return ctx.enter_context(nc.sbuf_tensor(name, shape, dt))

        def signal(name, **per):
            return Signal(ctx.enter_context(nc.semaphore(name)), per)

        def once(name):
            return ctx.enter_context(nc.semaphore(name))

        x = sb("x", [P, B * T, D])
        consts_at, n_const = offsets(CONSTS)
        const = sb("const", [P, n_const])

        def C(name, rows=P):
            at, n = consts_at[name]
            return const[0:rows, at:at + n]

        places = {ph: offsets(COLUMNS[ph]) for ph in WEIGHED}
        region = [sb(f"weights{i}", [P, max(places[ph][1] for ph in WEIGHED[i::2])]) for i in range(2)]

        def W(ph, name, rows=P):
            at, n = places[ph][0][name]
            return region[WEIGHED.index(ph) % 2][0:rows, at:at + n]

        silu_c = sb("silu_c", [P, 4 * B])
        silu_b = sb("silu_b", [P, P])
        ones = sb("ones", [P, P])
        identb = sb("identb", [P, P], BF16)
        future = sb("future", [P, P], BF16)
        minus_half = sb("minus_half", [P, T])
        half = sb("half", [P, T * E2])

        xb = sb("xb", [P, T, D])
        hb = sb("hb", [P, T, D])
        nb = sb("nb", [P, T, D])
        sum_b = sb("sum_b", [P, T, D])
        gate_b = sb("gate_b", [P, D])
        next_gate_b = sb("next_gate_b", [P, D])
        gate_sign = sb("gate_sign", [P, D])
        next_feat = sb("next_feat", [P, T * P])
        scale_b = sb("scale_b", [P, D])
        stats = sb("stats", [P, T, 6])
        moments = sb("moments", [P, T, 2])
        square = sb("square", [P, T])
        var = sb("var", [P, T])
        rstd = sb("rstd", [P, T])
        gap = sb("gap", [P, 1])
        main_stats = sb("main_stats", [P, T, 6])
        main_moments = sb("main_moments", [P, T, 2])
        main_square = sb("main_square", [P, T])
        main_var = sb("main_var", [P, T])
        main_rstd = sb("main_rstd", [P, T])
        front_n = sb("front_n", [P, T, D])
        feat = sb("feat", [P, T * P])
        feat_o = sb("feat_o", [P, NG3, T * P])
        qT = sb("qT", [P, NG3, S])
        kT = sb("kT", [P, NG3, S])
        rope_c = sb("rope_c", [P, S])
        rope_s = sb("rope_s", [P, S])
        V = sb("V", [P, T, H * HD3])
        nmax = sb("nmax", [P, H, T])
        rowsum = sb("rowsum", [P, H, T])
        rinv = sb("rinv", [P, H, T])
        probs = sb("probs", [P, 3, T * S])
        probsT = sb("probsT", [P, 2, T * S])
        O = sb("O", [P, T, H * HD3])
        big = sb("big", [P, ROWS1, S])
        small = [sb(f"small{i}", [P, T * E1]) for i in range(10)]
        hid = sb("hid", [P, 2, C0, T * P])
        keep, aim, low, mid, neg_mid, above, counts = (
            sb(n, [P, ROWS1]) for n in ("keep", "aim", "low", "mid", "neg_mid", "above", "counts"))
        tried, under, over = (small[i][:, 0:2 * ROWS1].rearrange("p (u j) -> p u j", u=2) for i in range(3))
        enough, short = (small[3][:, i * ROWS1:(i + 1) * ROWS1] for i in range(2))
        part, span = (small[4][:, i * ROWS1:(i + 1) * ROWS1] for i in range(2))
        left, doubt = (small[5][:, i * ROWS1:(i + 1) * ROWS1] for i in range(2))
        largest = small[6][:].rearrange("p (j e) -> p j e", e=LEFT)
        past = small[7][:].rearrange("p (j e) -> p j e", e=LEFT)
        doubts = small[8][:, 0:1]
        rkept = small[9][:, 0:H * T].rearrange("p (h t) -> p h t", t=T)
        doubts_i = sb("doubts_i", [1, 1], I32)
        width = sb("width", [P, 1])
        keep_i = sb("keep_i", [P, H], I32)
        ones_e = sb("ones_e", [P, E1])

        def halves(buffer):
            axes = " ".join("abc"[:len(buffer.shape) - 1])
            return buffer.rearrange(f"p {axes} -> p ({axes})").bitcast(BF16).rearrange("p (j k) -> p j k", k=S)

        masks = halves(hid[:])
        spare = halves(feat_o[:])
        flags = [masks[:, j, :] for j in range(16)] + [halves(probs[:])[:, 8 + j, :] for j in range(ROWS_DVE - 16)]
        signs = [spare[:, j, :] for j in range(ROWS1 - ROWS_DVE)]
        bisect_flags = [masks[:, j, :] for j in range(16)] + [spare[:, j, :] for j in range(16)]
        candidates = hid[:].rearrange("p u c n -> p (u c) n")
        marked = feat_o[:]
        within = halves(probs[:])[:, 0:8, :]
        place = halves(O[:, 1:2, :])
        restart = halves(kT[:, 0:NG3 // 2, :])
        stack = halves(qT[:]).rearrange("p (g side) n -> p g side n", side=2)
        compact, rest = kT[:, 4:6, :], kT[:, 6:8, :]
        parts = sb("parts", [P, 2 * PARTS, S], BF16)

        def pair(rows, of_query, of_key):
            first, last = PARTS - 1 - of_query, PARTS + of_key
            return parts[rows, first:last + 1:last - first, :]

        routes = sb("routes", [P, T, B, E3])
        masks3 = sb("masks3", [P, T, B, E3])
        gates_all = V[:, 0, :].rearrange("p (b d) -> p b d", b=B)
        colmax = sb("colmax", [P, T * B * E3])
        colsum = sb("colsum", [P, B, E3])
        rowsum3 = sb("rowsum3", [P, T * B])
        best = sb("best", [P, T * B])
        pb = [ctx.enter_context(nc.psum_tensor(f"bank{i}", [P, 512], F32)) for i in range(8)]

        every = dict.fromkeys(PHASES, 1)
        attn = ("l0_attn", "l0_ffn", "l1_attn", "l2_attn", "l3_attn")
        heads = dict.fromkeys(attn, H)
        n_norm = {"l0_attn": 0, "l0_ffn": 1, "l1_attn": 0, "l1_ffn": 1, "l2_attn": 0, "l2_ffn": 2, "l3_attn": 0, "l3_ffn": 1}
        n_turn = {"l0_attn": 1, "l0_ffn": 2, "l1_attn": 1, "l1_ffn": 1, "l2_attn": 1, "l2_ffn": 2, "l3_attn": 0, "l3_ffn": 1}
        narrow_phases = ("l0_attn", "l0_ffn", "l1_attn", "l2_attn")
        n_proj = {"l0_attn": 2, "l0_ffn": 4, "l1_attn": 2, "l2_attn": 2, "l3_attn": NG3}
        n_qkv = {**n_proj, "l0_ffn": 3}
        x_loaded, c_loaded, const_loaded, silu_done, masks_ready, stored = map(
            once, ("x_loaded", "c_loaded", "const_loaded", "silu_done", "masks_ready", "stored"))
        fixed_ready = once("fixed_ready")
        loaded = [once(f"weights_loaded_{ph}") for ph in WEIGHED]
        pass_done = signal("pass_done", **every)
        unled = {ph: 1 for ph in PHASES if ph not in FRONT_STEPS}
        silu_ready = signal("silu_ready", **unled)
        mod_psum = signal("mod_psum", **unled)
        var_ready = signal("var_ready", **n_norm)
        rstd_ready = signal("rstd_ready", **n_norm)
        tok_ready = signal("tok_ready", **n_turn)
        turned = signal("turned", **n_turn)
        feat_ready = signal("feat_ready", **n_turn)
        proj_psum = signal("proj_psum", **n_proj)
        qkv_ready = signal("qkv_ready", **n_qkv)
        parts_ready = signal("parts_ready", **dict.fromkeys(narrow_phases, 1))
        stacked = [signal(f"stacked_half{u}", **dict.fromkeys(narrow_phases, 16 * EXPANDS)) for u in range(2)]
        ali_loaded, stacks_clear = once("ali_loaded"), once("stacks_clear")
        scores_psum = signal("scores_psum", **heads)
        max_ready = signal("max_ready", **heads)
        probs_ready = signal("probs_ready", **heads)
        probsT_psum = signal("probsT_psum", **heads)
        probsT_ready = signal("probsT_ready", **heads)
        pv_done = signal("pv_done", **heads)
        out_psum = signal("out_psum", l0_attn=1, l0_ffn=1, l1_attn=1, l2_attn=1, l2_ffn=1, l3_attn=1)
        dve_step = signal("dve_step", **DVE_STEPS)
        led = dict.fromkeys(FRONT_STEPS, 1)
        front_step = signal("front_step", **FRONT_STEPS)
        front_silu = signal("front_silu", **led)
        front_mod = signal("front_mod", **led)
        n_front_norm = {**led, "l0_ffn": 3, "l3_attn": 2}
        n_front_turn = {**led, "l0_ffn": 2}
        front_var = signal("front_var", **n_front_norm)
        front_rstd = signal("front_rstd", **n_front_norm)
        front_ready = signal("front_ready", **n_front_turn)
        front_turned = signal("front_turned", **n_front_turn)
        front_feat = signal("front_feat", **n_front_turn)
        gate_psum = signal("gate_psum", l0_ffn=1, l1_ffn=1, l2_ffn=1, l3_ffn=1)
        gated = signal("gated", l2_ffn=1)
        hid_psum = signal("hid_psum", l0_ffn=E0 * 2, l1_ffn=EA, l2_ffn=2)
        hid_ready = signal("hid_ready", l0_ffn=E0 * 2, l1_ffn=EA, l2_ffn=2)
        silu_g = signal("silu_g", l1_ffn=EA)
        expert_psum = signal("expert_psum", l0_ffn=E0, l1_ffn=EA, l3_out=T)
        expert_used = signal("expert_used", l0_ffn=E0, l1_ffn=EA)
        keep_exp, keep_exped, keep_count = once("keep_exp"), once("keep_exped"), once("keep_count")
        mid_ready = signal("mid_ready", l1_attn=QUICK_STEPS)
        counts_act = signal("counts_act", l1_attn=QUICK_STEPS)
        quick_step = signal("quick_step", l1_attn=QUICK_STEPS * QUICK_RAISES)
        bisect_step = signal("bisect_step", l1_attn=SEARCH_STEPS * BISECT_RAISES)
        doubts_ready = signal("doubts_ready", l1_attn=1)
        doubts_psum = signal("doubts_psum", l1_attn=1)
        kept_ready = signal("kept_ready", l1_attn=H)
        max_route = signal("max_route", l1_ffn=1)
        exp_route = signal("exp_route", l1_ffn=1)
        delta_ready = signal("delta_ready", l2_ffn=1)
        root_ready = signal("root_ready", l2_ffn=1)
        z_psum = signal("z_psum", l2_ffn=2)
        z_ready = signal("z_ready", l2_ffn=2)
        v_psum = signal("v_psum", l3_attn=2)
        v_ready = signal("v_ready", l3_attn=2)
        row_ready = signal("row_ready", l3_out=1)
        sink_max, sink_next, sink_sum, sink_step = map(once, ("sink_max", "sink_next", "sink_sum", "sink_step"))
        o_ready = signal("o_ready", l3_attn=4)
        o_turned = signal("o_turned", l3_attn=4)
        o_feat = signal("o_feat", l3_attn=4)

        block = ctx.enter_context(nc.Block())

        def tiles(flat):
            return flat.rearrange("p (t n) -> p t n", t=T)

        def both(row):
            return row.unsqueeze(1).to_broadcast([P, T, row.shape[1]])


        def score_banks(ph):
            return [2, 3, 4, 0] if ph == "l1_attn" else [2, 3, 4]

        CAUSAL = [(0, 0, 128), (1, 128, 256)]
        FULL = [(0, 0, 256), (1, 256, 256)]

        def early(ph):
            return ph in ("l0_attn", "l2_attn")

        def rows_of(h):
            return slice(64 * (h % 2), 64 * (h % 2) + 64), h // 2

        def turned_input(ph):
            return front_n[:] if ph in ("l0_ffn", "l3_attn") else xb[:]

        @block.sync
        def _(sp):
            sp.dma_start(x[:], x_in.rearrange("b (t p) d -> p (b t) d", p=P)).then_inc(x_loaded, 16)
            sp.dma_start(silu_c[:], c_in).then_inc(c_loaded, 16)
            sp.dma_start(const[:], const_in).then_inc(const_loaded, 16)
            for i in range(HPG):
                sp.wait_ge(stacks_clear, 1)
                sp.dma_start(big[64 * i + 48:64 * i + 48 + ALI_ROWS, 0:2 * NG, :], ali_in[i].rearrange("r (s n) -> r s n", n=S)).then_inc(ali_loaded, 16)

            def load(i):
                n = places[WEIGHED[i]][1]
                sp.dma_start(region[i % 2][:, 0:n], weights_in[WEIGHED[i]]).then_inc(loaded[i], 16)

            def expand(ph, b, first=False):
                sp.wait_ge(parts_ready.sem, parts_ready(ph, b, 1))
                for u in range(2):
                    if not first:
                        sp.wait_ge(scores_psum.sem, scores_psum(ph, b, (u - 1) * H // 2))
                    for i in range(HPG):
                        for slot, of in enumerate(SLOTS):
                            to = slice(64 * i + HD * slot, 64 * i + HD * slot + HD)
                            at = slice((2 * i + u) * HD * HALF, (2 * i + u + 1) * HD * HALF)
                            sp.dma_start(stack[to, u * HALF:(u + 1) * HALF], pair(at, *of)).then_inc(stacked[u].sem, 16)

            load(0)
            load(1)
            for i, ph in enumerate(WEIGHED):
                if 1 <= i < len(WEIGHED) - 1:
                    sp.wait_ge(pass_done.sem, pass_done(ph, 0, 1))
                    load(i + 1)
                if ph in narrow_phases:
                    expand(ph, 0, i == 0)
                    with sp.Fori(0, B - 1) as b:
                        expand(ph, b + 1)
            sp.wait_ge(pass_done.sem, len(PHASES) * B + 1)
            sp.dma_start(out.rearrange("b (t p) d -> p (b t) d", p=P), x[:]).then_inc(stored, 16)
            sp.wait_ge(stored, 16)

        @block.gpsimd
        def _(pool):
            nc.gpsimd.memset(identb[:], 0.0).then_inc(masks_ready, 1)
            nc.gpsimd.memset(future[:], 0.0).then_inc(masks_ready, 1)
            pool.wait_ge(masks_ready, 2)
            nc.gpsimd.affine_select(out=identb[:], in_=identb[:], compare_op=ALU.not_equal, fill=1.0, base=0,
                                    pattern=[[-1, P]], channel_multiplier=1).then_inc(masks_ready, 1)
            nc.gpsimd.affine_select(out=future[:], in_=future[:], compare_op=ALU.is_ge, fill=MASKED, base=0,
                                    pattern=[[-1, P]], channel_multiplier=1).then_inc(masks_ready, 1)
            pool.wait_ge(fixed_ready, 4)

            def prepare(ph, b):
                for n in range(n_front_norm[ph]):
                    pool.wait_ge(front_var.sem, front_var(ph, b, n + 1))
                    nc.gpsimd.tensor_tensor(rstd[:], var[:], minus_half[:], ALU.pow).then_inc(front_rstd.sem, 1)

            def finish(ph, b):
                pool.wait_ge(var_ready.sem, var_ready(ph, b, 1))
                nc.gpsimd.tensor_tensor(main_rstd[:], main_var[:], minus_half[:], ALU.pow).then_inc(rstd_ready.sem, 1)

            for ph in WEIGHED:
                if ph in FRONT_STEPS:
                    prepare(ph, 0)
                    with pool.Fori(0, B - 1) as b:
                        prepare(ph, b + 1)
                        if n_norm[ph]:
                            finish(ph, b)
                    if n_norm[ph]:
                        finish(ph, B - 1)
                    continue
                with pool.Fori(0, B) as b:
                    for n in range(n_norm[ph]):
                        pool.wait_ge(var_ready.sem, var_ready(ph, b, n + 1))
                        nc.gpsimd.tensor_tensor(rstd[:], var[:], minus_half[:], ALU.pow).then_inc(rstd_ready.sem, 1)
                    if ph == "l2_ffn":
                        pool.wait_ge(delta_ready.sem, delta_ready(ph, b, 1))
                        nc.gpsimd.tensor_tensor(small[5][:, 0:T * E2], small[4][:, 0:T * E2], half[:],
                                                ALU.pow).then_inc(root_ready.sem, 1)
                if ph == "l3_ffn":
                    pool.wait_ge(pass_done.sem, pass_done("l3_out", 0, 1))
                    nc.gpsimd.partition_all_reduce(colmax[:], routes[:].rearrange("p t b e -> p (t b e)"), P,
                                                   bass.bass_isa.ReduceOp.max).then_inc(sink_max, 1)

        @block.tensor
        def _(pe):
            mm = nc.tensor.matmul

            def start_pass(ph, b):
                pe.wait_ge(pass_done.sem, pass_done(ph, b, 1))
                pe.wait_ge(silu_ready.sem, silu_ready(ph, b, 1))
                mm(pb[7][:, 0:3 * D], silu_b[:], W(ph, "wmod"), start=True, stop=True).then_inc(mod_psum.sem, 1)

            def turn(ph, b, n, src, width=P):
                pe.wait_ge(tok_ready.sem, tok_ready(ph, b, n))
                for t in range(T):
                    last = nc.tensor.transpose(pb[0][0:width, t * P:(t + 1) * P], src[:, t, :], C("ident"))
                last.then_inc(turned.sem, 1)
                pe.wait_ge(feat_ready.sem, feat_ready(ph, b, n))

            def front_modulation(ph, b):
                pe.wait_ge(front_silu.sem, front_silu(ph, b, 1))
                mm(pb[5][:, 0:3 * D], silu_b[:], W(ph, "wmod"), start=True, stop=True).then_inc(front_mod.sem, 1)

            def front_turn(ph, b, src, n=1):
                pe.wait_ge(front_ready.sem, front_ready(ph, b, n))
                for t in range(T):
                    last = nc.tensor.transpose(pb[5][:, t * P:(t + 1) * P], src[:, t, :], C("ident"))
                last.then_inc(front_turned.sem, 1)

            def project_qkv(ph, b):
                pe.wait_ge(front_feat.sem, front_feat(ph, b, 1))
                f = next_feat[:]
                mm(pb[0][:, 0:S], W(ph, "wq"), f, start=True, stop=True)
                mm(pb[0][:, S:2 * S], W(ph, "wk"), f, start=True, stop=True).then_inc(proj_psum.sem, 1)
                for t in range(T):
                    last = mm(pb[5][:, S + t * D:S + (t + 1) * D], f[:, t * P:(t + 1) * P], W(ph, "wv"), start=True, stop=True)
                last.then_inc(proj_psum.sem, 1)

            def scores(ph, b, h, blocks):
                rows, g = rows_of(h)
                n_banks = len(score_banks(ph))
                bank = pb[score_banks(ph)[h % n_banks]]
                if h % (H // 2) == 0 and ph in narrow_phases:
                    half_in_place = stacked[h // (H // 2)]
                    pe.wait_ge(half_in_place.sem, half_in_place(ph, b, 16 * EXPANDS))
                if h < n_banks:
                    pe.wait_ge(qkv_ready.sem, qkv_ready(ph, b, 1 if ph in narrow_phases else n_qkv[ph]))
                else:
                    pe.wait_ge(probs_ready.sem, probs_ready(ph, b, h + 1 - n_banks))
                for t, at, n in blocks:
                    causal = blocks is CAUSAL
                    if ph in narrow_phases:
                        qs, ks = stack[rows, g, 0, :], stack[rows, g, 1, :]
                    else:
                        qs, ks = qT[rows, g, :], kT[rows, g, :]
                    last = mm(bank[:, at:at + n], qs[:, t * P:(t + 1) * P], ks[:, 0:n],
                              start=True, stop=not causal)
                    if causal:
                        last = mm(bank[:, at + t * P:at + n], identb[:], future[:], start=False, stop=True)
                last.then_inc(scores_psum.sem, 1)

            def turn_probs(ph, b, h, src, blocks):
                if h >= 2:
                    pe.wait_ge(probsT_ready.sem, probsT_ready(ph, b, h - 1))
                for _, at, n in blocks:
                    for k in range(n // P):
                        cols = slice(at + k * P, at + (k + 1) * P)
                        last = nc.tensor.transpose(pb[6 + h % 2][:, cols], src[:, cols], C("ident"))
                last.then_inc(probsT_psum.sem, 1)

            def weigh(ph, b, h, o, v, blocks):
                if h == 0 and ph in narrow_phases:
                    pe.wait_ge(qkv_ready.sem, qkv_ready(ph, b, n_qkv[ph]))
                pe.wait_ge(probsT_ready.sem, probsT_ready(ph, b, h + 1))
                for t, at, n in blocks:
                    for k in range(n // P):
                        last = mm(o(t), probsT[:, h % 2, at + k * P:at + (k + 1) * P], v(k),
                                  start=k == 0, stop=k == n // P - 1)
                last.then_inc(pv_done.sem, 1)

            def narrow_attention(ph, b, blocks, following=None):
                width = HD
                def o(h):
                    return lambda t: pb[1][:, (t * H + h) * width:(t * H + h + 1) * width]

                def v(h):
                    return lambda k: V[:, k, h * width:(h + 1) * width]

                for s in range(H + 3):
                    if s == 2 and ph in FRONT_STEPS:
                        pe.wait_ge(pass_done.sem, pass_done(ph, b, 1))
                    if following is not None and s == 3:
                        front_modulation(ph, following)
                    if following is not None and s == (9 if ph == "l0_ffn" else 7):
                        front_turn(ph, following, turned_input(ph))
                    if following is not None and s == (12 if ph == "l0_ffn" else 9):
                        if ph == "l0_ffn":
                            l0_queries(ph, following)
                        else:
                            project_qkv(ph, following)
                    if following is not None and ph == "l0_ffn" and s == 15:
                        l0_latent(ph, following)
                    if following is not None and ph == "l0_ffn" and s == 17:
                        l0_keys_values(ph, following)
                    if s < H and not (early(ph) and s < len(score_banks(ph))):
                        scores(ph, b, s, blocks)
                    if 2 <= s < H + 2:
                        pe.wait_ge(probs_ready.sem, probs_ready(ph, b, s - 1))
                        turn_probs(ph, b, s - 2, probs[:, (s - 2) % 3, :], blocks)
                    if s >= 3:
                        weigh(ph, b, s - 3, o(s - 3), v(s - 3), blocks)

            def turn_out(ph, b):
                pe.wait_ge(tok_ready.sem, tok_ready(ph, b, 1))
                for t in range(T):
                    last = nc.tensor.transpose(pb[1][:, t * P:(t + 1) * P], O[:, t, 0:D], C("ident"))
                last.then_inc(turned.sem, 1)
                pe.wait_ge(feat_ready.sem, feat_ready(ph, b, 1))
                for t in range(T):
                    last = mm(pb[1][:, S + t * D:S + (t + 1) * D], feat[:, t * P:(t + 1) * P], W(ph, "wo"), start=True, stop=True)
                last.then_inc(out_psum.sem, 1)

            def project_out(ph, b):
                for t in range(T):
                    last = mm(pb[0][:, t * D:(t + 1) * D], feat[:, t * P:(t + 1) * P], W(ph, "wo"), start=True, stop=True)
                last.then_inc(out_psum.sem, 1)

            def first_scores(ph, b):
                for h in range(len(score_banks(ph))):
                    scores(ph, b, h, CAUSAL)

            def plain_front(b, ph):
                front_modulation(ph, b)
                front_turn(ph, b, xb)
                project_qkv(ph, b)
                if early(ph):
                    first_scores(ph, b)

            def plain_attn(b, ph, following):
                narrow_attention(ph, b, CAUSAL, following)
                if following is not None:
                    first_scores(ph, following)
                turn_out(ph, b)

            def l0_queries(ph, b):
                pe.wait_ge(front_feat.sem, front_feat(ph, b, 1))
                mm(pb[0][:, 0:S], W(ph, "wq"), next_feat[:], start=True, stop=True)
                mm(pb[0][:, S:2 * S], W(ph, "wqr"), next_feat[:], start=True, stop=True).then_inc(proj_psum.sem, 1)
                for t in range(T):
                    last = mm(pb[5][:, S + t * 64:S + (t + 1) * 64], next_feat[:, t * P:(t + 1) * P], W(ph, "wdkv"), start=True, stop=True)
                last.then_inc(proj_psum.sem, 1)

            def l0_latent(ph, b):
                front_turn(ph, b, front_n[:], 2)

            def l0_keys_values(ph, b):
                pe.wait_ge(front_feat.sem, front_feat(ph, b, 2))
                pe.wait_ge(qkv_ready.sem, qkv_ready(ph, b, 1))
                mm(pb[0][:, 0:S], W(ph, "wuk", 64), next_feat[0:64, :], start=True, stop=True)
                mm(pb[0][:, S:2 * S], W(ph, "wukr", 64), next_feat[0:64, :], start=True, stop=True).then_inc(proj_psum.sem, 1)
                for t in range(T):
                    last = mm(pb[5][:, S + t * D:S + (t + 1) * D], next_feat[0:64, t * P:(t + 1) * P], W(ph, "wuv", 64), start=True, stop=True)
                last.then_inc(proj_psum.sem, 1)

            def l0_front(b, ph="l0_ffn"):
                front_modulation(ph, b)
                front_turn(ph, b, front_n[:])
                l0_queries(ph, b)
                l0_latent(ph, b)
                l0_keys_values(ph, b)

            def l0_ffn(b, following, ph="l0_ffn"):
                narrow_attention(ph, b, CAUSAL, following)
                turn_out(ph, b)
                pe.wait_ge(tok_ready.sem, tok_ready(ph, b, 2))
                for t in range(T):
                    last = nc.tensor.transpose(pb[1][:, t * P:(t + 1) * P], nb[:, t, :], C("ident"))
                last.then_inc(turned.sem, 1)
                pe.wait_ge(feat_ready.sem, feat_ready(ph, b, 2))
                for t in range(T):
                    last = mm(pb[1][:, t * E0:(t + 1) * E0], feat[:, t * P:(t + 1) * P], W(ph, "gate"), start=True, stop=True)
                last.then_inc(gate_psum.sem, 1)

                def rise(e):
                    for u in range(2):
                        n = 2 * e + u
                        if n >= 3:
                            pe.wait_ge(hid_ready.sem, hid_ready(ph, b, n - 2))
                        for c in range(2):
                            at = (e * C0 + 2 * u + c) * P
                            last = mm(pb[2 + n % 3][:, c * S:(c + 1) * S], W(ph, "w1")[:, at:at + P], feat[:], start=True, stop=True)
                        last.then_inc(hid_psum.sem, 1)

                def fall(e):
                    pe.wait_ge(hid_ready.sem, hid_ready(ph, b, 2 * e + 2))
                    if e >= 2:
                        pe.wait_ge(expert_used.sem, expert_used(ph, b, e - 1))
                    for t in range(T):
                        o = pb[6 + e % 2][:, t * D:(t + 1) * D]
                        for c in range(C0):
                            at = (e * C0 + c) * D
                            mm(o, hid[:, e % 2, c, t * P:(t + 1) * P], W(ph, "w2")[:, at:at + D], start=c == 0, stop=False)
                        last = mm(o, ones[0:1, :], W(ph, "b2", 1)[:, e * D:(e + 1) * D], start=False, stop=True)
                    last.then_inc(expert_psum.sem, 1)

                for e in range(E0 + 1):
                    if e < E0:
                        rise(e)
                    if e >= 1:
                        fall(e - 1)

            def l1_front(b, ph="l1_attn"):
                plain_front(b, ph)
                for h in range(H):
                    scores(ph, b, h, FULL)

            def l1_attn(b, following, ph="l1_attn"):
                pe.wait_ge(probs_ready.sem, probs_ready(ph, b, H))
                pe.wait_ge(pass_done.sem, pass_done(ph, b, 1))
                if following is not None:
                    plain_front(following, ph)
                pe.wait_ge(doubts_ready.sem, doubts_ready(ph, b, 1))
                mm(pb[1][0:1, 0:1], ones[:, 0:1], doubts, start=True, stop=True).then_inc(doubts_psum.sem, 1)
                ahead = len(score_banks(ph))
                if following is not None:
                    for h in range(ahead):
                        scores(ph, following, h, FULL)
                width = HD + 1
                for s in range(H + 1):
                    if s < H:
                        pe.wait_ge(kept_ready.sem, kept_ready(ph, b, s + 1))
                        turn_probs(ph, b, s, big[:, 2 * s:2 * s + 2, :].rearrange("p t k -> p (t k)"), FULL)
                    if following is not None and 1 <= s and s - 1 + ahead < H:
                        scores(ph, following, s - 1 + ahead, FULL)
                    if s >= 1:
                        h = s - 1
                        weigh(ph, b, h, lambda t: pb[1][:, t * 256 + h * width:t * 256 + (h + 1) * width],
                              lambda k: V[:, k, h * width:(h + 1) * width], FULL)
                turn_out(ph, b)

            def l1_ffn(b, ph="l1_ffn"):
                start_pass(ph, b)
                turn(ph, b, 1, hb)
                for t in range(T):
                    last = mm(pb[1][:, t * E1:(t + 1) * E1], feat[:, t * P:(t + 1) * P], W(ph, "router"), start=True, stop=True)
                last.then_inc(gate_psum.sem, 1)

                def rise(e):
                    if e >= 4:
                        pe.wait_ge(hid_ready.sem, hid_ready(ph, b, e - 3))
                    cols = slice(e * P, (e + 1) * P)
                    mm(pb[2 + e % 4][:, 0:S], W(ph, "gate")[:, cols], feat[:], start=True, stop=True)
                    mm(pb[2 + e % 4][:, S:2 * S], W(ph, "up")[:, cols], feat[:], start=True, stop=True).then_inc(hid_psum.sem, 1)

                def fall(e):
                    pe.wait_ge(hid_ready.sem, hid_ready(ph, b, e + 1))
                    if e >= 2:
                        pe.wait_ge(expert_used.sem, expert_used(ph, b, e - 1))
                    for t in range(T):
                        last = mm(pb[6 + e % 2][:, t * D:(t + 1) * D], hid[:, e % 2, 0, t * P:(t + 1) * P],
                                  W(ph, "down")[:, e * D:(e + 1) * D], start=True, stop=True)
                    last.then_inc(expert_psum.sem, 1)

                for e in range(EA + 2):
                    if e < EA:
                        rise(e)
                    if e >= 2:
                        fall(e - 2)

            def l2_ffn(b, ph="l2_ffn"):
                start_pass(ph, b)
                turn(ph, b, 1, hb)
                for t in range(T):
                    last = mm(pb[1][:, t * E2:(t + 1) * E2], feat[:, t * P:(t + 1) * P], W(ph, "proj"), start=True, stop=True)
                last.then_inc(gate_psum.sem, 1)
                mm(pb[2][0:R2, 0:S], W(ph, "win1"), feat[:], start=True, stop=True)
                pe.wait_ge(tok_ready.sem, tok_ready(ph, b, 2))
                for t in range(T):
                    last = nc.tensor.transpose(pb[0][0:E2, t * P:(t + 1) * P], nb[:, t, 0:E2], C("ident"))
                last.then_inc(turned.sem, 1)
                pe.wait_ge(feat_ready.sem, feat_ready(ph, b, 2))
                mm(pb[3][0:R2, 0:S], W(ph, "c1", E2), feat_o[0:E2, 0, :], start=True, stop=True)
                mm(pb[3][0:R2, S:2 * S], W(ph, "c2", E2), feat_o[0:E2, 0, :], start=True, stop=True).then_inc(z_psum.sem, 1)
                pe.wait_ge(z_ready.sem, z_ready(ph, b, 1))
                for u in range(2):
                    for c in range(2):
                        at = (2 * u + c) * P
                        last = mm(pb[4 + u][:, c * S:(c + 1) * S], W(ph, "wout1", R2)[:, at:at + P], rope_c[0:R2, :], start=True, stop=True)
                    last.then_inc(hid_psum.sem, 1)
                for c in range(O2):
                    pe.wait_ge(hid_ready.sem, hid_ready(ph, b, c // 2 + 1))
                    last = mm(pb[2][0:R2, 0:S], W(ph, "win2")[:, c * R2:(c + 1) * R2], hid[:, 0, c, :], start=c == 0, stop=c == O2 - 1)
                last.then_inc(z_psum.sem, 1)
                pe.wait_ge(z_ready.sem, z_ready(ph, b, 2))
                for t in range(T):
                    last = mm(pb[0][:, t * D:(t + 1) * D], rope_s[0:R2, t * P:(t + 1) * P], W(ph, "wout2", R2), start=True, stop=True)
                last.then_inc(out_psum.sem, 1)

            def l3_project(ph, b):
                pe.wait_ge(front_feat.sem, front_feat(ph, b, 1))
                for g in range(NG3):
                    two = 2 + 2 * (g % 2)
                    if g >= 2:
                        pe.wait_ge(qkv_ready.sem, qkv_ready(ph, b, g - 1))
                    for j in range(4):
                        at = (g * 4 + j) * P
                        last = mm(pb[two + j // 2][:, (j % 2) * S:(j % 2 + 1) * S], W(ph, "wqk")[:, at:at + P], next_feat[:], start=True, stop=True)
                    last.then_inc(proj_psum.sem, 1)
                    if g in (1, 3):
                        t = g // 2
                        if t:
                            pe.wait_ge(v_ready.sem, v_ready(ph, b, 1))
                        for j in range(2):
                            last = mm(pb[6 + j][:], next_feat[:, t * P:(t + 1) * P], W(ph, "wv")[:, j * 512:(j + 1) * 512], start=True, stop=True)
                        last.then_inc(v_psum.sem, 1)

            def l3_front(b, ph="l3_attn"):
                front_modulation(ph, b)
                front_turn(ph, b, turned_input(ph))
                l3_project(ph, b)

            def l3_attn(b, following, ph="l3_attn"):
                pe.wait_ge(v_ready.sem, v_ready(ph, b, 2))
                for s in range(H + 3):
                    if s == 2:
                        pe.wait_ge(pass_done.sem, pass_done(ph, b, 1))
                    if following is not None and s == 3:
                        front_modulation(ph, following)
                    if following is not None and s == 10:
                        front_turn(ph, following, turned_input(ph))
                    if s < H:
                        scores(ph, b, s, FULL)
                    if 2 <= s < H + 2:
                        pe.wait_ge(probs_ready.sem, probs_ready(ph, b, s - 1))
                        turn_probs(ph, b, s - 2, probs[:, (s - 2) % 3, :], FULL)
                    if s >= 3:
                        h = s - 3
                        if h >= 8 and h % 4 == 0:
                            pe.wait_ge(o_ready.sem, o_ready(ph, b, h // 4 - 1))
                        weigh(ph, b, h, lambda t: pb[h // 4 % 2][:, (t * 4 + h % 4) * HD3:(t * 4 + h % 4 + 1) * HD3],
                              lambda k: V[:, k, h * HD3:(h + 1) * HD3], FULL)
                if following is not None:
                    l3_project(ph, following)
                    pe.wait_ge(qkv_ready.sem, qkv_ready(ph, following, NG3))
                for u in range(4):
                    pe.wait_ge(o_ready.sem, o_ready(ph, b, u + 1))
                    for j in range(2):
                        for t in range(T):
                            g = 2 * u + j
                            last = nc.tensor.transpose(pb[2 + u][:, j * S + t * P:j * S + (t + 1) * P], O[:, t, g * P:(g + 1) * P], C("ident"))
                    last.then_inc(o_turned.sem, 1)
                pe.wait_ge(o_feat.sem, o_feat(ph, b, 4))
                for t in range(T):
                    for g in range(NG3):
                        last = mm(pb[0][:, t * D:(t + 1) * D], feat_o[:, g, t * P:(t + 1) * P], W(ph, "wo")[:, g * D:(g + 1) * D],
                                  start=g == 0, stop=g == NG3 - 1)
                last.then_inc(out_psum.sem, 1)

            def l3_ffn(b, ph="l3_ffn"):
                start_pass(ph, b)
                turn(ph, b, 1, hb)
                for t in range(T):
                    last = mm(pb[1][:, t * E3:(t + 1) * E3], feat[:, t * P:(t + 1) * P], W(ph, "gate"), start=True, stop=True)
                last.then_inc(gate_psum.sem, 1)

            def l3_route():
                for r in range(ROUNDS3):
                    pe.wait_ge(sink_next, r + 1)
                    for t in range(T):
                        last = mm(pb[0][:, 0:B * E3], ones[:], routes[:, t].rearrange("p b e -> p (b e)"), start=t == 0, stop=t == T - 1)
                    last.then_inc(sink_sum, 1)
                pe.wait_ge(sink_next, ROUNDS3 + 1)
                for t in range(T):
                    last = nc.tensor.transpose(pb[1][0:B * E3, t * P:(t + 1) * P], routes[:, t].rearrange("p b e -> p (b e)"), C("ident"))
                last.then_inc(sink_sum, 1)
                pe.wait_ge(sink_next, ROUNDS3 + 2)
                n = B * E3
                for t in range(T):
                    last = nc.tensor.transpose(pb[0][:, t * n:(t + 1) * n], qT[0:n, 2, t * P:(t + 1) * P], C("ident", n)[:, 0:n])
                last.then_inc(sink_sum, 1)

            def l3_out(b, ph="l3_out"):
                pe.wait_ge(row_ready.sem, row_ready(ph, b, 1))
                for t in range(T):
                    for j in range(2):
                        last = mm(pb[2 + 2 * t + j][:], feat[:, t * P:(t + 1) * P], W("l3_ffn", "experts")[:, j * 512:(j + 1) * 512], start=True, stop=True)
                    last.then_inc(expert_psum.sem, 1)

            pe.wait_ge(masks_ready, 4)
            pe.wait_ge(const_loaded, 16)
            pe.wait_ge(fixed_ready, 4)
            pe.wait_ge(loaded[0], 16)
            plain_front(0, "l0_attn")
            with pe.Fori(0, B - 1) as b:
                plain_attn(b, "l0_attn", b + 1)
            plain_attn(B - 1, "l0_attn", None)
            pe.wait_ge(loaded[1], 16)
            l0_front(0)
            with pe.Fori(0, B - 1) as b:
                l0_ffn(b, b + 1)
            l0_ffn(B - 1, None)
            pe.wait_ge(loaded[2], 16)
            l1_front(0)
            with pe.Fori(0, B - 1) as b:
                l1_attn(b, b + 1)
            l1_attn(B - 1, None)
            pe.wait_ge(loaded[3], 16)
            with pe.Fori(0, B) as b:
                l1_ffn(b)
            pe.wait_ge(loaded[4], 16)
            plain_front(0, "l2_attn")
            with pe.Fori(0, B - 1) as b:
                plain_attn(b, "l2_attn", b + 1)
            plain_attn(B - 1, "l2_attn", None)
            pe.wait_ge(loaded[5], 16)
            with pe.Fori(0, B) as b:
                l2_ffn(b)
            pe.wait_ge(loaded[6], 16)
            l3_front(0)
            with pe.Fori(0, B - 1) as b:
                l3_attn(b, b + 1)
            l3_attn(B - 1, None)
            pe.wait_ge(loaded[7], 16)
            with pe.Fori(0, B) as b:
                l3_ffn(b)
            l3_route()
            with pe.Fori(0, B) as b:
                l3_out(b)

        @block.vector
        def _(dve):
            V_ = nc.vector
            count = [0]

            def step(ins):
                count[0] += 1
                ins.then_inc(dve_step.sem, 1)

            def settle(ph, b):
                dve.wait_ge(dve_step.sem, dve_step(ph, b, count[0]))

            def settle_apart(ph, b):
                settle(ph, b)
                step(V_.memset(gap[:], 0.0))

            front_count = [0]

            def front_step_of(ins):
                front_count[0] += 1
                ins.then_inc(front_step.sem, 1)

            def front_settle(ph, b):
                dve.wait_ge(front_step.sem, front_step(ph, b, front_count[0]))

            def front_settle_apart(ph, b):
                front_settle(ph, b)
                front_step_of(V_.memset(gap[:], 0.0))

            def front_row(ph, b, first):
                front_count[0] = 0
                if first:
                    dve.wait_ge(pass_done.sem, pass_done(ph, b, 1))
                else:
                    dve.wait_ge(front_turned.sem, front_turned(ph, b, 0))
                front_step_of(V_.memset(gap[:], 0.0))
                front_step_of(V_.tensor_copy(xb[:], x[:, bass.ds(b * T, T), :]))
                layer = PHASES.index(ph) // 2
                V_.tensor_copy(silu_b[:], silu_c[:, bass.ds(b + layer * B, 1)].to_broadcast([P, P])).then_inc(front_silu.sem, 1)
                front_settle(ph, b)
                for t in range(T):
                    front_step_of(V_.bn_stats(stats[:, t, :], xb[:, t, :]))
                front_settle_apart(ph, b)
                for t in range(T):
                    front_step_of(V_.bn_aggr(moments[:, t, :], stats[:, t, :]))
                front_settle(ph, b)
                V_.tensor_scalar(var[:], moments[:, :, 1], LN_EPS, None, ALU.add).then_inc(front_var.sem, 1)

            def front_adaln(ph, b):
                dve.wait_ge(front_rstd.sem, front_rstd(ph, b, 1))
                for t in range(T):
                    front_step_of(V_.tensor_scalar(xb[:, t, :], xb[:, t, :], moments[:, t, 0:1], rstd[:, t:t + 1], ALU.subtract, ALU.mult))
                dve.wait_ge(front_mod.sem, front_mod(ph, b, 1))
                shift, scale, gate = (pb[5][:, j * D:(j + 1) * D] for j in range(3))
                front_step_of(V_.tensor_scalar(scale_b[:], scale, 1.0, None, ALU.add))
                front_step_of(V_.tensor_scalar(next_gate_b[:], gate, -1.0, 0.25, ALU.mult, ALU.max))
                front_step_of(V_.tensor_scalar(gate_sign[:], gate, 0.0, 2.0, ALU.is_ge, ALU.mult))
                front_settle(ph, b)
                front_step_of(V_.tensor_tensor(xb[:], xb[:], both(scale_b[:]), ALU.mult))
                front_step_of(V_.tensor_tensor(next_gate_b[:], gate, next_gate_b[:], ALU.max))
                front_settle(ph, b)
                front_step_of(V_.scalar_tensor_tensor(next_gate_b[:], gate_sign[:], 1.0, next_gate_b[:], ALU.subtract, ALU.mult))
                return V_.tensor_tensor(xb[:], xb[:], both(shift), ALU.add)

            def front_end(ph, b):
                assert front_count[0] == FRONT_STEPS[ph], f"NSTEPS front {ph} {front_count[0]}"

            def start_main(ph, b):
                count[0] = 0
                dve.wait_ge(front_step.sem, front_step(ph, b, FRONT_STEPS[ph]))
                dve.wait_ge(pass_done.sem, pass_done(ph, b, 1))
                step(V_.tensor_copy(gate_b[:], next_gate_b[:]))
                settle(ph, b)

            def end_main(ph, b):
                settle(ph, b)
                step(V_.tensor_tensor(sum_b[:], sum_b[:], both(gate_b[:]), ALU.mult))
                settle(ph, b)
                row = x[:, bass.ds(b * T, T), :]
                V_.tensor_tensor(row, row, sum_b[:], ALU.add).then_inc(pass_done.sem, 1)
                assert count[0] == DVE_STEPS[ph], f"NSTEPS main {ph} {count[0]}"

            def take_row(ph, b):
                count[0] = 0
                dve.wait_ge(pass_done.sem, pass_done(ph, b, 1))
                step(V_.memset(gap[:], 0.0))
                step(V_.tensor_copy(xb[:], x[:, bass.ds(b * T, T), :]))
                layer = PHASES.index(ph) // 2
                V_.tensor_copy(silu_b[:], silu_c[:, bass.ds(b + layer * B, 1)].to_broadcast([P, P])).then_inc(silu_ready.sem, 1)
                settle(ph, b)

            def put_row(ph, b):
                settle_apart(ph, b)
                V_.tensor_copy(x[:, bass.ds(b * T, T), :], xb[:]).then_inc(pass_done.sem, 1)
                assert count[0] == DVE_STEPS[ph], f"NSTEPS main {ph} {count[0]}"

            def norm(ph, b, n, dst, src, eps, mean=True):
                w = src.shape[2]
                for t in range(T):
                    step(V_.bn_stats(stats[:, t, :], src[:, t, :]))
                settle_apart(ph, b)
                for t in range(T):
                    step(V_.bn_aggr(moments[:, t, :], stats[:, t, :]))
                settle(ph, b)
                spread = moments[:, :, 1]
                if not mean:
                    step(V_.tensor_tensor(square[:], moments[:, :, 0], moments[:, :, 0], ALU.mult))
                    settle(ph, b)
                    step(V_.tensor_tensor(square[:], square[:], moments[:, :, 1], ALU.add))
                    settle(ph, b)
                    spread = square[:]
                V_.tensor_scalar(var[:], spread, eps, None, ALU.add).then_inc(var_ready.sem, 1)
                dve.wait_ge(rstd_ready.sem, rstd_ready(ph, b, n))
                for t in range(T):
                    if mean:
                        step(V_.tensor_scalar(dst[:, t, 0:w], src[:, t, :], moments[:, t, 0:1], rstd[:, t:t + 1], ALU.subtract, ALU.mult))
                    else:
                        step(V_.tensor_scalar(dst[:, t, 0:w], src[:, t, :], rstd[:, t:t + 1], None, ALU.mult))
                settle(ph, b)

            def adaln(ph, b):
                norm(ph, b, 1, nb[:], xb[:], LN_EPS)
                dve.wait_ge(mod_psum.sem, mod_psum(ph, b, 1))
                shift, scale, gate = (pb[7][:, j * D:(j + 1) * D] for j in range(3))
                step(V_.tensor_scalar(scale_b[:], scale, 1.0, None, ALU.add))
                step(V_.tensor_scalar(gate_b[:], gate, -1.0, 0.25, ALU.mult, ALU.max))
                step(V_.tensor_scalar(sum_b[:, 0, :], gate, 0.0, 2.0, ALU.is_ge, ALU.mult))
                settle(ph, b)
                step(V_.tensor_tensor(gate_b[:], gate, gate_b[:], ALU.max))
                settle(ph, b)
                step(V_.scalar_tensor_tensor(gate_b[:], sum_b[:, 0, :], 1.0, gate_b[:], ALU.subtract, ALU.mult))
                step(V_.tensor_tensor(nb[:], nb[:], both(scale_b[:]), ALU.mult))
                settle(ph, b)
                return V_.tensor_tensor(hb[:], nb[:], both(shift), ALU.add)

            def add_gated(ph, b):
                settle(ph, b)
                step(V_.tensor_tensor(sum_b[:], sum_b[:], both(gate_b[:]), ALU.mult))
                settle(ph, b)
                step(V_.tensor_tensor(xb[:], xb[:], sum_b[:], ALU.add))

            def row_max(ph, b, h, blocks):
                dve.wait_ge(scores_psum.sem, scores_psum(ph, b, h + 1))
                bank = pb[score_banks(ph)[h % len(score_banks(ph))]]
                if blocks is CAUSAL:
                    for t, at, n in blocks:
                        last = V_.tensor_reduce(nmax[:, h, t:t + 1], bank[:, at:at + n], AX.X, ALU.max, negate=True)
                else:
                    last = V_.tensor_reduce(nmax[:, h, :], tiles(bank[:]), AX.X, ALU.max, negate=True)
                last.then_inc(max_ready.sem, 1)

            def take_probsT(ph, b, h, blocks):
                n = blocks[-1][1] + blocks[-1][2]
                dve.wait_ge(probsT_psum.sem, probsT_psum(ph, b, h + 1))
                if h >= 2:
                    dve.wait_ge(pv_done.sem, pv_done(ph, b, h - 1))
                V_.tensor_copy(probsT[:, h % 2, 0:n], pb[6 + h % 2][:, 0:n]).then_inc(probsT_ready.sem, 1)

            def narrow_softmax(ph, b, blocks, following=None):
                for s in range(H + 2):
                    if following is not None and s == 2:
                        front_row(ph, following, False)
                    if following is not None and s == 5:
                        if ph == "l0_ffn":
                            front_step_of(front_adaln(ph, following))
                            l0_square(ph, following)
                        else:
                            front_adaln(ph, following).then_inc(front_ready.sem, 1)
                    if following is not None and s == 7 and ph == "l0_ffn":
                        l0_rms(ph, following)
                    if following is not None and s == (14 if ph == "l0_ffn" else 11):
                        if ph == "l0_ffn":
                            l0_queries(ph, following)
                            l0_latent_stats(ph, following)
                            l0_latent(ph, following)
                        else:
                            intake_qk(ph, following)
                    if s < H:
                        row_max(ph, b, s, blocks)
                    if s >= 2:
                        take_probsT(ph, b, s - 2, blocks)
                dve.wait_ge(probs_ready.sem, probs_ready(ph, b, H))
                step(V_.reciprocal(rinv[:], rowsum[:]))
                settle(ph, b)
                dve.wait_ge(pv_done.sem, pv_done(ph, b, H))
                for t in range(T):
                    last = V_.tensor_tensor(O[:, t, 0:D].rearrange("p (h d) -> p h d", h=H),
                                            pb[1][:, t * D:(t + 1) * D].rearrange("p (h d) -> p h d", h=H),
                                            rinv[:, :, t].unsqueeze(2).to_broadcast([P, H, HD]), ALU.mult)
                last.then_inc(tok_ready.sem, 1)

            def split(ph, b):
                front_settle(ph, b)
                for half_in_place in stacked:
                    dve.wait_ge(half_in_place.sem, half_in_place(ph, b, 0))
                front_step_of(V_.tensor_copy(pair(slice(0, P), 0, 0), compact))
                front_settle(ph, b)
                front_step_of(V_.tensor_tensor(rest, compact, pair(slice(0, P), 0, 0), ALU.subtract))
                front_settle(ph, b)
                front_step_of(V_.tensor_copy(pair(slice(0, P), 1, 1), rest))
                front_settle(ph, b)
                front_step_of(V_.tensor_tensor(rest, rest, pair(slice(0, P), 1, 1), ALU.subtract))
                front_settle(ph, b)
                V_.tensor_copy(pair(slice(0, P), 2, 2), rest).then_inc(parts_ready.sem, 1)

            def intake_qk(ph, b):
                dve.wait_ge(proj_psum.sem, proj_psum(ph, b, 1))
                front_step_of(V_.tensor_scalar(compact[:, 0, :], pb[0][:, 0:S], W(ph, "bq"), HD ** -0.5, ALU.add, ALU.mult))
                V_.tensor_scalar(compact[:, 1, :], pb[0][:, S:2 * S], W(ph, "bk"), None, ALU.add).then_inc(qkv_ready.sem, 1)
                dve.wait_ge(qkv_ready.sem, qkv_ready(ph, b, 1))
                split(ph, b)
                front_end(ph, b)

            def intake_values(ph, b):
                dve.wait_ge(proj_psum.sem, proj_psum(ph, b, 2))
                V_.tensor_tensor(V[:, :, 0:D], tiles(pb[5][:, S:S + T * D]), both(W(ph, "bv")), ALU.add).then_inc(qkv_ready.sem, 1)

            def intake_values_and_ones(ph, b):
                dve.wait_ge(proj_psum.sem, proj_psum(ph, b, 2))
                v1 = V[:, :, 0:H * (HD + 1)].rearrange("p t (h d) -> p t h d", h=H)
                for t in range(T):
                    last = V_.tensor_tensor(v1[:, t, :, 0:HD], pb[5][:, S + t * D:S + (t + 1) * D].rearrange("p (h d) -> p h d", h=H),
                                            W(ph, "bv").rearrange("p (h d) -> p h d", h=H), ALU.add)
                last.then_inc(qkv_ready.sem, 1)

            def plain_front(b, ph):
                front_row(ph, b, True)
                front_adaln(ph, b).then_inc(front_ready.sem, 1)
                intake_qk(ph, b)
                intake_values(ph, b)

            def plain_attn(b, ph, following):
                start_main(ph, b)
                narrow_softmax(ph, b, CAUSAL, following)
                if following is not None:
                    intake_values(ph, following)
                dve.wait_ge(out_psum.sem, out_psum(ph, b, 1))
                step(V_.tensor_tensor(sum_b[:], tiles(pb[1][:, S:S + T * D]), both(W(ph, "bo")), ALU.add))
                end_main(ph, b)

            def rope(dst, bank, cos, sin, ph, b):
                front_step_of(V_.tensor_tensor(rope_c[:], bank[:, 0:S], W(ph, cos), ALU.mult))
                front_step_of(V_.tensor_tensor(rope_s[:], bank[:, S:2 * S], W(ph, sin), ALU.mult))
                front_settle(ph, b)
                return V_.tensor_tensor(dst, rope_c[:], rope_s[:], ALU.add)

            def l0_square(ph, b):
                front_settle(ph, b)
                for t in range(T):
                    front_step_of(V_.bn_stats(stats[:, t, :], xb[:, t, :]))
                front_settle_apart(ph, b)
                for t in range(T):
                    front_step_of(V_.bn_aggr(moments[:, t, :], stats[:, t, :]))
                front_settle(ph, b)
                front_step_of(V_.tensor_tensor(square[:], moments[:, :, 0], moments[:, :, 0], ALU.mult))
                front_settle(ph, b)
                front_step_of(V_.tensor_tensor(square[:], square[:], moments[:, :, 1], ALU.add))
                front_settle(ph, b)
                V_.tensor_scalar(var[:], square[:], RMS_EPS, None, ALU.add).then_inc(front_var.sem, 1)

            def l0_rms(ph, b):
                dve.wait_ge(front_rstd.sem, front_rstd(ph, b, 2))
                for t in range(T):
                    front_step_of(V_.tensor_scalar(front_n[:, t, :], xb[:, t, :], rstd[:, t:t + 1], None, ALU.mult))
                front_settle(ph, b)
                V_.tensor_tensor(front_n[:], front_n[:], both(W(ph, "n1")), ALU.mult).then_inc(front_ready.sem, 1)

            def l0_queries(ph, b):
                dve.wait_ge(proj_psum.sem, proj_psum(ph, b, 1))
                rope(compact[:, 0, :], pb[0], "cosq", "sinq", ph, b).then_inc(qkv_ready.sem, 1)

            def latent_of():
                return pb[5][:, S:S + T * 64].rearrange("p (t n) -> p t n", t=T)

            def l0_latent_stats(ph, b):
                dve.wait_ge(proj_psum.sem, proj_psum(ph, b, 2))
                for t in range(T):
                    front_step_of(V_.bn_stats(stats[:, t, :], latent_of()[:, t, :]))
                front_settle_apart(ph, b)
                for t in range(T):
                    front_step_of(V_.bn_aggr(moments[:, t, :], stats[:, t, :]))
                front_settle(ph, b)
                V_.tensor_scalar(var[:], moments[:, :, 1], LN_EPS, None, ALU.add).then_inc(front_var.sem, 1)

            def l0_latent(ph, b):
                dve.wait_ge(front_rstd.sem, front_rstd(ph, b, 3))
                latent = front_n[:, :, 0:64]
                for t in range(T):
                    front_step_of(V_.tensor_scalar(latent[:, t, :], latent_of()[:, t, :], moments[:, t, 0:1], rstd[:, t:t + 1], ALU.subtract, ALU.mult))
                front_settle(ph, b)
                front_step_of(V_.tensor_tensor(latent, latent, both(W(ph, "lng")), ALU.mult))
                front_settle(ph, b)
                V_.tensor_tensor(latent, latent, both(W(ph, "lnb")), ALU.add).then_inc(front_ready.sem, 1)

            def l0_keys_values(ph, b):
                dve.wait_ge(proj_psum.sem, proj_psum(ph, b, 3))
                dve.wait_ge(qkv_ready.sem, qkv_ready(ph, b, 1))
                rope(compact[:, 1, :], pb[0], "cosk", "sink", ph, b).then_inc(qkv_ready.sem, 1)
                dve.wait_ge(qkv_ready.sem, qkv_ready(ph, b, 2))
                split(ph, b)
                dve.wait_ge(proj_psum.sem, proj_psum(ph, b, 4))
                V_.tensor_copy(V[:, :, 0:D], tiles(pb[5][:, S:S + T * D])).then_inc(qkv_ready.sem, 1)
                front_end(ph, b)

            def l0_front(b, ph="l0_ffn"):
                front_row(ph, b, True)
                front_step_of(front_adaln(ph, b))
                l0_square(ph, b)
                l0_rms(ph, b)
                l0_queries(ph, b)
                l0_latent_stats(ph, b)
                l0_latent(ph, b)
                l0_keys_values(ph, b)

            def l0_ffn(b, following, ph="l0_ffn"):
                start_main(ph, b)
                step(V_.tensor_copy(hb[:], xb[:]))
                settle(ph, b)
                narrow_softmax(ph, b, CAUSAL, following)
                if following is not None:
                    l0_keys_values(ph, following)
                dve.wait_ge(out_psum.sem, out_psum(ph, b, 1))
                step(V_.tensor_tensor(hb[:], hb[:], tiles(pb[1][:, S:S + T * D]), ALU.add))
                settle(ph, b)
                for t in range(T):
                    step(V_.bn_stats(main_stats[:, t, :], hb[:, t, :]))
                settle_apart(ph, b)
                for t in range(T):
                    step(V_.bn_aggr(main_moments[:, t, :], main_stats[:, t, :]))
                settle(ph, b)
                step(V_.tensor_tensor(main_square[:], main_moments[:, :, 0], main_moments[:, :, 0], ALU.mult))
                settle(ph, b)
                step(V_.tensor_tensor(main_square[:], main_square[:], main_moments[:, :, 1], ALU.add))
                settle(ph, b)
                V_.tensor_scalar(main_var[:], main_square[:], RMS_EPS, None, ALU.add).then_inc(var_ready.sem, 1)
                dve.wait_ge(rstd_ready.sem, rstd_ready(ph, b, 1))
                for t in range(T):
                    step(V_.tensor_scalar(nb[:, t, :], hb[:, t, :], main_rstd[:, t:t + 1], None, ALU.mult))
                settle(ph, b)
                V_.tensor_tensor(nb[:], nb[:], both(W(ph, "n2")), ALU.mult).then_inc(tok_ready.sem, 1)
                logit, order, top, pick = (small[i][:, 0:T * E0].rearrange("p (t e) -> p t e", t=T) for i in range(4))
                top1 = small[4][:, 0:T]
                every_e = top1.unsqueeze(2).to_broadcast([P, T, E0])
                dve.wait_ge(gate_psum.sem, gate_psum(ph, b, 1))
                step(V_.tensor_tensor(logit, pb[1][:, 0:T * E0].rearrange("p (t e) -> p t e", t=T), both(W(ph, "gateb")), ALU.add))
                settle(ph, b)
                step(V_.tensor_reduce(top1, logit, AX.X, ALU.max))
                settle(ph, b)
                step(V_.tensor_tensor(order, logit, every_e, ALU.is_equal))
                settle(ph, b)
                step(V_.tensor_tensor(order, order, both(C("first")), ALU.mult))
                settle(ph, b)
                step(V_.tensor_reduce(top1, order, AX.X, ALU.max))
                settle(ph, b)
                step(V_.tensor_tensor(pick, order, every_e, ALU.is_equal))
                step(V_.tensor_copy(sum_b[:], hb[:]))
                for e in range(E0):
                    dve.wait_ge(expert_psum.sem, expert_psum(ph, b, e + 1))
                    settle(ph, b)
                    for t in range(T):
                        ins = V_.scalar_tensor_tensor(sum_b[:, t, :], pb[6 + e % 2][:, t * D:(t + 1) * D], pick[:, t, e:e + 1],
                                                      sum_b[:, t, :], ALU.mult, ALU.add)
                        if t < T - 1:
                            step(ins)
                    ins.then_inc(expert_used.sem, 1)
                    dve.wait_ge(expert_used.sem, expert_used(ph, b, e + 1))
                end_main(ph, b)

            def l1_keep_counts(ph="l1_attn"):
                z, e, q, f, kf = (small[i][:, 0:H] for i in range(5))
                n = [0]

                def then(ins):
                    n[0] += 1
                    ins.then_inc(keep_count, 1)
                    dve.wait_ge(keep_count, n[0])

                then(V_.memset(V[:, :, 0:H * (HD + 1)], 1.0))
                then(V_.memset(restart, 1.0))
                then(V_.memset(restart[:, :, 0:1], 0.0))
                V_.tensor_tensor(z, W(ph, "ema"), W(ph, "thr"), ALU.subtract).then_inc(keep_exp, 1)
                dve.wait_ge(keep_exped, 1)
                then(V_.tensor_scalar(e, e, 1.0, None, ALU.add))
                then(V_.reciprocal(q, e))
                then(V_.tensor_scalar(q, q, 0.9, 0.1, ALU.mult, ALU.add))
                then(V_.tensor_scalar(q, q, -1.0, 1.0, ALU.mult, ALU.add))
                then(V_.tensor_scalar(q, q, float(S), None, ALU.mult))
                then(V_.tensor_copy(keep_i[:], q))
                then(V_.tensor_copy(f, keep_i[:]))
                then(V_.tensor_tensor(kf, f, q, ALU.is_gt))
                then(V_.tensor_tensor(f, f, kf, ALU.subtract))
                then(V_.tensor_scalar(f, f, 1.0, None, ALU.max))
                then(V_.tensor_copy(keep[:].rearrange("p (h t) -> p h t", t=T), f.unsqueeze(2).to_broadcast([P, H, T])))
                then(V_.tensor_scalar(aim[:], keep[:], -(LEFT + 1) / 2, None, ALU.add))

            def quick_search(ph, b):
                raised = [0]

                def then(ins, b, it):
                    raised[0] += 1
                    ins.then_inc(quick_step.sem, 1)
                    dve.wait_ge(quick_step.sem, quick_step(ph, b, raised[0]) + it * QUICK_RAISES)

                mean = rowsum[:].rearrange("p h t -> p (h t)")
                step(V_.tensor_scalar(under[:, 0, :], mean, (1 + QUICK_LO) / S, -QUICK_LO, ALU.mult, ALU.add))
                step(V_.tensor_scalar(over[:, 0, :], mean, (1 - QUICK_HI) / S, QUICK_HI, ALU.mult, ALU.add))
                step(V_.memset(under[:, 1, :], float(S)))
                step(V_.memset(over[:, 1, :], UNSEEN))
                settle_apart(ph, b)
                with dve.Fori(0, QUICK_STEPS) as it:
                    V_.tensor_tensor(span, over[:, 0, :], under[:, 0, :], ALU.subtract)
                    V_.tensor_tensor(enough, under[:, 1, :], aim[:], ALU.subtract)
                    then(V_.tensor_tensor(part, under[:, 1, :], over[:, 1, :], ALU.subtract), b, it)
                    then(V_.reciprocal(short, part), b, it)
                    then(V_.tensor_tensor(part, enough, short, ALU.mult), b, it)
                    then(V_.scalar_tensor_tensor(part, part, 0.99, span, ALU.min, ALU.mult), b, it)
                    then(V_.tensor_tensor(tried[:, 0, :], under[:, 0, :], part, ALU.add), b, it)
                    V_.tensor_scalar(neg_mid[:], tried[:, 0, :], -1.0, None, ALU.mult).then_inc(mid_ready.sem, 1)
                    for j in range(ROWS_DVE):
                        last = V_.tensor_scalar(flags[j], big[:, j, :], tried[:, 0, j:j + 1], 0.0, ALU.is_gt, ALU.add,
                                                accum_out=tried[:, 1, j:j + 1])
                    dve.wait_ge(counts_act.sem, counts_act(ph, b, 1) + it)
                    then(V_.tensor_scalar(tried[:, 1, ROWS_DVE:], tried[:, 1, ROWS_DVE:], 0.5, S / 2, ALU.mult, ALU.add), b, it)
                    V_.tensor_tensor(enough, tried[:, 1, :], keep[:], ALU.is_ge)
                    then(V_.tensor_tensor(short, tried[:, 1, :], keep[:], ALU.is_lt), b, it)
                    V_.memset(gap[:], 0.0)
                    two = [P, 2, ROWS1]
                    V_.copy_predicated(under, enough.bitcast(I32).unsqueeze(1).to_broadcast(two), tried)
                    then(V_.copy_predicated(over, short.bitcast(I32).unsqueeze(1).to_broadcast(two), tried), b, it)
                assert raised[0] == QUICK_RAISES, f"QUICK {raised[0]}"
                for j in range(ROWS_DVE, ROWS1):
                    step(V_.tensor_scalar(signs[j - ROWS_DVE], big[:, j, :], over[:, 0, j:j + 1], 0.0, ALU.is_gt, ALU.add,
                                          accum_out=over[:, 1, j:j + 1]))
                settle(ph, b)
                step(V_.tensor_tensor(left, keep[:], over[:, 1, :], ALU.subtract))
                settle(ph, b)
                step(V_.tensor_scalar(doubt, left, -(LEFT + 1) / 2, None, ALU.add))
                settle(ph, b)
                step(V_.tensor_tensor(doubt, doubt, doubt, ALU.mult))
                settle(ph, b)
                V_.tensor_scalar(part, doubt, (LEFT / 2) ** 2, 0.0, ALU.is_gt, ALU.add, accum_out=doubts).then_inc(doubts_ready.sem, 1)
                dve.wait_ge(doubts_ready.sem, doubts_ready(ph, b, 1))

            def choose(ph, b, following):
                def next_max(u, first, end):
                    if following is not None and u >= 1:
                        for h in range(4 * (u - 1) + first, 4 * (u - 1) + end):
                            row_max(ph, following, h, FULL)

                for u in range(4):
                    js = range(8 * u, 8 * u + 8)
                    for j in js:
                        step(V_.scalar_tensor_tensor(candidates[:, j % 8, :], big[:, j, :], over[:, 0, j:j + 1], big[:, j, :],
                                                     ALU.is_le, ALU.mult))
                    next_max(u, 0, 2)
                    step(V_.tensor_tensor(past, C("order8").unsqueeze(1).to_broadcast([P, 8, LEFT]),
                                          left[:, 8 * u:8 * u + 8].unsqueeze(2).to_broadcast([P, 8, LEFT]), ALU.is_ge))
                    settle_apart(ph, b)
                    for j in js:
                        step(V_.max(largest[:, j % 8, :], candidates[:, j % 8, :]))
                    next_max(u, 2, 3)
                    settle(ph, b)
                    step(V_.scalar_tensor_tensor(largest, past, 2.0, largest, ALU.mult, ALU.max))
                    settle_apart(ph, b)
                    for j in js:
                        step(V_.match_replace(marked[:, j % 8, :], largest[:, j % 8, :], candidates[:, j % 8, :], -1.0))
                    next_max(u, 3, 4)
                    settle(ph, b)
                    for j in js:
                        last = V_.scalar_tensor_tensor(big[:, j, :], marked[:, j % 8, :], 0.0, big[:, j, :], ALU.is_le, ALU.mult)
                        if j % T == T - 1:
                            last.then_inc(kept_ready.sem, 1)
                    dve.wait_ge(kept_ready.sem, kept_ready(ph, b, 4 * u + 4))
                next_max(4, 0, 4)

            def bisect(ph, b, following):
                step(V_.memset(low[:], SEARCH_LO))
                step(V_.memset(width[:], SEARCH_SPAN / 2))
                step(V_.memset(mid[:], SEARCH_LO + SEARCH_SPAN / 2))
                settle_apart(ph, b)
                raised = [0]

                def then(ins, b, it):
                    raised[0] += 1
                    ins.then_inc(bisect_step.sem, 1)
                    dve.wait_ge(bisect_step.sem, bisect_step(ph, b, raised[0]) + it * BISECT_RAISES)

                with dve.Fori(0, SEARCH_STEPS) as it:
                    for j in range(ROWS1):
                        last = V_.tensor_scalar(bisect_flags[j], big[:, j, :], mid[:, j:j + 1], 0.0, ALU.is_gt, ALU.add,
                                                accum_out=counts[:, j:j + 1])
                    then(last, b, it)
                    then(V_.tensor_tensor(above[:], counts[:], keep[:], ALU.is_ge), b, it)
                    then(V_.scalar_tensor_tensor(low[:], above[:], width[:, 0:1], low[:], ALU.mult, ALU.add), b, it)
                    then(V_.tensor_scalar(width[:], width[:], 0.5, None, ALU.mult), b, it)
                    then(V_.tensor_scalar(mid[:], low[:], width[:, 0:1], None, ALU.add), b, it)
                assert raised[0] == BISECT_RAISES, f"BISECT {raised[0]}"
                step(V_.tensor_scalar(mid[:], low[:], 2 * LAST_STEP, None, ALU.add))
                settle(ph, b)
                step(V_.tensor_scalar(low[:], low[:], -LAST_STEP, None, ALU.add))
                settle(ph, b)
                for u in range(4):
                    js = range(8 * u, 8 * u + 8)
                    for j in js:
                        step(V_.tensor_scalar(masks[:, j % 8, :], big[:, j, :], mid[:, j:j + 1], 0.0, ALU.is_gt, ALU.add,
                                              accum_out=counts[:, j:j + 1]))
                        step(V_.tensor_scalar(within[:, j % 8, :], big[:, j, :], low[:, j:j + 1], None, ALU.is_gt))
                    settle(ph, b)
                    step(V_.tensor_tensor(within, within, masks[:, 0:8, :], ALU.subtract))
                    step(V_.tensor_tensor(counts[:, 8 * u:8 * u + 8], keep[:, 8 * u:8 * u + 8], counts[:, 8 * u:8 * u + 8], ALU.subtract))
                    settle(ph, b)
                    step(V_.tensor_tensor_scan(place.rearrange("p j k -> p (j k)"), restart.rearrange("p j k -> p (j k)"),
                                               within.rearrange("p j k -> p (j k)"), 0.0, ALU.mult, ALU.add))
                    settle(ph, b)
                    for j in js:
                        step(V_.scalar_tensor_tensor(place[:, j % 8, :], place[:, j % 8, :], counts[:, j:j + 1], within[:, j % 8, :],
                                                     ALU.is_le, ALU.mult))
                    settle(ph, b)
                    step(V_.tensor_tensor(masks[:, 0:8, :], masks[:, 0:8, :], place, ALU.add))
                    settle(ph, b)
                    V_.tensor_tensor(big[:, 8 * u:8 * u + 8, :], big[:, 8 * u:8 * u + 8, :], masks[:, 0:8, :], ALU.mult).then_inc(kept_ready.sem, 4)
                    dve.wait_ge(kept_ready.sem, kept_ready(ph, b, 4 * u + 4))
                    if following is not None:
                        for h in range(4 * u, 4 * u + 4):
                            row_max(ph, following, h, FULL)

            def l1_front(b, ph="l1_attn"):
                front_row(ph, b, True)
                front_adaln(ph, b).then_inc(front_ready.sem, 1)
                intake_qk(ph, b)
                intake_values_and_ones(ph, b)
                for h in range(H):
                    row_max(ph, b, h, FULL)

            def l1_attn(b, following, ph="l1_attn"):
                start_main(ph, b)
                if following is not None:
                    front_row(ph, following, False)
                dve.wait_ge(probs_ready.sem, probs_ready(ph, b, H))
                step(V_.tensor_scalar(rinv[:], rowsum[:], 1e-10, None, ALU.mult))
                if following is not None:
                    front_adaln(ph, following).then_inc(front_ready.sem, 1)
                quick_search(ph, b)
                if following is not None:
                    intake_qk(ph, following)
                dve.wait_ge(doubts_psum.sem, doubts_psum(ph, b, 1))
                step(V_.tensor_copy(doubts_i[:], pb[1][0:1, 0:1]))
                settle_apart(ph, b)
                found = dve.value_load(doubts_i[:], min_val=0, max_val=P * ROWS1)
                start = count[0]
                with dve.If(found > 0):
                    bisect(ph, b, following)
                    dve.sem_inc(dve_step.sem, start + SELECT_STEPS - count[0])
                slow = count[0]
                count[0] = start
                with dve.Else():
                    choose(ph, b, following)
                    dve.sem_inc(dve_step.sem, start + SELECT_STEPS - count[0])
                    dve.sem_inc(bisect_step.sem, SEARCH_STEPS * BISECT_RAISES)
                assert max(slow, count[0]) < start + SELECT_STEPS, f"SELECT {slow - start} {count[0] - start}"
                count[0] = start + SELECT_STEPS
                dve.wait_ge(pv_done.sem, pv_done(ph, b, H))
                settle(ph, b)
                for t in range(T):
                    o1 = pb[1][:, t * 256:t * 256 + H * (HD + 1)].rearrange("p (h d) -> p h d", h=H)
                    step(V_.tensor_tensor(rinv[:, :, t], rinv[:, :, t], o1[:, :, HD], ALU.add))
                settle(ph, b)
                step(V_.reciprocal(rkept[:], rinv[:]))
                settle(ph, b)
                for t in range(T):
                    o1 = pb[1][:, t * 256:t * 256 + H * (HD + 1)].rearrange("p (h d) -> p h d", h=H)
                    last = V_.tensor_tensor(O[:, t, 0:D].rearrange("p (h d) -> p h d", h=H), o1[:, :, 0:HD],
                                            rkept[:, :, t].unsqueeze(2).to_broadcast([P, H, HD]), ALU.mult)
                last.then_inc(tok_ready.sem, 1)
                if following is not None:
                    intake_values_and_ones(ph, following)
                dve.wait_ge(out_psum.sem, out_psum(ph, b, 1))
                step(V_.tensor_tensor(sum_b[:], tiles(pb[1][:, S:S + T * D]), both(W(ph, "bo")), ALU.add))
                end_main(ph, b)

            def l1_ffn(b, ph="l1_ffn"):
                take_row(ph, b)
                adaln(ph, b).then_inc(tok_ready.sem, 1)
                score, prob, most, tied = (small[i][:, 0:T * E1].rearrange("p (t e) -> p t e", t=T) for i in range(4))
                rank = small[4][:, 0:T * E1].rearrange("p (t e) -> p t e", t=T)
                one, total, top8 = small[5][:, 0:T], small[6][:, 0:T], small[7][:, 0:T * 8].rearrange("p (t e) -> p t e", t=T)
                weight = small[8][:].rearrange("p (t e) -> p t e", t=T)
                spread = lambda v: v.unsqueeze(2).to_broadcast([P, T, E1])
                dve.wait_ge(gate_psum.sem, gate_psum(ph, b, 1))
                step(V_.tensor_tensor(score, pb[1][:, 0:T * E1].rearrange("p (t e) -> p t e", t=T), both(W(ph, "routerb")), ALU.add))
                settle(ph, b)
                step(V_.tensor_reduce(one, score, AX.X, ALU.max))
                settle(ph, b)
                V_.tensor_tensor(score, score, spread(one), ALU.subtract).then_inc(max_route.sem, 1)
                dve.wait_ge(exp_route.sem, exp_route(ph, b, 1))
                step(V_.tensor_reduce(one, prob, AX.X, ALU.add))
                settle(ph, b)
                step(V_.reciprocal(total, one))
                settle(ph, b)
                step(V_.tensor_tensor(score, prob, spread(total), ALU.mult))
                settle_apart(ph, b)
                for t in range(T):
                    step(V_.max(top8[:, t, :], score[:, t, :]))
                settle(ph, b)
                fourth = top8[:, :, TOP1 - 1:TOP1].to_broadcast([P, T, E1])
                step(V_.tensor_tensor(most, score, fourth, ALU.is_gt))
                step(V_.tensor_tensor(tied, score, fourth, ALU.is_equal))
                settle(ph, b)
                step(V_.tensor_reduce(one, most, AX.X, ALU.add))
                for t in range(T):
                    step(V_.tensor_tensor_scan(rank[:, t, :], ones_e[:], tied[:, t, :], 0.0, ALU.mult, ALU.add))
                settle(ph, b)
                step(V_.tensor_scalar(one, one, -1.0, float(TOP1), ALU.mult, ALU.add))
                settle(ph, b)
                step(V_.tensor_tensor(rank, rank, spread(one), ALU.is_le))
                settle(ph, b)
                step(V_.tensor_tensor(tied, tied, rank, ALU.mult))
                settle(ph, b)
                step(V_.tensor_tensor(most, most, tied, ALU.add))
                settle(ph, b)
                step(V_.tensor_tensor(score, score, most, ALU.mult))
                settle(ph, b)
                step(V_.tensor_reduce(one, score, AX.X, ALU.add))
                settle(ph, b)
                step(V_.tensor_scalar(one, one, 1e-12, None, ALU.max))
                settle(ph, b)
                step(V_.reciprocal(total, one))
                settle(ph, b)
                step(V_.tensor_tensor(weight, score, spread(total), ALU.mult))
                settle(ph, b)

                def rise(e):
                    dve.wait_ge(silu_g.sem, silu_g(ph, b, e + 1))
                    if e >= 2:
                        dve.wait_ge(expert_psum.sem, expert_psum(ph, b, e - 1))
                    V_.tensor_tensor(hid[:, e % 2, 0, :], hid[:, e % 2, 1, :], pb[2 + e % 4][:, S:2 * S], ALU.mult).then_inc(hid_ready.sem, 1)

                def fall(e):
                    dve.wait_ge(expert_psum.sem, expert_psum(ph, b, e + 1))
                    if e:
                        dve.wait_ge(expert_used.sem, expert_used(ph, b, e))
                    down = pb[6 + e % 2]
                    if e == 0:
                        for t in range(T):
                            last = V_.tensor_scalar(sum_b[:, t, :], down[:, t * D:(t + 1) * D], weight[:, t, e:e + 1], None, ALU.mult)
                    elif e < E1:
                        for t in range(T):
                            last = V_.scalar_tensor_tensor(sum_b[:, t, :], down[:, t * D:(t + 1) * D], weight[:, t, e:e + 1],
                                                           sum_b[:, t, :], ALU.mult, ALU.add)
                    else:
                        last = V_.tensor_tensor(sum_b[:], sum_b[:], tiles(down[:, 0:T * D]), ALU.add)
                    last.then_inc(expert_used.sem, 1)

                for e in range(EA + 2):
                    if e < EA:
                        rise(e)
                    if e >= 2:
                        fall(e - 2)
                dve.wait_ge(expert_used.sem, expert_used(ph, b, EA))
                add_gated(ph, b)
                put_row(ph, b)

            def l2_ffn(b, ph="l2_ffn"):
                take_row(ph, b)
                adaln(ph, b).then_inc(tok_ready.sem, 1)
                view = lambda i: small[i][:, 0:T * E2].rearrange("p (t e) -> p t e", t=T)
                z, zs, rest, mean, tau, a = view(0), view(1), view(2), view(3), view(6), view(7)
                flat = lambda i: small[i][:, 0:T * E2]
                one = small[8][:, 0:T]
                spread = one.unsqueeze(2).to_broadcast([P, T, E2])
                dve.wait_ge(gate_psum.sem, gate_psum(ph, b, 1))
                step(V_.tensor_copy(a, pb[1][:, 0:T * E2].rearrange("p (t e) -> p t e", t=T)))
                settle(ph, b)
                norm(ph, b, 2, z, a, LN_EPS)
                step(V_.tensor_scalar(z, z, 0.5, None, ALU.mult))
                settle(ph, b)
                step(V_.tensor_reduce(one, z, AX.X, ALU.max))
                settle(ph, b)
                step(V_.tensor_tensor(z, z, spread, ALU.subtract))
                settle_apart(ph, b)
                for t in range(T):
                    step(V_.max(zs[:, t, 0:8], z[:, t, :]))
                settle_apart(ph, b)
                for t in range(T):
                    step(V_.match_replace(rest[:, t, :], zs[:, t, 0:8], z[:, t, :], MASKED))
                settle_apart(ph, b)
                for t in range(T):
                    step(V_.max(zs[:, t, 8:16], rest[:, t, :]))
                settle(ph, b)
                step(V_.tensor_tensor_scan(flat(3), C("restart"), flat(1), 0.0, ALU.mult, ALU.add))
                step(V_.tensor_tensor(rest, zs, zs, ALU.mult))
                settle(ph, b)
                step(V_.tensor_tensor_scan(flat(4), C("restart"), flat(2), 0.0, ALU.mult, ALU.add))
                step(V_.tensor_tensor(mean, mean, both(C("kinv")), ALU.mult))
                settle(ph, b)
                meansq = view(4)
                step(V_.tensor_tensor(meansq, meansq, both(C("kinv")), ALU.mult))
                step(V_.tensor_tensor(rest, mean, mean, ALU.mult))
                settle(ph, b)
                step(V_.tensor_tensor(meansq, meansq, rest, ALU.subtract))
                settle(ph, b)
                step(V_.tensor_tensor(meansq, meansq, both(C("karange")), ALU.mult))
                settle(ph, b)
                step(V_.tensor_scalar(meansq, meansq, -1.0, 1.0, ALU.mult, ALU.add))
                settle(ph, b)
                step(V_.tensor_tensor(meansq, meansq, both(C("kinv")), ALU.mult))
                settle(ph, b)
                V_.tensor_scalar(meansq, meansq, 0.0, None, ALU.max).then_inc(delta_ready.sem, 1)
                dve.wait_ge(root_ready.sem, root_ready(ph, b, 1))
                step(V_.tensor_tensor(tau, mean, view(5), ALU.subtract))
                settle(ph, b)
                step(V_.tensor_tensor(rest, tau, zs, ALU.is_le))
                settle(ph, b)
                step(V_.tensor_reduce(one, rest, AX.X, ALU.add))
                settle(ph, b)
                step(V_.tensor_tensor(rest, both(C("karange")), spread, ALU.is_equal))
                settle(ph, b)
                step(V_.tensor_tensor(rest, rest, tau, ALU.mult))
                settle(ph, b)
                step(V_.tensor_reduce(one, rest, AX.X, ALU.add))
                settle(ph, b)
                step(V_.tensor_tensor(z, z, spread, ALU.subtract))
                settle(ph, b)
                step(V_.tensor_scalar(z, z, 0.0, None, ALU.max))
                settle(ph, b)
                V_.tensor_tensor(nb[:, :, 0:E2], z, z, ALU.mult).then_inc(tok_ready.sem, 1)
                dve.wait_ge(gated.sem, gated(ph, b, 1))
                V_.scalar_tensor_tensor(rope_c[0:R2, :], pb[2][0:R2, 0:S], W(ph, "win1b", R2), feat_o[0:R2, 1, :], ALU.add, ALU.mult).then_inc(z_ready.sem, 1)
                dve.wait_ge(z_psum.sem, z_psum(ph, b, 2))
                V_.scalar_tensor_tensor(rope_s[0:R2, :], pb[2][0:R2, 0:S], W(ph, "win2b", R2), feat_o[0:R2, 2, :], ALU.add, ALU.mult).then_inc(z_ready.sem, 1)
                dve.wait_ge(out_psum.sem, out_psum(ph, b, 1))
                step(V_.tensor_copy(sum_b[:], tiles(pb[0][:, 0:T * D])))
                add_gated(ph, b)
                put_row(ph, b)

            def l3_square(ph, b):
                front_settle(ph, b)
                for t in range(T):
                    front_step_of(V_.bn_stats(stats[:, t, :], xb[:, t, :]))
                front_settle_apart(ph, b)
                for t in range(T):
                    front_step_of(V_.bn_aggr(moments[:, t, :], stats[:, t, :]))
                front_settle(ph, b)
                V_.tensor_scalar(var[:], moments[:, :, 1], LN_EPS, None, ALU.add).then_inc(front_var.sem, 1)

            def l3_norm(ph, b):
                dve.wait_ge(front_rstd.sem, front_rstd(ph, b, 2))
                for t in range(T):
                    front_step_of(V_.tensor_scalar(front_n[:, t, :], xb[:, t, :], moments[:, t, 0:1], rstd[:, t:t + 1], ALU.subtract, ALU.mult))
                front_settle(ph, b)
                front_step_of(V_.tensor_tensor(front_n[:], front_n[:], both(W(ph, "gamma")), ALU.mult))
                front_settle(ph, b)
                V_.tensor_tensor(front_n[:], front_n[:], both(W(ph, "beta")), ALU.add).then_inc(front_ready.sem, 1)

            def l3_queries_keys(ph, b):
                for g in range(NG3):
                    dve.wait_ge(proj_psum.sem, proj_psum(ph, b, g + 1))
                    two = 2 + 2 * (g % 2)
                    if g:
                        dve.wait_ge(qkv_ready.sem, qkv_ready(ph, b, g))
                    front_step_of(rope(qT[:, g, :], pb[two], "cosq", "sinq", ph, b))
                    front_settle(ph, b)
                    rope(kT[:, g, :], pb[two + 1], "cosk", "sink", ph, b).then_inc(qkv_ready.sem, 1)
                front_end(ph, b)

            def l3_front(b, ph="l3_attn"):
                front_row(ph, b, True)
                front_step_of(front_adaln(ph, b))
                l3_square(ph, b)
                l3_norm(ph, b)
                l3_queries_keys(ph, b)

            def l3_attn(b, following, ph="l3_attn"):
                start_main(ph, b)
                for s in range(H + 3):
                    if following is not None and s == 2:
                        front_row(ph, following, False)
                    if following is not None and s == 5:
                        front_step_of(front_adaln(ph, following))
                        l3_square(ph, following)
                    if following is not None and s == 7:
                        l3_norm(ph, following)
                    if s < H:
                        row_max(ph, b, s, FULL)
                    if 2 <= s < H + 2:
                        take_probsT(ph, b, s - 2, FULL)
                    if s >= 3 and (s - 3) % 4 == 3:
                        u = (s - 3) // 4
                        hs = slice(4 * u, 4 * u + 4)
                        dve.wait_ge(pv_done.sem, pv_done(ph, b, 4 * u + 4))
                        step(V_.reciprocal(rinv[:, hs, :], rowsum[:, hs, :]))
                        settle(ph, b)
                        for t in range(T):
                            last = V_.tensor_tensor(O[:, t, 4 * u * HD3:(4 * u + 4) * HD3].rearrange("p (h d) -> p h d", h=4),
                                                    pb[u % 2][:, t * 256:(t + 1) * 256].rearrange("p (h d) -> p h d", h=4),
                                                    rinv[:, hs, t].unsqueeze(2).to_broadcast([P, 4, HD3]), ALU.mult)
                        last.then_inc(o_ready.sem, 1)
                if following is not None:
                    l3_queries_keys(ph, following)
                dve.wait_ge(out_psum.sem, out_psum(ph, b, 1))
                step(V_.tensor_copy(sum_b[:], tiles(pb[0][:, 0:T * D])))
                end_main(ph, b)

            def l3_ffn(b, ph="l3_ffn"):
                take_row(ph, b)
                adaln(ph, b).then_inc(tok_ready.sem, 1)
                dve.wait_ge(gate_psum.sem, gate_psum(ph, b, 1))
                step(V_.tensor_scalar(small[0][:, 0:T * E3], pb[1][:, 0:T * E3], CLIP3, None, ALU.max))
                settle(ph, b)
                step(V_.memset(gap[:], 0.0))
                step(V_.tensor_copy(routes[:, :, bass.ds(b, 1), :], small[0][:, 0:T * E3].rearrange("p (t o e) -> p t o e", t=T, o=1)))
                step(V_.tensor_copy(big[:, bass.ds(b, 1), :], feat[:].unsqueeze(1)))
                V_.tensor_copy(gates_all[:, bass.ds(b, 1), :], gate_b[:].unsqueeze(1)).then_inc(pass_done.sem, 1)
                assert count[0] == DVE_STEPS[ph], f"NSTEPS main {ph} {count[0]}"

            def l3_route():
                n = [0]

                def then(ins):
                    n[0] += 1
                    ins.then_inc(sink_step, 1)
                    dve.wait_ge(sink_step, n[0])

                over_t = lambda v: v.unsqueeze(1).to_broadcast([P, T, B * E3])
                cols = routes[:].rearrange("p t b e -> p t (b e)")
                rows = routes[:].rearrange("p t b e -> p (t b) e")
                cs = colsum[:].rearrange("p b e -> p (b e)")
                over_e = lambda v: v.unsqueeze(2).to_broadcast([P, T * B, E3])
                dve.wait_ge(sink_max, 1)
                then(V_.tensor_tensor(cs, colmax[:, 0:B * E3], colmax[:, B * E3:], ALU.max))
                then(V_.reciprocal(colmax[:, 0:B * E3], cs))
                V_.tensor_tensor(cols, cols, over_t(colmax[:, 0:B * E3]), ALU.mult).then_inc(sink_next, 1)
                for r in range(ROUNDS3):
                    dve.wait_ge(sink_sum, r + 1)
                    then(V_.reciprocal(cs, pb[0][:, 0:B * E3]))
                    then(V_.tensor_tensor(cols, cols, over_t(cs), ALU.mult))
                    then(V_.tensor_reduce(rowsum3[:], rows, AX.X, ALU.add))
                    then(V_.reciprocal(best[:], rowsum3[:]))
                    V_.tensor_tensor(rows, rows, over_e(best[:]), ALU.mult).then_inc(sink_next, 1)
                R = B * E3
                gate, work, key, strict, seen, same, run, one = (qT[0:R, i, :] for i in range(8))
                top = small[9][0:R, 0:M3]
                dve.wait_ge(sink_sum, ROUNDS3 + 1)
                then(V_.tensor_copy(gate, pb[1][0:R, 0:S]))
                then(V_.memset(one, 1.0))
                then(V_.memset(strict, 0.0))
                then(V_.memset(seen, 0.0))
                src, other = gate, [work, key]
                for i in range(M3 // 8):
                    then(V_.max(top[:, 8 * i:8 * i + 8], src))
                    then(V_.match_replace(other[i % 2], top[:, 8 * i:8 * i + 8], src, -1.0))
                    src = other[i % 2]
                for m in range(M3):
                    v = top[:, m:m + 1]
                    then(V_.scalar_tensor_tensor(strict, gate, v, strict, ALU.is_lt, ALU.add))
                    then(V_.tensor_scalar(same, gate, v, None, ALU.is_equal))
                    then(V_.tensor_tensor_scan(run, one, same, 0.0, ALU.mult, ALU.add))
                    then(V_.tensor_tensor(run, run, same, ALU.mult))
                    then(V_.tensor_tensor(seen, seen, run, ALU.max))
                then(V_.tensor_tensor(strict, strict, seen, ALU.add))
                then(V_.tensor_scalar(same, src, 0.0, None, ALU.is_lt))
                then(V_.tensor_scalar(strict, strict, float(E3), -float(E3), ALU.mult, ALU.add))
                V_.scalar_tensor_tensor(key, strict, C("expert1", R), same, ALU.add, ALU.mult).then_inc(sink_next, 1)
                dve.wait_ge(sink_sum, ROUNDS3 + 2)
                keys = masks3[:].rearrange("p t b e -> p (t b) e")
                won = colmax[:].rearrange("p (r e) -> p r e", e=E3)
                then(V_.tensor_copy(masks3[:].rearrange("p t b e -> p (t b e)"), pb[0][:, 0:T * R]))
                then(V_.tensor_reduce(best[:], keys, AX.X, ALU.max))
                then(V_.tensor_tensor(won, keys, over_e(best[:]), ALU.is_equal))
                then(V_.tensor_scalar(keys, keys, 0.0, None, ALU.is_gt))
                then(V_.tensor_tensor(won, won, keys, ALU.mult))
                then(V_.tensor_scalar(rows, rows, 0.5, None, ALU.is_gt))
                then(V_.tensor_tensor(keys, won, rows, ALU.mult))

            def l3_out(b, ph="l3_out"):
                count[0] = 0
                dve.wait_ge(pass_done.sem, pass_done(ph, b, 1))
                step(V_.memset(gap[:], 0.0))
                step(V_.tensor_copy(xb[:], x[:, bass.ds(b * T, T), :]))
                step(V_.tensor_copy(gate_b[:].unsqueeze(1), gates_all[:, bass.ds(b, 1), :]))
                step(V_.tensor_copy(small[0][:, 0:T * E3].rearrange("p (t o e) -> p t o e", t=T, o=1), masks3[:, :, bass.ds(b, 1), :]))
                V_.tensor_copy(feat[:].unsqueeze(1), big[:, bass.ds(b, 1), :]).then_inc(row_ready.sem, 1)
                settle(ph, b)
                for t in range(T):
                    dve.wait_ge(expert_psum.sem, expert_psum(ph, b, t + 1))
                for e in range(E3):
                    for t in range(T):
                        o = pb[2 + 2 * t + e // 4][:, e % 4 * D:(e % 4 + 1) * D]
                        w = small[0][:, t * E3 + e:t * E3 + e + 1]
                        if e == 0:
                            step(V_.tensor_scalar(sum_b[:, t, :], o, w, None, ALU.mult))
                        else:
                            step(V_.scalar_tensor_tensor(sum_b[:, t, :], o, w, sum_b[:, t, :], ALU.mult, ALU.add))
                    settle(ph, b)
                add_gated(ph, b)
                put_row(ph, b)

            V_.memset(ones[:], 1.0).then_inc(fixed_ready, 1)
            V_.memset(ones_e[:], 1.0).then_inc(fixed_ready, 1)
            V_.memset(minus_half[:], -0.5).then_inc(fixed_ready, 1)
            V_.memset(half[:], 0.5).then_inc(fixed_ready, 1)
            V_.memset(big[:, 0:2 * NG, :], 0.0).then_inc(stacks_clear, 1)
            dve.wait_ge(fixed_ready, 4)
            dve.wait_ge(ali_loaded, 16 * HPG)
            V_.tensor_copy(stack.rearrange("p g side n -> p (g side) n"), big[:, 0:2 * NG, :]).then_inc(stacks_clear, 1)
            dve.wait_ge(stacks_clear, 2)
            dve.wait_ge(x_loaded, 16)
            dve.wait_ge(silu_done, 1)
            dve.wait_ge(const_loaded, 16)
            V_.memset(gap[:], 0.0).then_inc(pass_done.sem, 1)
            dve.wait_ge(loaded[0], 16)
            plain_front(0, "l0_attn")
            with dve.Fori(0, B - 1) as b:
                plain_attn(b, "l0_attn", b + 1)
            plain_attn(B - 1, "l0_attn", None)
            dve.wait_ge(loaded[1], 16)
            dve.wait_ge(pass_done.sem, pass_done("l0_ffn", 0, 1))
            V_.memset(stack, 0.0).then_inc(stacks_clear, 1)
            dve.wait_ge(stacks_clear, 3)
            l0_front(0)
            with dve.Fori(0, B - 1) as b:
                l0_ffn(b, b + 1)
            l0_ffn(B - 1, None)
            dve.wait_ge(loaded[2], 16)
            l1_keep_counts()
            l1_front(0)
            with dve.Fori(0, B - 1) as b:
                l1_attn(b, b + 1)
            l1_attn(B - 1, None)
            dve.wait_ge(loaded[3], 16)
            with dve.Fori(0, B) as b:
                l1_ffn(b)
            dve.wait_ge(loaded[4], 16)
            plain_front(0, "l2_attn")
            with dve.Fori(0, B - 1) as b:
                plain_attn(b, "l2_attn", b + 1)
            plain_attn(B - 1, "l2_attn", None)
            dve.wait_ge(loaded[5], 16)
            with dve.Fori(0, B) as b:
                l2_ffn(b)
            dve.wait_ge(loaded[6], 16)
            l3_front(0)
            with dve.Fori(0, B - 1) as b:
                l3_attn(b, b + 1)
            l3_attn(B - 1, None)
            dve.wait_ge(loaded[7], 16)
            with dve.Fori(0, B) as b:
                l3_ffn(b)
            l3_route()
            with dve.Fori(0, B) as b:
                l3_out(b)

        @block.scalar
        def _(act):
            def take_turn(ph, b, n, width=P, dst=None):
                act.wait_ge(turned.sem, turned(ph, b, n))
                nc.scalar.activation(feat[0:width, :] if dst is None else dst, pb[0][0:width, 0:T * P], ACT.Copy).then_inc(feat_ready.sem, 1)

            def take_front(ph, b, n=1, width=P):
                act.wait_ge(front_turned.sem, front_turned(ph, b, n))
                nc.scalar.activation(next_feat[0:width, :], pb[5][0:width, 0:T * P], ACT.Copy).then_inc(front_feat.sem, 1)

            def take_out(ph, b, n=1):
                act.wait_ge(turned.sem, turned(ph, b, n))
                nc.scalar.activation(feat[:], pb[1][:, 0:T * P], ACT.Copy).then_inc(feat_ready.sem, 1)

            def exps(ph, b, blocks, following=None):
                for h in range(H):
                    if following is not None and h == (11 if ph in ("l0_ffn", "l3_attn") else 8):
                        take_front(ph, following)
                    act.wait_ge(max_ready.sem, max_ready(ph, b, h + 1))
                    if h >= 3:
                        act.wait_ge(probsT_psum.sem, probsT_psum(ph, b, h - 2))
                    bank = pb[score_banks(ph)[h % len(score_banks(ph))]]
                    for t, at, n in blocks:
                        last = nc.scalar.activation(probs[:, h % 3, at:at + n], bank[:, at:at + n], ACT.Exp,
                                                    bias=nmax[:, h, t:t + 1], accum_out=rowsum[:, h, t:t + 1])
                    last.then_inc(probs_ready.sem, 1)

            def plain_front(b, ph):
                take_front(ph, b)

            def plain_attn(b, ph, following):
                exps(ph, b, CAUSAL, following)
                take_out(ph, b)

            def l0_front(b, ph="l0_ffn"):
                take_front(ph, b)
                take_front(ph, b, 2, 64)

            def l0_ffn(b, following, ph="l0_ffn"):
                exps(ph, b, CAUSAL, following)
                if following is not None:
                    take_front(ph, following, 2, 64)
                take_out(ph, b)
                take_out(ph, b, 2)
                for n in range(2 * E0):
                    e, u = n // 2, n % 2
                    act.wait_ge(hid_psum.sem, hid_psum(ph, b, n + 1))
                    if e >= 2:
                        act.wait_ge(expert_psum.sem, expert_psum(ph, b, e - 1))
                    for c in range(2):
                        at = e * C0 + 2 * u + c
                        last = nc.scalar.activation(hid[:, e % 2, 2 * u + c, :], pb[2 + n % 3][:, c * S:(c + 1) * S], ACT.Relu,
                                                    bias=W(ph, "b1")[:, at:at + 1])
                    last.then_inc(hid_ready.sem, 1)

            def l1_exps(ph, b, h):
                act.wait_ge(max_ready.sem, max_ready(ph, b, h + 1))
                bank = pb[score_banks(ph)[h % len(score_banks(ph))]]
                for t in range(T):
                    last = nc.scalar.activation(big[:, h * T + t, :], bank[:, t * S:(t + 1) * S], ACT.Exp,
                                                bias=nmax[:, h, t:t + 1], accum_out=rowsum[:, h, t:t + 1])
                last.then_inc(probs_ready.sem, 1)

            def l1_front(b, ph="l1_attn"):
                take_front(ph, b)
                for h in range(H):
                    l1_exps(ph, b, h)

            def l1_attn(b, following, ph="l1_attn"):
                with act.Fori(0, QUICK_STEPS) as it:
                    act.wait_ge(mid_ready.sem, mid_ready(ph, b, 1) + it)
                    for j in range(ROWS_DVE, ROWS1):
                        last = nc.scalar.activation(signs[j - ROWS_DVE], big[:, j, :], ACT.Sign, bias=neg_mid[:, j:j + 1],
                                                    accum_out=tried[:, 1, j:j + 1])
                    last.then_inc(counts_act.sem, 1)
                if following is not None:
                    take_front(ph, following)
                for h in range(H):
                    act.wait_ge(probsT_psum.sem, probsT_psum(ph, b, h + 1))
                    if h >= 2:
                        act.wait_ge(pv_done.sem, pv_done(ph, b, h - 1))
                    nc.scalar.activation(probsT[:, h % 2, :], pb[6 + h % 2][:], ACT.Copy).then_inc(probsT_ready.sem, 1)
                    if following is not None:
                        l1_exps(ph, following, h)
                take_out(ph, b)

            def l1_ffn(b, ph="l1_ffn"):
                take_turn(ph, b, 1)
                act.wait_ge(max_route.sem, max_route(ph, b, 1))
                nc.scalar.activation(small[1][:, 0:T * E1], small[0][:, 0:T * E1], ACT.Exp).then_inc(exp_route.sem, 1)
                for e in range(EA):
                    act.wait_ge(hid_psum.sem, hid_psum(ph, b, e + 1))
                    if e >= 2:
                        act.wait_ge(hid_ready.sem, hid_ready(ph, b, e - 1))
                    nc.scalar.activation(hid[:, e % 2, 1, :], pb[2 + e % 4][:, 0:S], ACT.Silu).then_inc(silu_g.sem, 1)

            def l2_ffn(b, ph="l2_ffn"):
                take_turn(ph, b, 1)
                take_turn(ph, b, 2, E2, feat_o[0:E2, 0, :])
                act.wait_ge(z_psum.sem, z_psum(ph, b, 1))
                nc.scalar.activation(feat_o[0:R2, 1:3, :], pb[3][0:R2, :].rearrange("p (u n) -> p u n", u=2), ACT.Copy).then_inc(gated.sem, 1)
                for u in range(2):
                    act.wait_ge(hid_psum.sem, hid_psum(ph, b, u + 1))
                    nc.scalar.activation(hid[:, 0, 2 * u:2 * u + 2, :], pb[4 + u][:].rearrange("p (c n) -> p c n", c=2), ACT.Gelu).then_inc(hid_ready.sem, 1)

            def l3_values(ph, b):
                for t in range(T):
                    act.wait_ge(v_psum.sem, v_psum(ph, b, t + 1))
                    for j in range(2):
                        last = nc.scalar.activation(V[:, t, j * 512:(j + 1) * 512], pb[6 + j][:], ACT.Copy)
                    last.then_inc(v_ready.sem, 1)

            def l3_front(b, ph="l3_attn"):
                take_front(ph, b)
                l3_values(ph, b)

            def l3_attn(b, following, ph="l3_attn"):
                exps(ph, b, FULL, following)
                if following is not None:
                    l3_values(ph, following)
                for u in range(4):
                    act.wait_ge(o_turned.sem, o_turned(ph, b, u + 1))
                    nc.scalar.activation(feat_o[:, 2 * u:2 * u + 2, :], pb[2 + u][:].rearrange("p (c n) -> p c n", c=2), ACT.Copy).then_inc(o_feat.sem, 1)

            act.wait_ge(c_loaded, 16)
            nc.scalar.activation(silu_c[:], silu_c[:], ACT.Silu).then_inc(silu_done, 1)
            plain_front(0, "l0_attn")
            with act.Fori(0, B - 1) as b:
                plain_attn(b, "l0_attn", b + 1)
            plain_attn(B - 1, "l0_attn", None)
            act.wait_ge(loaded[1], 16)
            l0_front(0)
            with act.Fori(0, B - 1) as b:
                l0_ffn(b, b + 1)
            l0_ffn(B - 1, None)
            act.wait_ge(keep_exp, 1)
            nc.scalar.activation(small[1][:, 0:H], small[0][:, 0:H], ACT.Exp, scale=-1.0).then_inc(keep_exped, 1)
            l1_front(0)
            with act.Fori(0, B - 1) as b:
                l1_attn(b, b + 1)
            l1_attn(B - 1, None)
            with act.Fori(0, B) as b:
                l1_ffn(b)
            plain_front(0, "l2_attn")
            with act.Fori(0, B - 1) as b:
                plain_attn(b, "l2_attn", b + 1)
            plain_attn(B - 1, "l2_attn", None)
            with act.Fori(0, B) as b:
                l2_ffn(b)
            l3_front(0)
            with act.Fori(0, B - 1) as b:
                l3_attn(b, b + 1)
            l3_attn(B - 1, None)
            with act.Fori(0, B) as b:
                take_turn("l3_ffn", b, 1)


def shape_constants():
    out = {"ident": np.eye(P)}
    row = np.arange(P)
    out["first"] = np.tile(np.arange(E0, 0, -1.0), (P, 1))
    out["order8"] = np.tile(np.arange(LEFT), (P, 1))
    k = np.arange(1, E2 + 1)
    out["karange"], out["kinv"] = np.tile(k, (P, 1)), np.tile(1.0 / k, (P, 1))
    out["restart"] = np.tile(k > 1, (P, T))
    out["expert1"] = (row % E3 + 1)[:, None]
    return out


def alibi_rows():
    slope = (2.0 ** (-8.0 / H * (np.arange(H) + 1))).astype(np.float32)
    part = []
    for _ in range(PARTS):
        part.append((slope.view(np.uint32) & np.uint32(0xFFFF0000)).view(np.float32))
        slope = slope - part[-1]
    pos = np.arange(S, dtype=np.float32)
    out = np.zeros((HPG, ALI_ROWS, NG, 2, S), np.float32)
    for u in range(PARTS):
        by_head = part[u].reshape(NG, HPG).T[:, :, None]
        out[:, u, :, 0], out[:, u, :, 1] = by_head, pos
        out[:, PARTS + u, :, 0], out[:, PARTS + u, :, 1] = -pos, by_head
    return out.reshape(HPG, ALI_ROWS, -1)


def rope_tables(angle, dim, half, scale):
    inside = dim >= 0
    sign = np.where(dim % (2 * half) < half, -1.0, 1.0)[:, None]
    cos, sin = np.cos(angle) * inside[:, None], np.sin(angle) * sign * inside[:, None]
    return {"cosq": cos * scale, "sinq": sin * scale, "cosk": cos, "sink": sin}


def rope_small():
    dim = np.arange(P) // HALF % HD
    inv = (1.0 / 10000.0 ** (np.arange(HD // 2, dtype=np.float32) / np.float32(HD // 2))).astype(np.float32)
    angle = (np.arange(S, dtype=np.float32)[None, :] * inv[dim % (HD // 2)][:, None]).astype(np.float64)
    return rope_tables(angle, dim, HD // 2, HD ** -0.5)


def rope_wide():
    dim = np.arange(P) % HD3
    inv = (1.0 / np.float32(10000.0) ** (np.arange(0, HD3, 2, dtype=np.float32) / HD3)).astype(np.float32)
    pos = np.maximum(np.arange(S) - 1, 0).astype(np.float32)
    angle = (pos[None, :] * inv[dim % (HD3 // 2)][:, None]).astype(np.float64)
    return rope_tables(angle, dim, HD3 // 2, HD3 ** -0.5)


def by_dimension(w):
    return w.reshape(-1, 2, HALF, HPG, HD).transpose(0, 3, 1, 4, 2).reshape(w.shape[0], -1)


def column(v):
    return by_dimension(v[None, :]).T


def swap_halves(w, width):
    n = w.shape[0]
    return w.reshape(n, -1, 2, width // 2)[:, :, ::-1].reshape(n, -1)


def everywhere(v):
    return np.broadcast_to(v[None, :], (P, v.shape[0]))


def laid_out(a):
    attn0 = lambda wq, wk, wv, bq, bk, bv, wo, bo: {
        "wq": by_dimension(wq), "wk": by_dimension(wk), "wv": wv, "bq": column(bq), "bk": column(bk),
        "bv": everywhere(bv), "wo": wo, "bo": everywhere(bo)}
    w, b = a["L0_attn_W_qkv"], a["L0_attn_b_qkv"]
    out = {"l0_attn": attn0(w[:, :D], w[:, D:2 * D], w[:, 2 * D:], b[:D], b[D:2 * D], b[2 * D:], a["L0_attn_W_out"], a["L0_attn_b_out"])}
    f = lambda n: a["L0_ffn_" + n]
    out["l0_ffn"] = {
        "n1": everywhere(f("norm1_w")), "n2": everywhere(f("norm2_w")),
        "wq": by_dimension(f("Wq").T), "wqr": by_dimension(swap_halves(f("Wq").T, HD)), "wdkv": f("Wdkv").T,
        "lng": everywhere(f("ln_g")), "lnb": everywhere(f("ln_b")),
        "wuk": by_dimension(f("Wuk").T), "wukr": by_dimension(swap_halves(f("Wuk").T, HD)), "wuv": f("Wuv").T, "wo": f("Wo").T,
        "gate": f("gate_w").T, "gateb": everywhere(f("gate_b")),
        "w1": f("W1").transpose(2, 0, 1).reshape(D, -1), "b1": f("b1").reshape(E0 * C0, P).T,
        "w2": f("W2").reshape(E0, D, C0, P).transpose(3, 0, 2, 1).reshape(P, -1), "b2": f("b2").reshape(1, -1)}
    f = lambda n: a["L1_attn_" + n]
    out["l1_attn"] = attn0(f("Wq").T, f("Wk").T, f("Wv").T, f("bq"), f("bk"), f("bv"), f("Wo").T, f("bo"))
    out["l1_attn"].update(ema=everywhere(f("entropy_ema")), thr=everywhere(f("entropy_threshold")))
    f = lambda n: a["L1_ffn_" + n]
    out["l1_ffn"] = {
        "router": f("router_w").T, "routerb": everywhere(f("router_bias")),
        "gate": np.concatenate([f("gate_w").transpose(2, 0, 1).reshape(D, -1), f("sgate_w").T], 1),
        "up": np.concatenate([f("up_w").transpose(2, 0, 1).reshape(D, -1), f("sup_w").T], 1),
        "down": np.concatenate([f("down_w").transpose(2, 0, 1).reshape(P, -1),
                                f("sdown_w").reshape(D, SH1, P).transpose(2, 1, 0).reshape(P, -1)], 1)}
    f = lambda n: a["L2_attn_" + n]
    out["l2_attn"] = attn0(f("wq"), f("wk"), f("wv"), f("bq"), f("bk"), f("bv"), f("wo"), f("bo"))
    f = lambda n: a["L2_ffn_" + n]
    out["l2_ffn"] = {
        "proj": f("proj"), "c1": f("C1"), "c2": f("C2"), "win1": f("Win1")[:D], "win1b": f("Win1")[D:].T,
        "wout1": f("Wout1").T, "win2": f("Win2")[:O2 * P].reshape(O2, P, R2).transpose(1, 0, 2).reshape(P, -1),
        "win2b": f("Win2")[O2 * P:].T, "wout2": f("Wout2").T}
    w = a["L3_attn_w_qkv"]
    n = H * HD3
    four = [w[:, :n], swap_halves(w[:, :n], HD3), w[:, n:2 * n], swap_halves(w[:, n:2 * n], HD3)]
    out["l3_attn"] = {
        "gamma": everywhere(a["L3_attn_ln_gamma"]), "beta": everywhere(a["L3_attn_ln_beta"]),
        "wqk": np.stack([v.reshape(D, NG3, P) for v in four], 2).reshape(D, -1), "wv": w[:, 2 * n:],
        "wo": a["L3_attn_w_out"].reshape(NG3, P, D).transpose(1, 0, 2).reshape(P, -1)}
    out["l3_ffn"] = {"gate": a["L3_ffn_gate_w"][0], "experts": a["L3_ffn_experts"].transpose(1, 0, 2).reshape(D, -1)}
    for i, ph in enumerate(WEIGHED):
        half = a[f"L{i // 2}_wmod"]
        out[ph]["wmod"] = half[:, :3 * D] if i % 2 == 0 else half[:, 3 * D:]
    out["l0_ffn"].update(rope_small())
    out["l3_attn"].update(rope_wide())
    return out


def side_by_side(cols, parts):
    at, n = offsets(cols)
    out = np.zeros((P, n), np.float32)
    for name, (first, width) in at.items():
        part = parts[name]
        assert part.shape[1] == width, (name, part.shape, width)
        out[:part.shape[0], first:first + width] = part
    return out


def kernel(**inputs):
    import concourse.bacc as bacc
    from concourse.bass_utils import run_bass_kernel_spmd

    a = {k: np.asarray(v) for k, v in inputs.items()}
    arrays = {"x": np.ascontiguousarray(a["L0_attn_x"]),
              "c": np.ascontiguousarray(np.stack([a[f"L{i}_c"] for i in range(4)]).reshape(4 * B, D).T),
              "const": side_by_side(CONSTS, shape_constants())}
    arrays["ali"] = alibi_rows()
    weights = laid_out(a)
    for ph in WEIGHED:
        arrays["weights_" + ph] = side_by_side(COLUMNS[ph], weights[ph])
    nc = bacc.Bacc("TRN2", target_bir_lowering=False, num_devices=1)
    dram = {k: nc.dram_tensor("in_" + k, v.shape, F32, kind="ExternalInput").ap() for k, v in arrays.items()}
    out = nc.dram_tensor("out", (B, S, D), F32, kind="ExternalOutput").ap()
    adaln_program(nc, dram["x"], dram["c"], dram["const"], dram["ali"], {ph: dram["weights_" + ph] for ph in WEIGHED}, out)
    r = run_bass_kernel_spmd(nc, [{"in_" + k: v for k, v in arrays.items()}], core_ids=[0])
    return r.results[0]["out"]
```

```python
import numpy as np
from contextlib import ExitStack

import concourse.bass as bass
from concourse import mybir

F32 = mybir.dt.float32
BF16 = mybir.dt.bfloat16
I32 = mybir.dt.int32
ALU = mybir.AluOpType
ACT = mybir.ActivationFunctionType
AX = mybir.AxisListType

P = 128
B, S, D = 8, 256, 128
T = S // P
H = 16
HD = D // H
HPG = 2
NG = H // HPG
PARTS = 3
SLOTS = [(0, 0), (1, 0), (2, 0), (0, 1), (1, 1), (0, 2)]
ALI_ROWS = 2 * PARTS
HALF = NG // 2
EXPANDS = HPG * len(SLOTS)
HD3 = 64
NG3 = H // 2
E0, C0 = 4, 4
E1, TOP1, SH1 = 32, 4, 4
EA = E1 + SH1
E2, R2, O2 = 16, 64, 4
E3 = 8
M3 = S // E3
ROUNDS3 = 8
LN_EPS, RMS_EPS = 1e-5, 1e-6
CLIP3 = 1e-6
MASKED = -1e30

SEARCH_LO = -2.0 ** -6
SEARCH_SPAN = 1.0 + 2.0 ** -5
SEARCH_STEPS = 24
LAST_STEP = SEARCH_SPAN * 2.0 ** -SEARCH_STEPS
ROWS1 = H * T
ROWS_DVE = 18
QUICK_STEPS = 5
QUICK_LO, QUICK_HI = 0.5, 0.6
UNSEEN = -10.0
LEFT = 8
QUICK_RAISES = 8
BISECT_RAISES = 5

PHASES = ["l0_attn", "l0_ffn", "l1_attn", "l1_ffn", "l2_attn", "l2_ffn", "l3_attn", "l3_ffn", "l3_out"]
WEIGHED = PHASES[:-1]
PAIRS = B // 2
PASSES = {**dict.fromkeys(PHASES, B), "l1_ffn": PAIRS, "l2_ffn": PAIRS, "l3_ffn": 1, "l3_out": PAIRS}
ONCE = dict.fromkeys(PHASES, 1)

ATTN = [("wmod", 3 * D), ("wq", D), ("wk", D), ("wv", D), ("bq", 1), ("bk", 1),
        ("bv", D), ("wo", D), ("bo", D)]
ROPE = [("cosq", S), ("sinq", S), ("cosk", S), ("sink", S)]
COLUMNS = {
    "l0_attn": ATTN,
    "l0_ffn": [("wmod", 3 * D), ("n1", D), ("n2", D), ("wq", D), ("wqr", D), ("wdkv", 64),
               ("lng", 64), ("lnb", 64), ("wuk", D), ("wukr", D), ("wuv", D), ("wo", D),
               ("gate", E0), ("gateb", E0), ("w1", E0 * C0 * P), ("b1", E0 * C0), ("w2", E0 * C0 * D), ("b2", E0 * D)] + ROPE,
    "l1_attn": ATTN + [("ema", H), ("thr", H)],
    "l1_ffn": [("wmod", 3 * D), ("router", E1), ("routerb", E1), ("gate", EA * P), ("up", EA * P), ("down", EA * D)],
    "l2_attn": ATTN,
    "l2_ffn": [("wmod", 3 * D), ("proj", E2), ("c12", 2 * R2), ("win1", R2), ("win1b", 1),
               ("wout1", O2 * P), ("win2", O2 * P), ("win2b", 1), ("wout2", D)],
    "l3_attn": [("wmod", 3 * D), ("gamma", D), ("beta", D), ("wqk", NG3 * 4 * P), ("wv", H * HD3), ("wo", NG3 * D)] + ROPE,
    "l3_ffn": [("wmod", 3 * D), ("gate", E3), ("experts", E3 * D)],
}
CONSTS = [("ident", P), 
          ("first", E0), ("order8", LEFT), ("karange", E2), ("kinv", E2), ("expert1", 1)]



def offsets(cols):
    at, out = 0, {}
    for name, n in cols:
        out[name] = (at, n)
        at += n
    return out, at


class Signal:

    def __init__(self, sem, per, passes=PASSES, before=0):
        self.sem, self.per = sem, per
        self.base = {}
        total = before
        for ph in PHASES:
            self.base[ph] = total
            total += per.get(ph, 0) * passes[ph]

    def __call__(self, ph, b, n):
        return b * self.per[ph] + (self.base[ph] + n)


DVE_STEPS = {"l0_attn": 4, "l0_ffn": 25, "l1_attn": 181, "l1_ffn": 4, "l2_attn": 4, "l2_ffn": 3, "l3_attn": 7, "l3_out": 36}
FRONT_STEPS = {"l0_attn": 20, "l0_ffn": 41, "l1_attn": 20, "l2_attn": 20, "l3_attn": 64}
SELECT_STEPS = 150


def adaln_program(nc, x_in, c_in, const_in, ali_in, weights_in, out):
    ctx = ExitStack()
    with ctx:
        def sb(name, shape, dt=F32):
            return ctx.enter_context(nc.sbuf_tensor(name, shape, dt))

        def signal(name, **per):
            return Signal(ctx.enter_context(nc.semaphore(name)), per)

        def wide_signal(name, **per):
            return Signal(ctx.enter_context(nc.semaphore(name)), per, ONCE)

        def once(name):
            return ctx.enter_context(nc.semaphore(name))

        x = sb("x", [P, B * T, D])
        consts_at, n_const = offsets(CONSTS)
        const = sb("const", [P, n_const])

        def C(name, rows=P):
            at, n = consts_at[name]
            return const[0:rows, at:at + n]

        places = {ph: offsets(COLUMNS[ph]) for ph in WEIGHED}
        region = [sb(f"weights{i}", [P, max(places[ph][1] for ph in WEIGHED[i::2])]) for i in range(2)]

        def W(ph, name, rows=P):
            at, n = places[ph][0][name]
            return region[WEIGHED.index(ph) % 2][0:rows, at:at + n]

        silu_c = sb("silu_c", [P, 4 * B])
        silu_b = sb("silu_b", [P, P])
        ones = sb("ones", [P, P])
        identb = sb("identb", [P, P], BF16)
        future = sb("future", [P, P], BF16)
        minus_half = sb("minus_half", [P, B * T])

        xb = sb("xb", [P, T, D])
        hb = sb("hb", [P, T, D])
        nb = sb("nb", [P, T, D])
        sum_b = sb("sum_b", [P, T, D])
        gate_b = sb("gate_b", [P, D])
        next_gate_b = sb("next_gate_b", [P, D])
        gate_sign = sb("gate_sign", [P, D])
        next_feat = sb("next_feat", [P, T * P])
        scale_b = sb("scale_b", [P, D])
        stats = sb("stats", [P, T, 6])
        moments = sb("moments", [P, T, 2])
        square = sb("square", [P, T])
        var = sb("var", [P, T])
        rstd = sb("rstd", [P, T])
        gap = sb("gap", [P, 1])
        main_stats = sb("main_stats", [P, T, 6])
        main_moments = sb("main_moments", [P, T, 2])
        main_square = sb("main_square", [P, T])
        main_var = sb("main_var", [P, T])
        main_rstd = sb("main_rstd", [P, T])
        front_n = sb("front_n", [P, T, D])
        feat = sb("feat", [P, T * P])
        feat_o = sb("feat_o", [P, NG3, T * P])
        qT = sb("qT", [P, NG3, S])
        kT = sb("kT", [P, NG3, S])
        rope_c = sb("rope_c", [P, S])
        rope_s = sb("rope_s", [P, S])
        V = sb("V", [P, T, H * HD3])
        nmax = sb("nmax", [P, H, T])
        rowsum = sb("rowsum", [P, H, T])
        rinv = sb("rinv", [P, H, T])
        probs = sb("probs", [P, 3, T * S])
        probsT = sb("probsT", [P, 2, T * S])
        O = sb("O", [P, T, H * HD3])
        big = sb("big", [P, ROWS1, S])
        small = [sb(f"small{i}", [P, T * E1]) for i in range(10)]
        hid = sb("hid", [P, 2, C0, T * P])
        keep, aim, low, mid, neg_mid, above, counts = (
            sb(n, [P, ROWS1]) for n in ("keep", "aim", "low", "mid", "neg_mid", "above", "counts"))
        tried, under, over = (small[i][:, 0:2 * ROWS1].rearrange("p (u j) -> p u j", u=2) for i in range(3))
        enough, short = (small[3][:, i * ROWS1:(i + 1) * ROWS1] for i in range(2))
        part, span = (small[4][:, i * ROWS1:(i + 1) * ROWS1] for i in range(2))
        left, doubt = (small[5][:, i * ROWS1:(i + 1) * ROWS1] for i in range(2))
        largest = small[6][:].rearrange("p (j e) -> p j e", e=LEFT)
        past = small[7][:].rearrange("p (j e) -> p j e", e=LEFT)
        doubts = small[8][:, 0:1]
        rkept = small[9][:, 0:H * T].rearrange("p (h t) -> p h t", t=T)
        doubts_i = sb("doubts_i", [1, 1], I32)
        width = sb("width", [P, 1])
        keep_i = sb("keep_i", [P, H], I32)
        ones_e = sb("ones_e", [P, E1])

        def halves(buffer):
            axes = " ".join("abc"[:len(buffer.shape) - 1])
            return buffer.rearrange(f"p {axes} -> p ({axes})").bitcast(BF16).rearrange("p (j k) -> p j k", k=S)

        masks = halves(hid[:])
        spare = halves(feat_o[:])
        flags = [masks[:, j, :] for j in range(16)] + [halves(probs[:])[:, 8 + j, :] for j in range(ROWS_DVE - 16)]
        signs = [spare[:, j, :] for j in range(ROWS1 - ROWS_DVE)]
        bisect_flags = [masks[:, j, :] for j in range(16)] + [spare[:, j, :] for j in range(16)]
        candidates = hid[:].rearrange("p u c n -> p (u c) n")
        marked = feat_o[:]
        within = halves(probs[:])[:, 0:8, :]
        place = halves(O[:, 1:2, :])
        restart = halves(kT[:, 0:NG3 // 2, :])
        stack = halves(qT[:]).rearrange("p (g side) n -> p g side n", side=2)
        compact, rest = kT[:, 4:6, :], kT[:, 6:8, :]
        parts = sb("parts", [P, 2 * PARTS, S], BF16)

        def pair(rows, of_query, of_key):
            first, last = PARTS - 1 - of_query, PARTS + of_key
            return parts[rows, first:last + 1:last - first, :]

        keys = big[:, 0:H, :]
        routes = sb("routes", [P, T, B, E3])
        masks3 = sb("masks3", [P, T, B, E3])
        gates_all = V[:, 0, :].rearrange("p (b d) -> p b d", b=B)
        N16 = B * T

        def rows(first, n):
            return big[:, first:first + n, :].rearrange("p r k -> p (r k)")

        feats = big[:, 0:B, :]
        normed = rows(8, 8).rearrange("p (j d) -> p j d", d=D)
        silu_8 = rows(16, 4).rearrange("p (b n) -> p b n", b=B)
        gate_mag, gate_two = rows(20, 4), rows(24, 4)
        wide_stats = rows(28, 1)[:, 0:6 * N16].rearrange("p (j n) -> p j n", n=6)
        wide_moments = rows(28, 1)[:, 96:128].rearrange("p (j n) -> p j n", n=2)
        wide_var, wide_rstd = rows(28, 1)[:, 128:144], rows(28, 1)[:, 144:160]
        shift_8, scale_8 = rows(28, 1)[:, 160:168], rows(28, 1)[:, 168:176]
        one, total = rows(29, 1)[:, 0:N16], rows(29, 1)[:, N16:2 * N16]
        top8 = rows(29, 1)[:, 128:256].rearrange("p (j e) -> p j e", e=8)
        weights_all = rows(30, 2).rearrange("p (j e) -> p j e", e=E1)
        ranks_gate, ranks_z = big[:, 20:28, :], big[0:R2, 8:16, :]
        pair_feat = O[:, 0, 0:2 * S]
        pair_sum = O[:, 1, 0:2 * S].rearrange("p (j d) -> p j d", d=D)
        pair_weight = O[:, 0, 512:640].rearrange("p (j e) -> p j e", e=E1)
        pair_rank2 = O[R2:2 * R2, 0, 512:1024]
        colmax = sb("colmax", [P, T * B * E3])
        colsum = sb("colsum", [P, B, E3])
        rowsum3 = sb("rowsum3", [P, T * B])
        best = sb("best", [P, T * B])
        pb = [ctx.enter_context(nc.psum_tensor(f"bank{i}", [P, 512], F32)) for i in range(8)]

        every = dict.fromkeys(PHASES, 1)
        attn = ("l0_attn", "l0_ffn", "l1_attn", "l2_attn", "l3_attn")
        heads = dict.fromkeys(attn, H)
        n_norm = {"l0_ffn": 1}
        n_turn = {"l0_attn": 1, "l0_ffn": 2, "l1_attn": 1, "l2_attn": 1}
        narrow_phases = ("l0_attn", "l0_ffn", "l1_attn", "l2_attn")
        n_proj = {"l0_attn": 2, "l0_ffn": 4, "l1_attn": 2, "l2_attn": 2, "l3_attn": NG3}
        n_qkv = {**n_proj, "l0_ffn": 3}
        x_loaded, c_loaded, const_loaded, silu_done, masks_ready, stored = map(
            once, ("x_loaded", "c_loaded", "const_loaded", "silu_done", "masks_ready", "stored"))
        fixed_ready = once("fixed_ready")
        loaded = [once(f"weights_loaded_{ph}") for ph in WEIGHED]
        pass_done = signal("pass_done", **every)
        wide = ("l1_ffn", "l2_ffn", "l3_ffn")
        wide_step = once("wide_step")
        wide_silu = wide_signal("wide_silu", **dict.fromkeys(wide, 1))
        wide_mod = wide_signal("wide_mod", **dict.fromkeys(wide, 2))
        n_wide_norm = {"l1_ffn": 1, "l2_ffn": 2, "l3_ffn": 1}
        wide_var_ready = wide_signal("wide_var_ready", **n_wide_norm)
        wide_rstd_ready = wide_signal("wide_rstd_ready", **n_wide_norm)
        wide_ready = wide_signal("wide_ready", **dict.fromkeys(wide, PAIRS))
        wide_turned = wide_signal("wide_turned", **dict.fromkeys(wide, PAIRS))
        wide_scaled = wide_signal("wide_scaled", **dict.fromkeys(wide, 1))
        wide_feat = wide_signal("wide_feat", **dict.fromkeys(wide, PAIRS))
        wide_logits = wide_signal("wide_logits", **dict.fromkeys(wide, 1))
        pair_ready = signal("pair_ready", l1_ffn=1, l2_ffn=1, l3_out=1)
        var_ready = signal("var_ready", **n_norm)
        rstd_ready = signal("rstd_ready", **n_norm)
        tok_ready = signal("tok_ready", **n_turn)
        turned = signal("turned", **n_turn)
        feat_ready = signal("feat_ready", **n_turn)
        proj_psum = signal("proj_psum", **n_proj)
        qkv_ready = signal("qkv_ready", **n_qkv)
        parts_ready = signal("parts_ready", **dict.fromkeys(narrow_phases, 1))
        stacked = [signal(f"stacked_half{u}", **dict.fromkeys(narrow_phases, 16 * EXPANDS)) for u in range(2)]
        ali_loaded, stacks_clear = once("ali_loaded"), once("stacks_clear")
        scores_psum = signal("scores_psum", **heads)
        max_ready = signal("max_ready", **heads)
        probs_ready = signal("probs_ready", **heads)
        probsT_psum = signal("probsT_psum", **heads)
        probsT_ready = signal("probsT_ready", **heads)
        pv_done = signal("pv_done", **heads)
        out_psum = signal("out_psum", l0_attn=1, l0_ffn=1, l1_attn=1, l2_attn=1, l2_ffn=1, l3_attn=1)
        dve_step = signal("dve_step", **DVE_STEPS)
        led = dict.fromkeys(FRONT_STEPS, 1)
        front_step = signal("front_step", **FRONT_STEPS)
        front_silu = signal("front_silu", **led)
        front_mod = signal("front_mod", **led)
        n_front_norm = {**led, "l0_ffn": 3, "l3_attn": 2}
        n_front_turn = {**led, "l0_ffn": 2}
        front_var = signal("front_var", **n_front_norm)
        front_rstd = signal("front_rstd", **n_front_norm)
        front_ready = signal("front_ready", **n_front_turn)
        front_turned = signal("front_turned", **n_front_turn)
        front_feat = signal("front_feat", **n_front_turn)
        gate_psum = signal("gate_psum", l0_ffn=1)
        hid_psum = signal("hid_psum", l0_ffn=E0 * 2, l1_ffn=EA, l2_ffn=O2)
        hid_ready = signal("hid_ready", l0_ffn=E0 * 2, l1_ffn=EA, l2_ffn=O2)
        silu_g = signal("silu_g", l1_ffn=EA)
        expert_psum = signal("expert_psum", l0_ffn=E0, l1_ffn=EA, l3_out=2)
        expert_used = signal("expert_used", l0_ffn=E0, l1_ffn=EA)
        keep_exp, keep_exped, keep_count = once("keep_exp"), once("keep_exped"), once("keep_count")
        mid_ready = signal("mid_ready", l1_attn=QUICK_STEPS)
        counts_act = signal("counts_act", l1_attn=QUICK_STEPS)
        quick_step = signal("quick_step", l1_attn=QUICK_STEPS * QUICK_RAISES)
        bisect_step = signal("bisect_step", l1_attn=SEARCH_STEPS * BISECT_RAISES)
        doubts_ready = signal("doubts_ready", l1_attn=1)
        doubts_psum = signal("doubts_psum", l1_attn=1)
        kept_ready = signal("kept_ready", l1_attn=H)
        max_route, exp_route = once("max_route"), once("exp_route")
        delta_ready, root_ready = once("delta_ready"), once("root_ready")
        mix_ready, mix_turned, mix_feat, ranks_psum, ranks_ready = map(
            once, ("mix_ready", "mix_turned", "mix_feat", "ranks_psum", "ranks_ready"))
        z_psum = Signal(ctx.enter_context(nc.semaphore("z_psum")), {"l2_ffn": 1}, before=PAIRS)
        z_ready = signal("z_ready", l2_ffn=1)
        keys_clear = once("keys_clear")
        v_psum = signal("v_psum", l3_attn=2)
        v_ready = signal("v_ready", l3_attn=2)
        routes_ready = once("routes_ready")
        sink_max, sink_next, sink_sum, sink_step = map(once, ("sink_max", "sink_next", "sink_sum", "sink_step"))
        o_ready = signal("o_ready", l3_attn=4)
        o_turned = signal("o_turned", l3_attn=4)
        o_feat = signal("o_feat", l3_attn=4)

        block = ctx.enter_context(nc.Block())

        def tiles(flat):
            return flat.rearrange("p (t n) -> p t n", t=T)

        def both(row):
            return row.unsqueeze(1).to_broadcast([P, T, row.shape[1]])


        def score_banks(ph):
            return [2, 3, 4, 0] if ph == "l1_attn" else [2, 3, 4]

        CAUSAL = [(0, 0, 128), (1, 128, 256)]
        FULL = [(0, 0, 256), (1, 256, 256)]

        def early(ph):
            return ph in ("l0_attn", "l2_attn")

        def rows_of(h):
            return slice(64 * (h % 2), 64 * (h % 2) + 64), h // 2

        def risen(e):
            return hid[:, e % 2, 2:4, :].rearrange("p c n -> p (c n)")

        def silus(e):
            return hid[:, e % 2, 0:2, :].rearrange("p c n -> p (c n)")

        def gelus(c):
            return hid[:, c // 2, 2 * (c % 2):2 * (c % 2) + 2, :].rearrange("p c n -> p (c n)")

        def mix_T(u):
            return hid[0:E2, u // 2, 2 * (u % 2):2 * (u % 2) + 2, :].rearrange("p c n -> p (c n)")

        mix = rows(17, 1).rearrange("p (j e) -> p j e", e=E2)
        RANK_BANKS = (0, 1, 6, 7)

        def turned_input(ph):
            return front_n[:] if ph in ("l0_ffn", "l3_attn") else xb[:]

        @block.sync
        def _(sp):
            sp.dma_start(x[:], x_in.rearrange("b (t p) d -> p (b t) d", p=P)).then_inc(x_loaded, 16)
            sp.dma_start(silu_c[:], c_in).then_inc(c_loaded, 16)
            sp.dma_start(const[:], const_in).then_inc(const_loaded, 16)
            for i in range(HPG):
                sp.wait_ge(stacks_clear, 1)
                sp.dma_start(big[64 * i + 48:64 * i + 48 + ALI_ROWS, 0:2 * NG, :], ali_in[i].rearrange("r (s n) -> r s n", n=S)).then_inc(ali_loaded, 16)

            def load(i):
                n = places[WEIGHED[i]][1]
                sp.dma_start(region[i % 2][:, 0:n], weights_in[WEIGHED[i]]).then_inc(loaded[i], 16)

            def expand(ph, b, first=False):
                sp.wait_ge(parts_ready.sem, parts_ready(ph, b, 1))
                for u in range(2):
                    if not first:
                        sp.wait_ge(scores_psum.sem, scores_psum(ph, b, (u - 1) * H // 2))
                    for i in range(HPG):
                        for slot, of in enumerate(SLOTS):
                            to = slice(64 * i + HD * slot, 64 * i + HD * slot + HD)
                            at = slice((2 * i + u) * HD * HALF, (2 * i + u + 1) * HD * HALF)
                            sp.dma_start(stack[to, u * HALF:(u + 1) * HALF], pair(at, *of)).then_inc(stacked[u].sem, 16)

            load(0)
            load(1)
            for i, ph in enumerate(WEIGHED):
                if 1 <= i < len(WEIGHED) - 1:
                    sp.wait_ge(pass_done.sem, pass_done(ph, 0, 1))
                    load(i + 1)
                if ph in narrow_phases:
                    expand(ph, 0, i == 0)
                    with sp.Fori(0, B - 1) as b:
                        expand(ph, b + 1)
            sp.wait_ge(pass_done.sem, sum(PASSES.values()) + 1)
            sp.dma_start(out.rearrange("b (t p) d -> p (b t) d", p=P), x[:]).then_inc(stored, 16)
            sp.wait_ge(stored, 16)

        @block.gpsimd
        def _(pool):
            nc.gpsimd.memset(identb[:], 0.0).then_inc(masks_ready, 1)
            nc.gpsimd.memset(future[:], 0.0).then_inc(masks_ready, 1)
            pool.wait_ge(masks_ready, 2)
            nc.gpsimd.affine_select(out=identb[:], in_=identb[:], compare_op=ALU.not_equal, fill=1.0, base=0,
                                    pattern=[[-1, P]], channel_multiplier=1).then_inc(masks_ready, 1)
            nc.gpsimd.affine_select(out=future[:], in_=future[:], compare_op=ALU.is_ge, fill=MASKED, base=0,
                                    pattern=[[-1, P]], channel_multiplier=1).then_inc(masks_ready, 1)
            pool.wait_ge(fixed_ready, 3)

            def prepare(ph, b):
                for n in range(n_front_norm[ph]):
                    pool.wait_ge(front_var.sem, front_var(ph, b, n + 1))
                    nc.gpsimd.tensor_tensor(rstd[:], var[:], minus_half[:, 0:T], ALU.pow).then_inc(front_rstd.sem, 1)

            def finish(ph, b):
                pool.wait_ge(var_ready.sem, var_ready(ph, b, 1))
                nc.gpsimd.tensor_tensor(main_rstd[:], main_var[:], minus_half[:, 0:T], ALU.pow).then_inc(rstd_ready.sem, 1)

            for ph in WEIGHED:
                if ph in FRONT_STEPS:
                    prepare(ph, 0)
                    if ph == "l3_attn":
                        nc.gpsimd.memset(keys, 0.0).then_inc(keys_clear, 1)
                    with pool.Fori(0, B - 1) as b:
                        prepare(ph, b + 1)
                        if ph in n_norm:
                            finish(ph, b)
                    if ph in n_norm:
                        finish(ph, B - 1)
                    continue
                for n in range(n_wide_norm[ph]):
                    pool.wait_ge(wide_var_ready.sem, wide_var_ready(ph, 0, n + 1))
                    nc.gpsimd.tensor_tensor(wide_rstd, wide_var, minus_half[:], ALU.pow).then_inc(wide_rstd_ready.sem, 1)
                if ph == "l3_ffn":
                    pool.wait_ge(routes_ready, 1)
                    nc.gpsimd.partition_all_reduce(colmax[:], routes[:].rearrange("p t b e -> p (t b e)"), P,
                                                   bass.bass_isa.ReduceOp.max).then_inc(sink_max, 1)

        @block.tensor
        def _(pe):
            mm = nc.tensor.matmul

            def wide_front(ph, logits):
                pe.wait_ge(pass_done.sem, pass_done(ph, 0, 1))
                layer = PHASES.index(ph) // 2
                for j in range(2):
                    last = mm(pb[0][:, j * B:(j + 1) * B], W(ph, "wmod")[:, j * D:(j + 1) * D],
                              silu_c[:, layer * B:(layer + 1) * B], start=True, stop=True)
                last.then_inc(wide_mod.sem, 1)
                pe.wait_ge(wide_silu.sem, wide_silu(ph, 0, 1))
                for b in range(B):
                    last = mm(pb[6 + b // 4][:, b % 4 * D:(b % 4 + 1) * D], silu_8[:, b, :], W(ph, "wmod")[:, 2 * D:3 * D],
                              start=True, stop=True)
                last.then_inc(wide_mod.sem, 1)
                for u in range(PAIRS):
                    pe.wait_ge(wide_ready.sem, wide_ready(ph, 0, u + 1))
                    for i in range(4):
                        last = nc.tensor.transpose(pb[2 + u][:, i * P:(i + 1) * P], normed[:, 4 * u + i, :], C("ident"))
                    last.then_inc(wide_turned.sem, 1)
                n = W(ph, logits).shape[1]
                for u in range(PAIRS):
                    pe.wait_ge(wide_feat.sem, wide_feat(ph, 0, u + 1))
                    for j in range(4 * u, 4 * u + 4):
                        last = mm(pb[1][:, j * n:(j + 1) * n], feats[:, j // T, j % T * P:(j % T + 1) * P], W(ph, logits),
                                  start=True, stop=True)
                last.then_inc(wide_logits.sem, 1)

            def front_modulation(ph, b):
                pe.wait_ge(front_silu.sem, front_silu(ph, b, 1))
                mm(pb[5][:, 0:3 * D], silu_b[:], W(ph, "wmod"), start=True, stop=True).then_inc(front_mod.sem, 1)

            def keep_busy(ph, bank, n=1, width=S):
                for _ in range(n):
                    mm(pb[bank][:, S:S + width], C("ident"), W(ph, "wmod")[:, 0:width], start=True, stop=True)

            def front_turn(ph, b, src, n=1):
                pe.wait_ge(front_ready.sem, front_ready(ph, b, n))
                for t in range(T):
                    last = nc.tensor.transpose(pb[5][:, t * P:(t + 1) * P], src[:, t, :], C("ident"))
                last.then_inc(front_turned.sem, 1)

            def project_qkv(ph, b):
                pe.wait_ge(front_feat.sem, front_feat(ph, b, 1))
                f = next_feat[:]
                mm(pb[0][:, 0:S], W(ph, "wq"), f, start=True, stop=True)
                mm(pb[0][:, S:2 * S], W(ph, "wk"), f, start=True, stop=True).then_inc(proj_psum.sem, 1)
                for t in range(T):
                    last = mm(pb[5][:, S + t * D:S + (t + 1) * D], f[:, t * P:(t + 1) * P], W(ph, "wv"), start=True, stop=True)
                last.then_inc(proj_psum.sem, 1)

            def scores(ph, b, h, blocks):
                rows, g = rows_of(h)
                n_banks = len(score_banks(ph))
                bank = pb[score_banks(ph)[h % n_banks]]
                if h % (H // 2) == 0 and ph in narrow_phases:
                    half_in_place = stacked[h // (H // 2)]
                    pe.wait_ge(half_in_place.sem, half_in_place(ph, b, 16 * EXPANDS))
                if h < n_banks:
                    n = n_qkv[ph] - 1 if ph == "l3_attn" and h < 2 else n_qkv[ph]
                    pe.wait_ge(qkv_ready.sem, qkv_ready(ph, b, 1 if ph in narrow_phases else n))
                else:
                    pe.wait_ge(probs_ready.sem, probs_ready(ph, b, h + 1 - n_banks))
                for t, at, n in blocks:
                    causal = blocks is CAUSAL
                    if ph in narrow_phases:
                        qs, ks = stack[rows, g, 0, :], stack[rows, g, 1, :]
                    else:
                        qs, ks = qT[:, g, :], keys[:, h, :]
                    last = mm(bank[:, at:at + n], qs[:, t * P:(t + 1) * P], ks[:, 0:n],
                              start=True, stop=not causal)
                    if causal:
                        last = mm(bank[:, at + t * P:at + n], identb[:], future[:], start=False, stop=True)
                last.then_inc(scores_psum.sem, 1)

            def turn_probs(ph, b, h, src, blocks):
                if h >= 2:
                    pe.wait_ge(probsT_ready.sem, probsT_ready(ph, b, h - 1))
                for _, at, n in blocks:
                    for k in range(n // P):
                        cols = slice(at + k * P, at + (k + 1) * P)
                        last = nc.tensor.transpose(pb[6 + h % 2][:, cols], src[:, cols], C("ident"))
                last.then_inc(probsT_psum.sem, 1)

            def weigh(ph, b, h, o, v, blocks):
                if h == 0 and ph in narrow_phases:
                    pe.wait_ge(qkv_ready.sem, qkv_ready(ph, b, n_qkv[ph]))
                pe.wait_ge(probsT_ready.sem, probsT_ready(ph, b, h + 1))
                for t, at, n in blocks:
                    for k in range(n // P):
                        last = mm(o(t), probsT[:, h % 2, at + k * P:at + (k + 1) * P], v(k),
                                  start=k == 0, stop=k == n // P - 1)
                last.then_inc(pv_done.sem, 1)

            def narrow_attention(ph, b, blocks, following=None):
                width = HD
                def o(h):
                    return lambda t: pb[1][:, (t * H + h) * width:(t * H + h + 1) * width]

                def v(h):
                    return lambda k: V[:, k, h * width:(h + 1) * width]

                for s in range(H + 3):
                    if s == 2 and ph == "l0_ffn":
                        pe.wait_ge(qkv_ready.sem, qkv_ready(ph, b, n_qkv[ph]))
                        keep_busy(ph, 0, 4)
                    if s == 2 and ph in FRONT_STEPS:
                        pe.wait_ge(pass_done.sem, pass_done(ph, b, 1))
                    if following is not None and s == 4:
                        front_modulation(ph, following)
                    if following is not None and s == (9 if ph == "l0_ffn" else 6):
                        front_turn(ph, following, turned_input(ph))
                    if following is not None and s == (11 if ph == "l0_ffn" else 7):
                        if ph == "l0_ffn":
                            l0_queries(ph, following)
                        else:
                            project_qkv(ph, following)
                    if following is not None and ph == "l0_ffn" and s == 14:
                        l0_latent(ph, following)
                    if following is not None and ph == "l0_ffn" and s == 16:
                        l0_keys_values(ph, following)
                    if s < H and not (early(ph) and s < len(score_banks(ph))):
                        scores(ph, b, s, blocks)
                    if s == 2 and ph == "l0_ffn":
                        keep_busy(ph, 0, 5)
                    if 2 <= s < H + 2:
                        pe.wait_ge(probs_ready.sem, probs_ready(ph, b, s - 1))
                        turn_probs(ph, b, s - 2, probs[:, (s - 2) % 3, :], blocks)
                    if 3 <= s < H + 2:
                        keep_busy(ph, 1, 1, P)
                    if ph == "l0_ffn" and 5 <= s < H + 2:
                        keep_busy(ph, 1, 2 if s < 10 else 1)
                    if s >= 3:
                        weigh(ph, b, s - 3, o(s - 3), v(s - 3), blocks)

            def turn_out(ph, b, following=None):
                if following is not None:
                    keep_busy(ph, 0, 2)
                pe.wait_ge(tok_ready.sem, tok_ready(ph, b, 1))
                for t in range(T):
                    last = nc.tensor.transpose(pb[1][:, t * P:(t + 1) * P], O[:, t, 0:D], C("ident"))
                last.then_inc(turned.sem, 1)
                if following is not None:
                    first_scores(ph, following)
                pe.wait_ge(feat_ready.sem, feat_ready(ph, b, 1))
                for t in range(T):
                    last = mm(pb[1][:, S + t * D:S + (t + 1) * D], feat[:, t * P:(t + 1) * P], W(ph, "wo"), start=True, stop=True)
                last.then_inc(out_psum.sem, 1)
                if following is not None:
                    keep_busy(ph, 0, 4)

            def first_scores(ph, b):
                for h in range(len(score_banks(ph))):
                    scores(ph, b, h, CAUSAL)

            WARM_UP = 8

            def plain_front(b, ph):
                front_modulation(ph, b)
                front_turn(ph, b, xb)
                project_qkv(ph, b)
                if early(ph):
                    keep_busy(ph, 1, WARM_UP)
                    first_scores(ph, b)

            def plain_attn(b, ph, following):
                narrow_attention(ph, b, CAUSAL, following)
                if following is not None:
                    pe.wait_ge(qkv_ready.sem, qkv_ready(ph, following, 1))
                turn_out(ph, b, following)

            def l0_queries(ph, b):
                pe.wait_ge(front_feat.sem, front_feat(ph, b, 1))
                mm(pb[0][:, 0:S], W(ph, "wq"), next_feat[:], start=True, stop=True)
                mm(pb[0][:, S:2 * S], W(ph, "wqr"), next_feat[:], start=True, stop=True).then_inc(proj_psum.sem, 1)
                for t in range(T):
                    last = mm(pb[5][:, S + t * 64:S + (t + 1) * 64], next_feat[:, t * P:(t + 1) * P], W(ph, "wdkv"), start=True, stop=True)
                last.then_inc(proj_psum.sem, 1)

            def l0_latent(ph, b):
                front_turn(ph, b, front_n[:], 2)

            def l0_keys_values(ph, b):
                pe.wait_ge(front_feat.sem, front_feat(ph, b, 2))
                pe.wait_ge(qkv_ready.sem, qkv_ready(ph, b, 1))
                mm(pb[0][:, 0:S], W(ph, "wuk", 64), next_feat[0:64, :], start=True, stop=True)
                mm(pb[0][:, S:2 * S], W(ph, "wukr", 64), next_feat[0:64, :], start=True, stop=True).then_inc(proj_psum.sem, 1)
                for t in range(T):
                    last = mm(pb[5][:, S + t * D:S + (t + 1) * D], next_feat[0:64, t * P:(t + 1) * P], W(ph, "wuv", 64), start=True, stop=True)
                last.then_inc(proj_psum.sem, 1)

            def l0_front(b, ph="l0_ffn"):
                front_modulation(ph, b)
                front_turn(ph, b, front_n[:])
                l0_queries(ph, b)
                l0_latent(ph, b)
                l0_keys_values(ph, b)

            def l0_ffn(b, following, ph="l0_ffn"):
                narrow_attention(ph, b, CAUSAL, following)
                turn_out(ph, b)
                keep_busy(ph, 6, 10)
                pe.wait_ge(tok_ready.sem, tok_ready(ph, b, 2))
                for t in range(T):
                    last = nc.tensor.transpose(pb[1][:, t * P:(t + 1) * P], nb[:, t, :], C("ident"))
                last.then_inc(turned.sem, 1)
                pe.wait_ge(feat_ready.sem, feat_ready(ph, b, 2))
                for t in range(T):
                    last = mm(pb[1][:, t * E0:(t + 1) * E0], feat[:, t * P:(t + 1) * P], W(ph, "gate"), start=True, stop=True)
                last.then_inc(gate_psum.sem, 1)

                def rise(e):
                    for u in range(2):
                        n = 2 * e + u
                        if n >= 3:
                            pe.wait_ge(hid_ready.sem, hid_ready(ph, b, n - 2))
                        for c in range(2):
                            at = (e * C0 + 2 * u + c) * P
                            last = mm(pb[2 + n % 3][:, c * S:(c + 1) * S], W(ph, "w1")[:, at:at + P], feat[:], start=True, stop=True)
                        last.then_inc(hid_psum.sem, 1)

                def fall(e):
                    pe.wait_ge(hid_ready.sem, hid_ready(ph, b, 2 * e + 2))
                    if e >= 2:
                        pe.wait_ge(expert_used.sem, expert_used(ph, b, e - 1))
                    for t in range(T):
                        o = pb[6 + e % 2][:, t * D:(t + 1) * D]
                        for c in range(C0):
                            at = (e * C0 + c) * D
                            mm(o, hid[:, e % 2, c, t * P:(t + 1) * P], W(ph, "w2")[:, at:at + D], start=c == 0, stop=False)
                        last = mm(o, ones[0:1, :], W(ph, "b2", 1)[:, e * D:(e + 1) * D], start=False, stop=True)
                    last.then_inc(expert_psum.sem, 1)

                for e in range(E0 + 1):
                    if e < E0:
                        rise(e)
                    if e >= 1:
                        fall(e - 1)

            def l1_attn_front(b, ph="l1_attn"):
                plain_front(b, ph)
                for h in range(H):
                    scores(ph, b, h, FULL)

            def l1_attn(b, following, ph="l1_attn"):
                pe.wait_ge(probs_ready.sem, probs_ready(ph, b, H))
                pe.wait_ge(pass_done.sem, pass_done(ph, b, 1))
                if following is not None:
                    plain_front(following, ph)
                pe.wait_ge(doubts_ready.sem, doubts_ready(ph, b, 1))
                mm(pb[1][0:1, 0:1], ones[:, 0:1], doubts, start=True, stop=True).then_inc(doubts_psum.sem, 1)
                ahead = len(score_banks(ph))
                if following is not None:
                    for h in range(ahead):
                        scores(ph, following, h, FULL)
                width = HD + 1
                for s in range(H + 1):
                    if s < H:
                        pe.wait_ge(kept_ready.sem, kept_ready(ph, b, s + 1))
                        turn_probs(ph, b, s, big[:, 2 * s:2 * s + 2, :].rearrange("p t k -> p (t k)"), FULL)
                    if following is not None and 1 <= s and s - 1 + ahead < H:
                        scores(ph, following, s - 1 + ahead, FULL)
                    if s >= 1:
                        h = s - 1
                        weigh(ph, b, h, lambda t: pb[1][:, t * 256 + h * width:t * 256 + (h + 1) * width],
                              lambda k: V[:, k, h * width:(h + 1) * width], FULL)
                turn_out(ph, b)

            def l1_ffn(p, ph="l1_ffn"):
                pe.wait_ge(pair_ready.sem, pair_ready(ph, p, 1))

                def rise(e):
                    pe.wait_ge(hid_ready.sem, hid_ready(ph, p, e - 2))
                    cols = slice(e * P, (e + 1) * P)
                    two = (2, 4, 0)[e % 3]
                    mm(pb[two][:], W(ph, "gate")[:, cols], pair_feat, start=True, stop=True)
                    mm(pb[two + 1][:], W(ph, "up")[:, cols], pair_feat, start=True, stop=True).then_inc(hid_psum.sem, 1)

                def fall(e):
                    pe.wait_ge(hid_ready.sem, hid_ready(ph, p, e + 1))
                    pe.wait_ge(expert_used.sem, expert_used(ph, p, e - 1))
                    for j in range(2 * T):
                        last = mm(pb[6 + e % 2][:, j * D:(j + 1) * D], risen(e)[:, j * P:(j + 1) * P],
                                  W(ph, "down")[:, e * D:(e + 1) * D], start=True, stop=True)
                    last.then_inc(expert_psum.sem, 1)

                for e in range(EA + 2):
                    if e < EA:
                        rise(e)
                    if e >= 2:
                        fall(e - 2)

            def l2_front(ph="l2_ffn"):
                wide_front(ph, "proj")
                pe.wait_ge(mix_ready, 1)
                for u in range(PAIRS):
                    for i in range(4):
                        last = nc.tensor.transpose(pb[2 + u][0:E2, i * P:(i + 1) * P], mix[:, 4 * u + i, :], C("ident"))
                    last.then_inc(mix_turned, 1)
                for u in range(PAIRS):
                    mm(pb[RANK_BANKS[u]][0:R2, :], W(ph, "win1"), feats[:, 2 * u:2 * u + 2, :].rearrange("p r k -> p (r k)"),
                       start=True, stop=True).then_inc(z_psum.sem, 1)
                for u in range(PAIRS):
                    pe.wait_ge(mix_feat, u + 1)
                    mm(pb[2 + u][:], W(ph, "c12", E2), mix_T(u), start=True, stop=True).then_inc(ranks_psum, 1)

            def l2_rise(p, ph="l2_ffn"):
                pe.wait_ge(pair_ready.sem, pair_ready(ph, p, 1))
                for c in range(O2):
                    pe.wait_ge(hid_ready.sem, hid_ready(ph, p, c + 1 - O2))
                    mm(pb[2 + c][:], W(ph, "wout1", R2)[:, c * P:(c + 1) * P], pair_feat[0:R2, :], start=True, stop=True).then_inc(hid_psum.sem, 1)

            def l2_ffn(p, following, ph="l2_ffn"):
                for c in range(O2):
                    pe.wait_ge(hid_ready.sem, hid_ready(ph, p, c + 1))
                    last = mm(pb[6][:], W(ph, "win2")[:, c * P:(c + 1) * P], gelus(c), start=c == 0, stop=c == O2 - 1)
                last.then_inc(z_psum.sem, 1)
                if following is not None:
                    l2_rise(following)
                pe.wait_ge(pass_done.sem, pass_done(ph, p, 1))
                pe.wait_ge(z_ready.sem, z_ready(ph, p, 1))
                for j in range(2 * T):
                    last = mm(pb[7][:, j * D:(j + 1) * D], pair_rank2[:, j * P:(j + 1) * P], W(ph, "wout2")[R2:2 * R2, :], start=True, stop=True)
                last.then_inc(out_psum.sem, 1)

            def l3_project(ph, b, g):
                two = 2 + 2 * (g % 2)
                if g >= 2:
                    pe.wait_ge(qkv_ready.sem, qkv_ready(ph, b, g - 1))
                for j in range(4):
                    at = (g * 4 + j) * P
                    last = mm(pb[two + j // 2][:, (j % 2) * S:(j % 2 + 1) * S], W(ph, "wqk")[:, at:at + P], next_feat[:], start=True, stop=True)
                last.then_inc(proj_psum.sem, 1)

            def l3_values(ph, b, t):
                if t:
                    pe.wait_ge(v_ready.sem, v_ready(ph, b, 1))
                for j in range(2):
                    last = mm(pb[6 + j][:], next_feat[:, t * P:(t + 1) * P], W(ph, "wv")[:, j * 512:(j + 1) * 512], start=True, stop=True)
                last.then_inc(v_psum.sem, 1)

            def l3_front(b, ph="l3_attn"):
                front_modulation(ph, b)
                front_turn(ph, b, turned_input(ph))
                pe.wait_ge(front_feat.sem, front_feat(ph, b, 1))
                for g in range(NG3):
                    l3_project(ph, b, g)
                    if g in (1, 3):
                        l3_values(ph, b, g // 2)

            def l3_turn_out(ph, b, u):
                pe.wait_ge(o_ready.sem, o_ready(ph, b, u + 1))
                for j in range(2):
                    for t in range(T):
                        g = 2 * u + j
                        last = nc.tensor.transpose(pb[(6 + u) % 8][:, j * S + t * P:j * S + (t + 1) * P], O[:, t, g * P:(g + 1) * P], C("ident"))
                last.then_inc(o_turned.sem, 1)

            def l3_project_out(ph, b, t):
                if t == 0:
                    pe.wait_ge(o_feat.sem, o_feat(ph, b, 4))
                for g in range(NG3):
                    last = mm(pb[0][:, t * D:(t + 1) * D], feat_o[:, g, t * P:(t + 1) * P], W(ph, "wo")[:, g * D:(g + 1) * D],
                              start=g == 0, stop=g == NG3 - 1)
                if t == T - 1:
                    last.then_inc(out_psum.sem, 1)

            def l3_attn(b, following, ph="l3_attn"):
                pe.wait_ge(v_ready.sem, v_ready(ph, b, 2))
                keep_busy(ph, 6, 4)
                for s in range(H + 3):
                    if s == 2:
                        pe.wait_ge(pass_done.sem, pass_done(ph, b, 1))
                    if following is not None and s == 3:
                        front_modulation(ph, following)
                    if following is not None and s == 10:
                        front_turn(ph, following, turned_input(ph))
                    if s < H:
                        scores(ph, b, s, FULL)
                    if 2 <= s < H + 2:
                        pe.wait_ge(probs_ready.sem, probs_ready(ph, b, s - 1))
                        turn_probs(ph, b, s - 2, probs[:, (s - 2) % 3, :], FULL)
                    if s >= 3:
                        h = s - 3
                        if h >= 8 and h % 4 == 0:
                            pe.wait_ge(o_ready.sem, o_ready(ph, b, h // 4 - 1))
                        weigh(ph, b, h, lambda t: pb[h // 4 % 2][:, (t * 4 + h % 4) * HD3:(t * 4 + h % 4 + 1) * HD3],
                              lambda k: V[:, k, h * HD3:(h + 1) * HD3], FULL)
                pe.wait_ge(probsT_ready.sem, probsT_ready(ph, b, H))
                for u in range(2):
                    l3_turn_out(ph, b, u)
                if following is not None:
                    pe.wait_ge(front_feat.sem, front_feat(ph, following, 1))
                    l3_project(ph, following, 0)
                for u in range(2, 4):
                    l3_turn_out(ph, b, u)
                if following is not None:
                    l3_project(ph, following, 1)
                    pe.wait_ge(o_feat.sem, o_feat(ph, b, 2))
                    l3_values(ph, following, 0)
                for t in range(T):
                    l3_project_out(ph, b, t)
                    if following is not None:
                        l3_project(ph, following, 2 + 2 * t)
                        l3_project(ph, following, 3 + 2 * t)
                if following is not None:
                    l3_values(ph, following, 1)
                    for g in range(2 + 2 * T, NG3):
                        l3_project(ph, following, g)

            def l3_route():
                for r in range(ROUNDS3):
                    pe.wait_ge(sink_next, r + 1)
                    for t in range(T):
                        last = mm(pb[0][:, 0:B * E3], ones[:], routes[:, t].rearrange("p b e -> p (b e)"), start=t == 0, stop=t == T - 1)
                    last.then_inc(sink_sum, 1)
                pe.wait_ge(sink_next, ROUNDS3 + 1)
                for t in range(T):
                    last = nc.tensor.transpose(pb[1][0:B * E3, t * P:(t + 1) * P], routes[:, t].rearrange("p b e -> p (b e)"), C("ident"))
                last.then_inc(sink_sum, 1)
                pe.wait_ge(sink_next, ROUNDS3 + 2)
                n = B * E3
                for t in range(T):
                    last = nc.tensor.transpose(pb[0][:, t * n:(t + 1) * n], qT[0:n, 2, t * P:(t + 1) * P], C("ident", n)[:, 0:n])
                last.then_inc(sink_sum, 1)

            def l3_out(p, ph="l3_out"):
                pe.wait_ge(pair_ready.sem, pair_ready(ph, p, 1))
                for r in range(2):
                    if r:
                        pe.wait_ge(pass_done.sem, pass_done(ph, p, 1))
                    for t in range(T):
                        for j in range(2):
                            last = mm(pb[4 * r + 2 * t + j][:], pair_feat[:, (r * T + t) * P:(r * T + t + 1) * P],
                                      W("l3_ffn", "experts")[:, j * 512:(j + 1) * 512], start=True, stop=True)
                    last.then_inc(expert_psum.sem, 1)

            pe.wait_ge(masks_ready, 4)
            pe.wait_ge(const_loaded, 16)
            pe.wait_ge(fixed_ready, 3)
            pe.wait_ge(loaded[0], 16)
            plain_front(0, "l0_attn")
            with pe.Fori(0, B - 1) as b:
                plain_attn(b, "l0_attn", b + 1)
            plain_attn(B - 1, "l0_attn", None)
            pe.wait_ge(loaded[1], 16)
            l0_front(0)
            with pe.Fori(0, B - 1) as b:
                l0_ffn(b, b + 1)
            l0_ffn(B - 1, None)
            pe.wait_ge(loaded[2], 16)
            l1_attn_front(0)
            with pe.Fori(0, B - 1) as b:
                l1_attn(b, b + 1)
            l1_attn(B - 1, None)
            pe.wait_ge(loaded[3], 16)
            wide_front("l1_ffn", "router")
            pe.wait_ge(max_route, 1)
            with pe.Fori(0, PAIRS) as p:
                l1_ffn(p)
            pe.wait_ge(loaded[4], 16)
            plain_front(0, "l2_attn")
            with pe.Fori(0, B - 1) as b:
                plain_attn(b, "l2_attn", b + 1)
            plain_attn(B - 1, "l2_attn", None)
            pe.wait_ge(loaded[5], 16)
            l2_front()
            l2_rise(0)
            with pe.Fori(0, PAIRS - 1) as p:
                l2_ffn(p, p + 1)
            l2_ffn(PAIRS - 1, None)
            pe.wait_ge(loaded[6], 16)
            l3_front(0)
            with pe.Fori(0, B - 1) as b:
                l3_attn(b, b + 1)
            l3_attn(B - 1, None)
            pe.wait_ge(loaded[7], 16)
            wide_front("l3_ffn", "gate")
            l3_route()
            with pe.Fori(0, PAIRS) as p:
                l3_out(p)

        @block.vector
        def _(dve):
            V_ = nc.vector
            count = [0]

            def step(ins):
                count[0] += 1
                ins.then_inc(dve_step.sem, 1)

            def settle(ph, b):
                dve.wait_ge(dve_step.sem, dve_step(ph, b, count[0]))

            def settle_apart(ph, b):
                settle(ph, b)
                step(V_.memset(gap[:], 0.0))

            front_count = [0]

            def front_step_of(ins):
                front_count[0] += 1
                ins.then_inc(front_step.sem, 1)

            def front_settle(ph, b):
                dve.wait_ge(front_step.sem, front_step(ph, b, front_count[0]))

            def front_settle_apart(ph, b):
                front_settle(ph, b)
                front_step_of(V_.memset(gap[:], 0.0))

            def front_row(ph, b, first):
                front_count[0] = 0
                if first:
                    dve.wait_ge(pass_done.sem, pass_done(ph, b, 1))
                else:
                    dve.wait_ge(front_turned.sem, front_turned(ph, b, 0))
                front_step_of(V_.memset(gap[:], 0.0))
                front_step_of(V_.tensor_copy(xb[:], x[:, bass.ds(b * T, T), :]))
                layer = PHASES.index(ph) // 2
                V_.tensor_copy(silu_b[:], silu_c[:, bass.ds(b + layer * B, 1)].to_broadcast([P, P])).then_inc(front_silu.sem, 1)
                front_settle(ph, b)
                for t in range(T):
                    front_step_of(V_.bn_stats(stats[:, t, :], xb[:, t, :]))
                front_settle_apart(ph, b)
                for t in range(T):
                    front_step_of(V_.bn_aggr(moments[:, t, :], stats[:, t, :]))
                front_settle(ph, b)
                V_.tensor_scalar(var[:], moments[:, :, 1], LN_EPS, None, ALU.add).then_inc(front_var.sem, 1)

            def front_adaln(ph, b):
                front_norm(ph, b)
                return front_modulate(ph, b)

            def front_norm(ph, b):
                dve.wait_ge(front_rstd.sem, front_rstd(ph, b, 1))
                for t in range(T):
                    front_step_of(V_.tensor_scalar(xb[:, t, :], xb[:, t, :], moments[:, t, 0:1], rstd[:, t:t + 1], ALU.subtract, ALU.mult))

            def front_modulate(ph, b):
                dve.wait_ge(front_mod.sem, front_mod(ph, b, 1))
                shift, scale, gate = (pb[5][:, j * D:(j + 1) * D] for j in range(3))
                front_step_of(V_.tensor_scalar(scale_b[:], scale, 1.0, None, ALU.add))
                front_step_of(V_.tensor_scalar(next_gate_b[:], gate, -1.0, 0.25, ALU.mult, ALU.max))
                front_step_of(V_.tensor_scalar(gate_sign[:], gate, 0.0, 2.0, ALU.is_ge, ALU.mult))
                front_settle(ph, b)
                front_step_of(V_.tensor_tensor(xb[:], xb[:], both(scale_b[:]), ALU.mult))
                front_step_of(V_.tensor_tensor(next_gate_b[:], gate, next_gate_b[:], ALU.max))
                front_settle(ph, b)
                front_step_of(V_.scalar_tensor_tensor(next_gate_b[:], gate_sign[:], 1.0, next_gate_b[:], ALU.subtract, ALU.mult))
                return V_.tensor_tensor(xb[:], xb[:], both(shift), ALU.add)

            def front_end(ph, b):
                assert front_count[0] == FRONT_STEPS[ph], f"NSTEPS front {ph} {front_count[0]}"

            def start_main(ph, b):
                count[0] = 0
                dve.wait_ge(front_step.sem, front_step(ph, b, FRONT_STEPS[ph]))
                dve.wait_ge(pass_done.sem, pass_done(ph, b, 1))
                step(V_.tensor_copy(gate_b[:], next_gate_b[:]))
                settle(ph, b)

            def end_main(ph, b):
                settle(ph, b)
                step(V_.tensor_tensor(sum_b[:], sum_b[:], both(gate_b[:]), ALU.mult))
                settle(ph, b)
                row = x[:, bass.ds(b * T, T), :]
                V_.tensor_tensor(row, row, sum_b[:], ALU.add).then_inc(pass_done.sem, 1)
                assert count[0] == DVE_STEPS[ph], f"NSTEPS main {ph} {count[0]}"

            wide_count = [0]

            def wide_step_of(ins):
                wide_count[0] += 1
                ins.then_inc(wide_step, 1)

            def wide_settle():
                dve.wait_ge(wide_step, wide_count[0])

            def wide_front(ph):
                dve.wait_ge(pass_done.sem, pass_done(ph, 0, 1))
                layer = PHASES.index(ph) // 2
                V_.tensor_copy(silu_8, silu_c[:, layer * B:(layer + 1) * B].unsqueeze(2).to_broadcast([P, B, P])).then_inc(wide_silu.sem, 1)
                for j in range(N16):
                    wide_step_of(V_.bn_stats(wide_stats[:, j, :], x[:, j, :]))
                wide_settle()
                wide_step_of(V_.memset(gap[:], 0.0))
                for j in range(N16):
                    wide_step_of(V_.bn_aggr(wide_moments[:, j, :], wide_stats[:, j, :]))
                wide_settle()
                V_.tensor_scalar(wide_var, wide_moments[:, :, 1], LN_EPS, None, ALU.add).then_inc(wide_var_ready.sem, 1)
                dve.wait_ge(wide_mod.sem, wide_mod(ph, 0, 1))
                wide_step_of(V_.tensor_copy(shift_8, pb[0][:, 0:B]))
                V_.tensor_scalar(scale_8, pb[0][:, B:2 * B], 1.0, None, ALU.add).then_inc(wide_scaled.sem, 1)
                dve.wait_ge(wide_rstd_ready.sem, wide_rstd_ready(ph, 0, 1))
                for j in range(N16):
                    last = V_.tensor_scalar(normed[:, j, :], x[:, j, :], wide_moments[:, j, 0:1], wide_rstd[:, j:j + 1], ALU.subtract, ALU.mult)
                    if j % 4 == 3:
                        last.then_inc(wide_ready.sem, 1)

            def wide_gates(ph):
                dve.wait_ge(wide_mod.sem, wide_mod(ph, 0, 2))
                half = lambda v, u: v[:, u * 4 * D:(u + 1) * 4 * D]
                for u in range(2):
                    wide_step_of(V_.tensor_scalar(half(gate_mag, u), pb[6 + u][:], -1.0, 0.25, ALU.mult, ALU.max))
                    wide_step_of(V_.tensor_scalar(half(gate_two, u), pb[6 + u][:], 0.0, 2.0, ALU.is_ge, ALU.mult))
                wide_settle()
                for u in range(2):
                    wide_step_of(V_.tensor_tensor(half(gate_mag, u), pb[6 + u][:], half(gate_mag, u), ALU.max))
                wide_settle()
                wide_step_of(V_.scalar_tensor_tensor(gates_all, gate_two.rearrange("p (b d) -> p b d", b=B), 1.0,
                                                     gate_mag.rearrange("p (b d) -> p b d", b=B), ALU.subtract, ALU.mult))

            def each(row):
                return row.unsqueeze(1).to_broadcast([P, N16, row.shape[1]])

            def spread(v, n):
                return v.unsqueeze(2).to_broadcast([P, N16, n])

            def pair_rows(p):
                return x[:, bass.ds(p * 2 * T, 2 * T), :]

            def pair_gates(p):
                return gates_all[:, bass.ds(p * 2, 2), :].unsqueeze(2).to_broadcast([P, 2, T, D])

            def by_row(tiles_of_pair):
                return tiles_of_pair.rearrange("p (b t) d -> p b t d", t=T)

            def take_pair(ph, p):
                V_.tensor_copy(pair_feat.rearrange("p (r k) -> p r k", r=2), big[:, bass.ds(p * 2, 2), :]).then_inc(pair_ready.sem, 1)

            def row_max(ph, b, h, blocks):
                dve.wait_ge(scores_psum.sem, scores_psum(ph, b, h + 1))
                bank = pb[score_banks(ph)[h % len(score_banks(ph))]]
                if blocks is CAUSAL:
                    for t, at, n in blocks:
                        last = V_.tensor_reduce(nmax[:, h, t:t + 1], bank[:, at:at + n], AX.X, ALU.max, negate=True)
                else:
                    last = V_.tensor_reduce(nmax[:, h, :], tiles(bank[:]), AX.X, ALU.max, negate=True)
                last.then_inc(max_ready.sem, 1)

            def take_probsT(ph, b, h, blocks):
                n = blocks[-1][1] + blocks[-1][2]
                dve.wait_ge(probsT_psum.sem, probsT_psum(ph, b, h + 1))
                if h >= 2:
                    dve.wait_ge(pv_done.sem, pv_done(ph, b, h - 1))
                V_.tensor_copy(probsT[:, h % 2, 0:n], pb[6 + h % 2][:, 0:n]).then_inc(probsT_ready.sem, 1)

            def narrow_softmax(ph, b, blocks, following=None):
                for s in range(H + 2):
                    if s < H and not (early(ph) and s < len(score_banks(ph))):
                        row_max(ph, b, s, blocks)
                    if s >= 2:
                        take_probsT(ph, b, s - 2, blocks)
                    if following is None:
                        continue
                    if s == 2:
                        front_row(ph, following, False)
                    if s == 3:
                        front_norm(ph, following)
                    if ph == "l0_ffn":
                        if s == 4:
                            front_step_of(front_modulate(ph, following))
                        if s == 6:
                            l0_square(ph, following)
                        if s == 7:
                            l0_rms(ph, following)
                        if s == 11:
                            l0_queries(ph, following)
                        if s == 12:
                            l0_latent_stats(ph, following)
                        if s == 13:
                            l0_latent(ph, following)
                    else:
                        if s == 4:
                            front_modulate(ph, following).then_inc(front_ready.sem, 1)
                        if s == 7:
                            intake_qk(ph, following)
                        if 8 <= s < 8 + SPLITS:
                            split_step(ph, following, s - 8)
                dve.wait_ge(probs_ready.sem, probs_ready(ph, b, H))
                step(V_.reciprocal(rinv[:], rowsum[:]))
                settle(ph, b)
                dve.wait_ge(pv_done.sem, pv_done(ph, b, H))
                for t in range(T):
                    last = V_.tensor_tensor(O[:, t, 0:D].rearrange("p (h d) -> p h d", h=H),
                                            pb[1][:, t * D:(t + 1) * D].rearrange("p (h d) -> p h d", h=H),
                                            rinv[:, :, t].unsqueeze(2).to_broadcast([P, H, HD]), ALU.mult)
                last.then_inc(tok_ready.sem, 1)

            SPLITS = 2 * PARTS - 1

            def split_step(ph, b, n):
                front_settle(ph, b)
                if n == 0:
                    for half_in_place in stacked:
                        dve.wait_ge(half_in_place.sem, half_in_place(ph, b, 0))
                part = pair(slice(0, P), n // 2, n // 2)
                left = compact if n < 2 else rest
                if n % 2:
                    front_step_of(V_.tensor_tensor(rest, left, part, ALU.subtract))
                elif n < SPLITS - 1:
                    front_step_of(V_.tensor_copy(part, left))
                else:
                    V_.tensor_copy(part, left).then_inc(parts_ready.sem, 1)
                    front_end(ph, b)

            def split(ph, b):
                for n in range(SPLITS):
                    split_step(ph, b, n)

            def intake_qk(ph, b):
                dve.wait_ge(proj_psum.sem, proj_psum(ph, b, 1))
                front_step_of(V_.tensor_scalar(compact[:, 0, :], pb[0][:, 0:S], W(ph, "bq"), HD ** -0.5, ALU.add, ALU.mult))
                V_.tensor_scalar(compact[:, 1, :], pb[0][:, S:2 * S], W(ph, "bk"), None, ALU.add).then_inc(qkv_ready.sem, 1)
                dve.wait_ge(qkv_ready.sem, qkv_ready(ph, b, 1))

            def intake_values(ph, b):
                dve.wait_ge(proj_psum.sem, proj_psum(ph, b, 2))
                V_.tensor_tensor(V[:, :, 0:D], tiles(pb[5][:, S:S + T * D]), both(W(ph, "bv")), ALU.add).then_inc(qkv_ready.sem, 1)

            def intake_values_and_ones(ph, b):
                dve.wait_ge(proj_psum.sem, proj_psum(ph, b, 2))
                v1 = V[:, :, 0:H * (HD + 1)].rearrange("p t (h d) -> p t h d", h=H)
                for t in range(T):
                    last = V_.tensor_tensor(v1[:, t, :, 0:HD], pb[5][:, S + t * D:S + (t + 1) * D].rearrange("p (h d) -> p h d", h=H),
                                            W(ph, "bv").rearrange("p (h d) -> p h d", h=H), ALU.add)
                last.then_inc(qkv_ready.sem, 1)

            def plain_front(b, ph):
                front_row(ph, b, True)
                front_adaln(ph, b).then_inc(front_ready.sem, 1)
                intake_qk(ph, b)
                split(ph, b)
                intake_values(ph, b)
                first_maxima(ph, b)

            def first_maxima(ph, b):
                for h in range(len(score_banks(ph))):
                    row_max(ph, b, h, CAUSAL)

            def plain_attn(b, ph, following):
                start_main(ph, b)
                narrow_softmax(ph, b, CAUSAL, following)
                if following is not None:
                    intake_values(ph, following)
                    first_maxima(ph, following)
                dve.wait_ge(out_psum.sem, out_psum(ph, b, 1))
                step(V_.tensor_tensor(sum_b[:], tiles(pb[1][:, S:S + T * D]), both(W(ph, "bo")), ALU.add))
                end_main(ph, b)

            def rope_parts(bank, cos, sin, ph, b):
                front_step_of(V_.tensor_tensor(rope_c[:], bank[:, 0:S], W(ph, cos), ALU.mult))
                front_step_of(V_.tensor_tensor(rope_s[:], bank[:, S:2 * S], W(ph, sin), ALU.mult))
                front_settle(ph, b)

            def rope(dst, bank, cos, sin, ph, b):
                rope_parts(bank, cos, sin, ph, b)
                return V_.tensor_tensor(dst, rope_c[:], rope_s[:], ALU.add)

            def l0_square(ph, b):
                front_settle(ph, b)
                for t in range(T):
                    front_step_of(V_.bn_stats(stats[:, t, :], xb[:, t, :]))
                front_settle_apart(ph, b)
                for t in range(T):
                    front_step_of(V_.bn_aggr(moments[:, t, :], stats[:, t, :]))
                front_settle(ph, b)
                front_step_of(V_.tensor_tensor(square[:], moments[:, :, 0], moments[:, :, 0], ALU.mult))
                front_settle(ph, b)
                front_step_of(V_.tensor_tensor(square[:], square[:], moments[:, :, 1], ALU.add))
                front_settle(ph, b)
                V_.tensor_scalar(var[:], square[:], RMS_EPS, None, ALU.add).then_inc(front_var.sem, 1)

            def l0_rms(ph, b):
                dve.wait_ge(front_rstd.sem, front_rstd(ph, b, 2))
                for t in range(T):
                    front_step_of(V_.tensor_scalar(front_n[:, t, :], xb[:, t, :], rstd[:, t:t + 1], None, ALU.mult))
                front_settle(ph, b)
                V_.tensor_tensor(front_n[:], front_n[:], both(W(ph, "n1")), ALU.mult).then_inc(front_ready.sem, 1)

            def l0_queries(ph, b):
                dve.wait_ge(proj_psum.sem, proj_psum(ph, b, 1))
                rope(compact[:, 0, :], pb[0], "cosq", "sinq", ph, b).then_inc(qkv_ready.sem, 1)

            def latent_of():
                return pb[5][:, S:S + T * 64].rearrange("p (t n) -> p t n", t=T)

            def l0_latent_stats(ph, b):
                dve.wait_ge(proj_psum.sem, proj_psum(ph, b, 2))
                for t in range(T):
                    front_step_of(V_.bn_stats(stats[:, t, :], latent_of()[:, t, :]))
                front_settle_apart(ph, b)
                for t in range(T):
                    front_step_of(V_.bn_aggr(moments[:, t, :], stats[:, t, :]))
                front_settle(ph, b)
                V_.tensor_scalar(var[:], moments[:, :, 1], LN_EPS, None, ALU.add).then_inc(front_var.sem, 1)

            def l0_latent(ph, b):
                dve.wait_ge(front_rstd.sem, front_rstd(ph, b, 3))
                latent = front_n[:, :, 0:64]
                for t in range(T):
                    front_step_of(V_.tensor_scalar(latent[:, t, :], latent_of()[:, t, :], moments[:, t, 0:1], rstd[:, t:t + 1], ALU.subtract, ALU.mult))
                front_settle(ph, b)
                front_step_of(V_.tensor_tensor(latent, latent, both(W(ph, "lng")), ALU.mult))
                front_settle(ph, b)
                V_.tensor_tensor(latent, latent, both(W(ph, "lnb")), ALU.add).then_inc(front_ready.sem, 1)

            def l0_keys_values(ph, b):
                dve.wait_ge(proj_psum.sem, proj_psum(ph, b, 3))
                dve.wait_ge(qkv_ready.sem, qkv_ready(ph, b, 1))
                rope(compact[:, 1, :], pb[0], "cosk", "sink", ph, b).then_inc(qkv_ready.sem, 1)
                dve.wait_ge(qkv_ready.sem, qkv_ready(ph, b, 2))
                split(ph, b)
                dve.wait_ge(proj_psum.sem, proj_psum(ph, b, 4))
                V_.tensor_copy(V[:, :, 0:D], tiles(pb[5][:, S:S + T * D])).then_inc(qkv_ready.sem, 1)

            def l0_front(b, ph="l0_ffn"):
                front_row(ph, b, True)
                front_step_of(front_adaln(ph, b))
                l0_square(ph, b)
                l0_rms(ph, b)
                l0_queries(ph, b)
                l0_latent_stats(ph, b)
                l0_latent(ph, b)
                l0_keys_values(ph, b)

            def l0_ffn(b, following, ph="l0_ffn"):
                start_main(ph, b)
                step(V_.tensor_copy(hb[:], xb[:]))
                settle(ph, b)
                narrow_softmax(ph, b, CAUSAL, following)
                if following is not None:
                    l0_keys_values(ph, following)
                dve.wait_ge(out_psum.sem, out_psum(ph, b, 1))
                step(V_.tensor_tensor(hb[:], hb[:], tiles(pb[1][:, S:S + T * D]), ALU.add))
                settle(ph, b)
                for t in range(T):
                    step(V_.bn_stats(main_stats[:, t, :], hb[:, t, :]))
                settle_apart(ph, b)
                for t in range(T):
                    step(V_.bn_aggr(main_moments[:, t, :], main_stats[:, t, :]))
                settle(ph, b)
                step(V_.tensor_tensor(main_square[:], main_moments[:, :, 0], main_moments[:, :, 0], ALU.mult))
                settle(ph, b)
                step(V_.tensor_tensor(main_square[:], main_square[:], main_moments[:, :, 1], ALU.add))
                settle(ph, b)
                V_.tensor_scalar(main_var[:], main_square[:], RMS_EPS, None, ALU.add).then_inc(var_ready.sem, 1)
                dve.wait_ge(rstd_ready.sem, rstd_ready(ph, b, 1))
                for t in range(T):
                    step(V_.tensor_scalar(nb[:, t, :], hb[:, t, :], main_rstd[:, t:t + 1], None, ALU.mult))
                settle(ph, b)
                V_.tensor_tensor(nb[:], nb[:], both(W(ph, "n2")), ALU.mult).then_inc(tok_ready.sem, 1)
                logit, order, top, pick = (small[i][:, 0:T * E0].rearrange("p (t e) -> p t e", t=T) for i in range(4))
                top1 = small[4][:, 0:T]
                every_e = top1.unsqueeze(2).to_broadcast([P, T, E0])
                dve.wait_ge(gate_psum.sem, gate_psum(ph, b, 1))
                step(V_.tensor_tensor(logit, pb[1][:, 0:T * E0].rearrange("p (t e) -> p t e", t=T), both(W(ph, "gateb")), ALU.add))
                settle(ph, b)
                step(V_.tensor_reduce(top1, logit, AX.X, ALU.max))
                settle(ph, b)
                step(V_.tensor_tensor(order, logit, every_e, ALU.is_equal))
                settle(ph, b)
                step(V_.tensor_tensor(order, order, both(C("first")), ALU.mult))
                settle(ph, b)
                step(V_.tensor_reduce(top1, order, AX.X, ALU.max))
                settle(ph, b)
                step(V_.tensor_tensor(pick, order, every_e, ALU.is_equal))
                step(V_.tensor_copy(sum_b[:], hb[:]))
                for e in range(E0):
                    dve.wait_ge(expert_psum.sem, expert_psum(ph, b, e + 1))
                    settle(ph, b)
                    for t in range(T):
                        ins = V_.scalar_tensor_tensor(sum_b[:, t, :], pb[6 + e % 2][:, t * D:(t + 1) * D], pick[:, t, e:e + 1],
                                                      sum_b[:, t, :], ALU.mult, ALU.add)
                        if t < T - 1:
                            step(ins)
                    ins.then_inc(expert_used.sem, 1)
                    dve.wait_ge(expert_used.sem, expert_used(ph, b, e + 1))
                end_main(ph, b)

            def l1_keep_counts(ph="l1_attn"):
                z, e, q, f, kf = (small[i][:, 0:H] for i in range(5))
                n = [0]

                def then(ins):
                    n[0] += 1
                    ins.then_inc(keep_count, 1)
                    dve.wait_ge(keep_count, n[0])

                then(V_.memset(V[:, :, 0:H * (HD + 1)], 1.0))
                then(V_.memset(restart, 1.0))
                then(V_.memset(restart[:, :, 0:1], 0.0))
                V_.tensor_tensor(z, W(ph, "ema"), W(ph, "thr"), ALU.subtract).then_inc(keep_exp, 1)
                dve.wait_ge(keep_exped, 1)
                then(V_.tensor_scalar(e, e, 1.0, None, ALU.add))
                then(V_.reciprocal(q, e))
                then(V_.tensor_scalar(q, q, 0.9, 0.1, ALU.mult, ALU.add))
                then(V_.tensor_scalar(q, q, -1.0, 1.0, ALU.mult, ALU.add))
                then(V_.tensor_scalar(q, q, float(S), None, ALU.mult))
                then(V_.tensor_copy(keep_i[:], q))
                then(V_.tensor_copy(f, keep_i[:]))
                then(V_.tensor_tensor(kf, f, q, ALU.is_gt))
                then(V_.tensor_tensor(f, f, kf, ALU.subtract))
                then(V_.tensor_scalar(f, f, 1.0, None, ALU.max))
                then(V_.tensor_copy(keep[:].rearrange("p (h t) -> p h t", t=T), f.unsqueeze(2).to_broadcast([P, H, T])))
                then(V_.tensor_scalar(aim[:], keep[:], -(LEFT + 1) / 2, None, ALU.add))

            def quick_search(ph, b):
                raised = [0]

                def then(ins, b, it):
                    raised[0] += 1
                    ins.then_inc(quick_step.sem, 1)
                    dve.wait_ge(quick_step.sem, quick_step(ph, b, raised[0]) + it * QUICK_RAISES)

                mean = rowsum[:].rearrange("p h t -> p (h t)")
                step(V_.tensor_scalar(under[:, 0, :], mean, (1 + QUICK_LO) / S, -QUICK_LO, ALU.mult, ALU.add))
                step(V_.tensor_scalar(over[:, 0, :], mean, (1 - QUICK_HI) / S, QUICK_HI, ALU.mult, ALU.add))
                step(V_.memset(under[:, 1, :], float(S)))
                step(V_.memset(over[:, 1, :], UNSEEN))
                settle_apart(ph, b)
                for it in range(QUICK_STEPS):
                    raised[0] = 0
                    V_.tensor_tensor(span, over[:, 0, :], under[:, 0, :], ALU.subtract)
                    V_.tensor_tensor(enough, under[:, 1, :], aim[:], ALU.subtract)
                    then(V_.tensor_tensor(part, under[:, 1, :], over[:, 1, :], ALU.subtract), b, it)
                    then(V_.reciprocal(short, part), b, it)
                    then(V_.tensor_tensor(part, enough, short, ALU.mult), b, it)
                    then(V_.scalar_tensor_tensor(part, part, 0.99, span, ALU.min, ALU.mult), b, it)
                    then(V_.tensor_tensor(tried[:, 0, :], under[:, 0, :], part, ALU.add), b, it)
                    V_.tensor_scalar(neg_mid[:], tried[:, 0, :], -1.0, None, ALU.mult).then_inc(mid_ready.sem, 1)
                    for j in range(ROWS_DVE):
                        last = V_.tensor_scalar(flags[j], big[:, j, :], tried[:, 0, j:j + 1], 0.0, ALU.is_gt, ALU.add,
                                                accum_out=tried[:, 1, j:j + 1])
                    dve.wait_ge(counts_act.sem, counts_act(ph, b, 1) + it)
                    then(V_.tensor_scalar(tried[:, 1, ROWS_DVE:], tried[:, 1, ROWS_DVE:], 0.5, S / 2, ALU.mult, ALU.add), b, it)
                    V_.tensor_tensor(enough, tried[:, 1, :], keep[:], ALU.is_ge)
                    then(V_.tensor_tensor(short, tried[:, 1, :], keep[:], ALU.is_lt), b, it)
                    V_.memset(gap[:], 0.0)
                    two = [P, 2, ROWS1]
                    V_.copy_predicated(under, enough.bitcast(I32).unsqueeze(1).to_broadcast(two), tried)
                    then(V_.copy_predicated(over, short.bitcast(I32).unsqueeze(1).to_broadcast(two), tried), b, it)
                assert raised[0] == QUICK_RAISES, f"QUICK {raised[0]}"
                for j in range(ROWS_DVE, ROWS1):
                    step(V_.tensor_scalar(signs[j - ROWS_DVE], big[:, j, :], over[:, 0, j:j + 1], 0.0, ALU.is_gt, ALU.add,
                                          accum_out=over[:, 1, j:j + 1]))
                settle(ph, b)
                step(V_.tensor_tensor(left, keep[:], over[:, 1, :], ALU.subtract))
                settle(ph, b)
                step(V_.tensor_scalar(doubt, left, -(LEFT + 1) / 2, None, ALU.add))
                settle(ph, b)
                step(V_.tensor_tensor(doubt, doubt, doubt, ALU.mult))
                settle(ph, b)
                V_.tensor_scalar(part, doubt, (LEFT / 2) ** 2, 0.0, ALU.is_gt, ALU.add, accum_out=doubts).then_inc(doubts_ready.sem, 1)
                dve.wait_ge(doubts_ready.sem, doubts_ready(ph, b, 1))

            def choose(ph, b, following):
                def next_max(u, first, end):
                    if following is not None and u >= 1:
                        for h in range(4 * (u - 1) + first, 4 * (u - 1) + end):
                            row_max(ph, following, h, FULL)

                for u in range(4):
                    js = range(8 * u, 8 * u + 8)
                    for j in js:
                        step(V_.scalar_tensor_tensor(candidates[:, j % 8, :], big[:, j, :], over[:, 0, j:j + 1], big[:, j, :],
                                                     ALU.is_le, ALU.mult))
                    next_max(u, 0, 2)
                    step(V_.tensor_tensor(past, C("order8").unsqueeze(1).to_broadcast([P, 8, LEFT]),
                                          left[:, 8 * u:8 * u + 8].unsqueeze(2).to_broadcast([P, 8, LEFT]), ALU.is_ge))
                    settle_apart(ph, b)
                    for j in js:
                        step(V_.max(largest[:, j % 8, :], candidates[:, j % 8, :]))
                    next_max(u, 2, 3)
                    settle(ph, b)
                    step(V_.scalar_tensor_tensor(largest, past, 2.0, largest, ALU.mult, ALU.max))
                    settle_apart(ph, b)
                    for j in js:
                        step(V_.match_replace(marked[:, j % 8, :], largest[:, j % 8, :], candidates[:, j % 8, :], -1.0))
                    next_max(u, 3, 4)
                    settle(ph, b)
                    for j in js:
                        last = V_.scalar_tensor_tensor(big[:, j, :], marked[:, j % 8, :], 0.0, big[:, j, :], ALU.is_le, ALU.mult)
                        if j % T == T - 1:
                            last.then_inc(kept_ready.sem, 1)
                    dve.wait_ge(kept_ready.sem, kept_ready(ph, b, 4 * u + 4))
                next_max(4, 0, 4)

            def bisect(ph, b, following):
                step(V_.memset(low[:], SEARCH_LO))
                step(V_.memset(width[:], SEARCH_SPAN / 2))
                step(V_.memset(mid[:], SEARCH_LO + SEARCH_SPAN / 2))
                settle_apart(ph, b)
                raised = [0]

                def then(ins, b, it):
                    raised[0] += 1
                    ins.then_inc(bisect_step.sem, 1)
                    dve.wait_ge(bisect_step.sem, bisect_step(ph, b, raised[0]) + it * BISECT_RAISES)

                with dve.Fori(0, SEARCH_STEPS) as it:
                    for j in range(ROWS1):
                        last = V_.tensor_scalar(bisect_flags[j], big[:, j, :], mid[:, j:j + 1], 0.0, ALU.is_gt, ALU.add,
                                                accum_out=counts[:, j:j + 1])
                    then(last, b, it)
                    then(V_.tensor_tensor(above[:], counts[:], keep[:], ALU.is_ge), b, it)
                    then(V_.scalar_tensor_tensor(low[:], above[:], width[:, 0:1], low[:], ALU.mult, ALU.add), b, it)
                    then(V_.tensor_scalar(width[:], width[:], 0.5, None, ALU.mult), b, it)
                    then(V_.tensor_scalar(mid[:], low[:], width[:, 0:1], None, ALU.add), b, it)
                assert raised[0] == BISECT_RAISES, f"BISECT {raised[0]}"
                step(V_.tensor_scalar(mid[:], low[:], 2 * LAST_STEP, None, ALU.add))
                settle(ph, b)
                step(V_.tensor_scalar(low[:], low[:], -LAST_STEP, None, ALU.add))
                settle(ph, b)
                for u in range(4):
                    js = range(8 * u, 8 * u + 8)
                    for j in js:
                        step(V_.tensor_scalar(masks[:, j % 8, :], big[:, j, :], mid[:, j:j + 1], 0.0, ALU.is_gt, ALU.add,
                                              accum_out=counts[:, j:j + 1]))
                        step(V_.tensor_scalar(within[:, j % 8, :], big[:, j, :], low[:, j:j + 1], None, ALU.is_gt))
                    settle(ph, b)
                    step(V_.tensor_tensor(within, within, masks[:, 0:8, :], ALU.subtract))
                    step(V_.tensor_tensor(counts[:, 8 * u:8 * u + 8], keep[:, 8 * u:8 * u + 8], counts[:, 8 * u:8 * u + 8], ALU.subtract))
                    settle(ph, b)
                    step(V_.tensor_tensor_scan(place.rearrange("p j k -> p (j k)"), restart.rearrange("p j k -> p (j k)"),
                                               within.rearrange("p j k -> p (j k)"), 0.0, ALU.mult, ALU.add))
                    settle(ph, b)
                    for j in js:
                        step(V_.scalar_tensor_tensor(place[:, j % 8, :], place[:, j % 8, :], counts[:, j:j + 1], within[:, j % 8, :],
                                                     ALU.is_le, ALU.mult))
                    settle(ph, b)
                    step(V_.tensor_tensor(masks[:, 0:8, :], masks[:, 0:8, :], place, ALU.add))
                    settle(ph, b)
                    V_.tensor_tensor(big[:, 8 * u:8 * u + 8, :], big[:, 8 * u:8 * u + 8, :], masks[:, 0:8, :], ALU.mult).then_inc(kept_ready.sem, 4)
                    dve.wait_ge(kept_ready.sem, kept_ready(ph, b, 4 * u + 4))
                    if following is not None:
                        for h in range(4 * u, 4 * u + 4):
                            row_max(ph, following, h, FULL)

            def l1_attn_front(b, ph="l1_attn"):
                front_row(ph, b, True)
                front_adaln(ph, b).then_inc(front_ready.sem, 1)
                intake_qk(ph, b)
                split(ph, b)
                intake_values_and_ones(ph, b)
                for h in range(H):
                    row_max(ph, b, h, FULL)

            def l1_attn(b, following, ph="l1_attn"):
                start_main(ph, b)
                if following is not None:
                    front_row(ph, following, False)
                dve.wait_ge(probs_ready.sem, probs_ready(ph, b, H))
                step(V_.tensor_scalar(rinv[:], rowsum[:], 1e-10, None, ALU.mult))
                if following is not None:
                    front_adaln(ph, following).then_inc(front_ready.sem, 1)
                quick_search(ph, b)
                if following is not None:
                    intake_qk(ph, following)
                    split(ph, following)
                dve.wait_ge(doubts_psum.sem, doubts_psum(ph, b, 1))
                step(V_.tensor_copy(doubts_i[:], pb[1][0:1, 0:1]))
                settle_apart(ph, b)
                found = dve.value_load(doubts_i[:], min_val=0, max_val=P * ROWS1)
                start = count[0]
                with dve.If(found > 0):
                    bisect(ph, b, following)
                    dve.sem_inc(dve_step.sem, start + SELECT_STEPS - count[0])
                slow = count[0]
                count[0] = start
                with dve.Else():
                    choose(ph, b, following)
                    dve.sem_inc(dve_step.sem, start + SELECT_STEPS - count[0])
                    dve.sem_inc(bisect_step.sem, SEARCH_STEPS * BISECT_RAISES)
                assert max(slow, count[0]) < start + SELECT_STEPS, f"SELECT {slow - start} {count[0] - start}"
                count[0] = start + SELECT_STEPS
                dve.wait_ge(pv_done.sem, pv_done(ph, b, H))
                settle(ph, b)
                for t in range(T):
                    o1 = pb[1][:, t * 256:t * 256 + H * (HD + 1)].rearrange("p (h d) -> p h d", h=H)
                    step(V_.tensor_tensor(rinv[:, :, t], rinv[:, :, t], o1[:, :, HD], ALU.add))
                settle(ph, b)
                step(V_.reciprocal(rkept[:], rinv[:]))
                settle(ph, b)
                for t in range(T):
                    o1 = pb[1][:, t * 256:t * 256 + H * (HD + 1)].rearrange("p (h d) -> p h d", h=H)
                    last = V_.tensor_tensor(O[:, t, 0:D].rearrange("p (h d) -> p h d", h=H), o1[:, :, 0:HD],
                                            rkept[:, :, t].unsqueeze(2).to_broadcast([P, H, HD]), ALU.mult)
                last.then_inc(tok_ready.sem, 1)
                if following is not None:
                    intake_values_and_ones(ph, following)
                dve.wait_ge(out_psum.sem, out_psum(ph, b, 1))
                step(V_.tensor_tensor(sum_b[:], tiles(pb[1][:, S:S + T * D]), both(W(ph, "bo")), ALU.add))
                end_main(ph, b)

            def l1_front(ph="l1_ffn"):
                wide_front(ph)
                score, prob, most, tied, rank, restart_e = (
                    rows(8 + 2 * i, 2).rearrange("p (j e) -> p j e", e=E1) for i in range(6))
                weight = weights_all
                take_pair_first(ph)
                dve.wait_ge(wide_logits.sem, wide_logits(ph, 0, 1))
                wide_step_of(V_.tensor_tensor(score, pb[1][:].rearrange("p (j e) -> p j e", e=E1), each(W(ph, "routerb")), ALU.add))
                wide_settle()
                wide_step_of(V_.tensor_reduce(one, score, AX.X, ALU.max))
                wide_settle()
                V_.tensor_tensor(score, score, spread(one, E1), ALU.subtract).then_inc(max_route, 1)
                wide_step_of(V_.memset(restart_e, 1.0))
                wide_settle()
                wide_step_of(V_.memset(restart_e[:, :, 0:1], 0.0))
                dve.wait_ge(exp_route, 1)
                wide_step_of(V_.tensor_reduce(one, prob, AX.X, ALU.add))
                wide_settle()
                wide_step_of(V_.reciprocal(total, one))
                wide_settle()
                wide_step_of(V_.tensor_tensor(score, prob, spread(total, E1), ALU.mult))
                wide_settle()
                wide_step_of(V_.memset(gap[:], 0.0))
                for j in range(N16):
                    wide_step_of(V_.max(top8[:, j, :], score[:, j, :]))
                wide_settle()
                fourth = top8[:, :, TOP1 - 1:TOP1].to_broadcast([P, N16, E1])
                wide_step_of(V_.tensor_tensor(most, score, fourth, ALU.is_gt))
                wide_step_of(V_.tensor_tensor(tied, score, fourth, ALU.is_equal))
                wide_settle()
                wide_step_of(V_.tensor_reduce(one, most, AX.X, ALU.add))
                wide_step_of(V_.tensor_tensor_scan(rows(16, 2), rows(18, 2), rows(14, 2), 0.0, ALU.mult, ALU.add))
                wide_settle()
                wide_step_of(V_.tensor_scalar(one, one, -1.0, float(TOP1), ALU.mult, ALU.add))
                wide_settle()
                wide_step_of(V_.tensor_tensor(rank, rank, spread(one, E1), ALU.is_le))
                wide_settle()
                wide_step_of(V_.tensor_tensor(tied, tied, rank, ALU.mult))
                wide_settle()
                wide_step_of(V_.tensor_tensor(most, most, tied, ALU.add))
                wide_settle()
                wide_step_of(V_.tensor_tensor(score, score, most, ALU.mult))
                wide_settle()
                wide_step_of(V_.tensor_reduce(one, score, AX.X, ALU.add))
                wide_settle()
                wide_step_of(V_.tensor_scalar(one, one, 1e-12, None, ALU.max))
                wide_settle()
                wide_step_of(V_.reciprocal(total, one))
                wide_settle()
                wide_step_of(V_.tensor_tensor(weight, score, spread(total, E1), ALU.mult))
                wide_gates(ph)
                wide_settle()

            def take_pair_first(ph):
                dve.wait_ge(wide_feat.sem, wide_feat(ph, 0, 1))
                V_.tensor_copy(pair_feat.rearrange("p (r k) -> p r k", r=2), feats[:, 0:2, :]).then_inc(pair_ready.sem, 1)

            def l1_ffn(p, following, ph="l1_ffn"):
                count[0] = 0
                dve.wait_ge(pass_done.sem, pass_done(ph, p, 1))
                step(V_.memset(gap[:], 0.0))
                step(V_.tensor_copy(pair_weight, weights_all[:, bass.ds(p * 2 * T, 2 * T), :]))
                settle(ph, p)

                def rise(e):
                    dve.wait_ge(silu_g.sem, silu_g(ph, p, e + 1))
                    dve.wait_ge(expert_psum.sem, expert_psum(ph, p, e - 1))
                    V_.tensor_tensor(risen(e), silus(e), pb[(2, 4, 0)[e % 3] + 1][:], ALU.mult).then_inc(hid_ready.sem, 1)

                def fall(e):
                    dve.wait_ge(expert_psum.sem, expert_psum(ph, p, e + 1))
                    if e:
                        dve.wait_ge(expert_used.sem, expert_used(ph, p, e))
                    down = pb[6 + e % 2][:].rearrange("p (j d) -> p j d", d=D)
                    if e < E1:
                        for j in range(2 * T):
                            w = pair_weight[:, j, e:e + 1]
                            if e == 0:
                                last = V_.tensor_scalar(pair_sum[:, j, :], down[:, j, :], w, None, ALU.mult)
                            else:
                                last = V_.scalar_tensor_tensor(pair_sum[:, j, :], down[:, j, :], w, pair_sum[:, j, :], ALU.mult, ALU.add)
                    else:
                        last = V_.tensor_tensor(pair_sum, pair_sum, down, ALU.add)
                    last.then_inc(expert_used.sem, 1)

                for e in range(EA + 2):
                    if e < EA:
                        rise(e)
                    if e == EA:
                        dve.wait_ge(hid_psum.sem, hid_psum(ph, p, EA))
                        step(V_.memset(gap[:], 0.0))
                        if following is not None:
                            take_pair(ph, following)
                    if e >= 2:
                        fall(e - 2)
                dve.wait_ge(expert_used.sem, expert_used(ph, p, EA))
                end_pair(ph, p)

            def end_pair(ph, p):
                settle(ph, p)
                step(V_.tensor_tensor(by_row(pair_sum), by_row(pair_sum), pair_gates(p), ALU.mult))
                settle(ph, p)
                V_.tensor_tensor(pair_rows(p), pair_rows(p), pair_sum, ALU.add).then_inc(pass_done.sem, 1)
                assert count[0] == DVE_STEPS[ph], f"NSTEPS main {ph} {count[0]}"

            def l2_front(ph="l2_ffn"):
                wide_front(ph)
                view = lambda i: rows(i, 1).rearrange("p (j e) -> p j e", e=E2)
                z, zs, rest, mean, meansq, root, tau, restart_2 = map(view, range(9, 17))
                logits = pb[1][:, 0:N16 * E2].rearrange("p (j e) -> p j e", e=E2)
                wide_gates(ph)
                dve.wait_ge(wide_logits.sem, wide_logits(ph, 0, 1))
                wide_step_of(V_.tensor_reduce(one, logits, AX.X, ALU.add))
                wide_step_of(V_.memset(restart_2, 1.0))
                wide_settle()
                wide_step_of(V_.memset(restart_2[:, :, 0:1], 0.0))
                wide_step_of(V_.tensor_scalar(one, one, 1.0 / E2, None, ALU.mult))
                wide_settle()
                wide_step_of(V_.tensor_tensor(z, logits, spread(one, E2), ALU.subtract))
                wide_settle()
                wide_step_of(V_.tensor_tensor(rest, z, z, ALU.mult))
                wide_settle()
                wide_step_of(V_.tensor_reduce(one, rest, AX.X, ALU.add))
                wide_settle()
                V_.tensor_scalar(wide_var, one, 1.0 / E2, LN_EPS, ALU.mult, ALU.add).then_inc(wide_var_ready.sem, 1)
                dve.wait_ge(wide_rstd_ready.sem, wide_rstd_ready(ph, 0, 2))
                wide_step_of(V_.scalar_tensor_tensor(z, z, 0.5, spread(wide_rstd, E2), ALU.mult, ALU.mult))
                wide_settle()
                wide_step_of(V_.tensor_reduce(one, z, AX.X, ALU.max))
                wide_settle()
                wide_step_of(V_.tensor_tensor(z, z, spread(one, E2), ALU.subtract))
                wide_settle()
                wide_step_of(V_.memset(gap[:], 0.0))
                for j in range(N16):
                    wide_step_of(V_.max(zs[:, j, 0:8], z[:, j, :]))
                wide_settle()
                wide_step_of(V_.memset(gap[:], 0.0))
                for j in range(N16):
                    wide_step_of(V_.match_replace(rest[:, j, :], zs[:, j, 0:8], z[:, j, :], MASKED))
                wide_settle()
                wide_step_of(V_.memset(gap[:], 0.0))
                for j in range(N16):
                    wide_step_of(V_.max(zs[:, j, 8:16], rest[:, j, :]))
                wide_settle()
                flat = lambda i: rows(i, 1)
                wide_step_of(V_.tensor_tensor_scan(flat(12), flat(16), flat(10), 0.0, ALU.mult, ALU.add))
                wide_step_of(V_.tensor_tensor(rest, zs, zs, ALU.mult))
                wide_settle()
                wide_step_of(V_.tensor_tensor_scan(flat(13), flat(16), flat(11), 0.0, ALU.mult, ALU.add))
                wide_step_of(V_.tensor_tensor(mean, mean, each(C("kinv")), ALU.mult))
                wide_settle()
                wide_step_of(V_.tensor_tensor(meansq, meansq, each(C("kinv")), ALU.mult))
                wide_step_of(V_.tensor_tensor(rest, mean, mean, ALU.mult))
                wide_settle()
                wide_step_of(V_.tensor_tensor(meansq, meansq, rest, ALU.subtract))
                wide_settle()
                wide_step_of(V_.tensor_tensor(meansq, meansq, each(C("karange")), ALU.mult))
                wide_settle()
                wide_step_of(V_.tensor_scalar(meansq, meansq, -1.0, 1.0, ALU.mult, ALU.add))
                wide_settle()
                wide_step_of(V_.tensor_tensor(meansq, meansq, each(C("kinv")), ALU.mult))
                wide_settle()
                V_.tensor_scalar(meansq, meansq, 0.0, None, ALU.max).then_inc(delta_ready, 1)
                dve.wait_ge(root_ready, 1)
                wide_step_of(V_.tensor_tensor(tau, mean, root, ALU.subtract))
                wide_settle()
                wide_step_of(V_.tensor_tensor(rest, tau, zs, ALU.is_le))
                wide_settle()
                wide_step_of(V_.tensor_reduce(one, rest, AX.X, ALU.add))
                wide_settle()
                wide_step_of(V_.tensor_tensor(rest, each(C("karange")), spread(one, E2), ALU.is_equal))
                wide_settle()
                wide_step_of(V_.tensor_tensor(rest, rest, tau, ALU.mult))
                wide_settle()
                wide_step_of(V_.tensor_reduce(one, rest, AX.X, ALU.add))
                wide_settle()
                wide_step_of(V_.tensor_tensor(z, z, spread(one, E2), ALU.subtract))
                wide_settle()
                wide_step_of(V_.tensor_scalar(z, z, 0.0, None, ALU.max))
                wide_settle()
                V_.tensor_tensor(mix, z, z, ALU.mult).then_inc(mix_ready, 1)
                for u in range(PAIRS):
                    dve.wait_ge(ranks_ready, u + 1)
                    two = slice(2 * u, 2 * u + 2)
                    wide_step_of(V_.scalar_tensor_tensor(ranks_z[:, two, :], pb[RANK_BANKS[u]][0:R2, :].rearrange("p (r k) -> p r k", r=2),
                                                         W(ph, "win1b", R2), ranks_gate[0:R2, two, :], ALU.add, ALU.mult))
                wide_settle()
                V_.tensor_copy(pair_feat[0:R2, :].rearrange("p (r k) -> p r k", r=2), ranks_z[:, 0:2, :]).then_inc(pair_ready.sem, 1)

            def l2_ffn(p, following, ph="l2_ffn"):
                count[0] = 0
                dve.wait_ge(pass_done.sem, pass_done(ph, p, 1))
                dve.wait_ge(hid_psum.sem, hid_psum(ph, p, O2))
                step(V_.memset(gap[:], 0.0))
                if following is not None:
                    V_.tensor_copy(pair_feat[0:R2, :].rearrange("p (r k) -> p r k", r=2),
                                   ranks_z[:, bass.ds(following * 2, 2), :]).then_inc(pair_ready.sem, 1)
                dve.wait_ge(z_psum.sem, z_psum(ph, p, 1))
                two = lambda v: v.rearrange("p (r k) -> p r k", r=2)
                V_.scalar_tensor_tensor(two(pair_rank2), two(pb[6][R2:2 * R2, :]), W(ph, "win2b")[R2:2 * R2, :],
                                        ranks_gate[R2:2 * R2, bass.ds(p * 2, 2), :], ALU.add, ALU.mult).then_inc(z_ready.sem, 1)
                dve.wait_ge(out_psum.sem, out_psum(ph, p, 1))
                step(V_.tensor_copy(pair_sum, pb[7][:].rearrange("p (j d) -> p j d", d=D)))
                end_pair(ph, p)

            def l3_square(ph, b):
                front_settle(ph, b)
                for t in range(T):
                    front_step_of(V_.bn_stats(stats[:, t, :], xb[:, t, :]))
                front_settle_apart(ph, b)
                for t in range(T):
                    front_step_of(V_.bn_aggr(moments[:, t, :], stats[:, t, :]))
                front_settle(ph, b)
                V_.tensor_scalar(var[:], moments[:, :, 1], LN_EPS, None, ALU.add).then_inc(front_var.sem, 1)

            def l3_norm(ph, b):
                dve.wait_ge(front_rstd.sem, front_rstd(ph, b, 2))
                for t in range(T):
                    front_step_of(V_.tensor_scalar(front_n[:, t, :], xb[:, t, :], moments[:, t, 0:1], rstd[:, t:t + 1], ALU.subtract, ALU.mult))
                front_settle(ph, b)
                front_step_of(V_.tensor_tensor(front_n[:], front_n[:], both(W(ph, "gamma")), ALU.mult))
                front_settle(ph, b)
                V_.tensor_tensor(front_n[:], front_n[:], both(W(ph, "beta")), ALU.add).then_inc(front_ready.sem, 1)

            def l3_queries_keys(ph, b):
                for g in range(NG3):
                    dve.wait_ge(proj_psum.sem, proj_psum(ph, b, g + 1))
                    two = 2 + 2 * (g % 2)
                    if g:
                        dve.wait_ge(qkv_ready.sem, qkv_ready(ph, b, g))
                    front_step_of(rope(qT[:, g, :], pb[two], "cosq", "sinq", ph, b))
                    front_settle(ph, b)
                    rope_parts(pb[two + 1], "cosk", "sink", ph, b)
                    for i in range(2):
                        half = slice(HD3 * i, HD3 * (i + 1))
                        last = V_.tensor_tensor(keys[half, 2 * g + i, :], rope_c[half, :], rope_s[half, :], ALU.add)
                    last.then_inc(qkv_ready.sem, 1)
                front_end(ph, b)

            def l3_front(b, ph="l3_attn"):
                front_row(ph, b, True)
                front_step_of(front_adaln(ph, b))
                l3_square(ph, b)
                l3_norm(ph, b)
                dve.wait_ge(keys_clear, 1)
                l3_queries_keys(ph, b)

            def l3_attn(b, following, ph="l3_attn"):
                start_main(ph, b)
                for s in range(H + 3):
                    if following is not None and s == 2:
                        front_row(ph, following, False)
                    if following is not None and s == 5:
                        front_step_of(front_adaln(ph, following))
                        l3_square(ph, following)
                    if following is not None and s == 7:
                        l3_norm(ph, following)
                    if s < H:
                        row_max(ph, b, s, FULL)
                    if 2 <= s < H + 2:
                        take_probsT(ph, b, s - 2, FULL)
                    if s >= 3 and (s - 3) % 4 == 3:
                        u = (s - 3) // 4
                        hs = slice(4 * u, 4 * u + 4)
                        dve.wait_ge(pv_done.sem, pv_done(ph, b, 4 * u + 4))
                        step(V_.reciprocal(rinv[:, hs, :], rowsum[:, hs, :]))
                        settle(ph, b)
                        for t in range(T):
                            last = V_.tensor_tensor(O[:, t, 4 * u * HD3:(4 * u + 4) * HD3].rearrange("p (h d) -> p h d", h=4),
                                                    pb[u % 2][:, t * 256:(t + 1) * 256].rearrange("p (h d) -> p h d", h=4),
                                                    rinv[:, hs, t].unsqueeze(2).to_broadcast([P, 4, HD3]), ALU.mult)
                        last.then_inc(o_ready.sem, 1)
                if following is not None:
                    l3_queries_keys(ph, following)
                dve.wait_ge(out_psum.sem, out_psum(ph, b, 1))
                step(V_.tensor_copy(sum_b[:], tiles(pb[0][:, 0:T * D])))
                end_main(ph, b)

            def l3_ffn(ph="l3_ffn"):
                wide_front(ph)
                dve.wait_ge(wide_logits.sem, wide_logits(ph, 0, 1))
                V_.tensor_scalar(routes[:].rearrange("p t b e -> p b t e"), pb[1][:, 0:N16 * E3].rearrange("p (b t e) -> p b t e", b=B, t=T),
                                 CLIP3, None, ALU.max).then_inc(routes_ready, 1)
                wide_gates(ph)
                wide_settle()
                V_.memset(gap[:], 0.0).then_inc(pass_done.sem, 1)

            def l3_route():
                n = [0]

                def then(ins):
                    n[0] += 1
                    ins.then_inc(sink_step, 1)
                    dve.wait_ge(sink_step, n[0])

                over_t = lambda v: v.unsqueeze(1).to_broadcast([P, T, B * E3])
                cols = routes[:].rearrange("p t b e -> p t (b e)")
                rows = routes[:].rearrange("p t b e -> p (t b) e")
                cs = colsum[:].rearrange("p b e -> p (b e)")
                over_e = lambda v: v.unsqueeze(2).to_broadcast([P, T * B, E3])
                dve.wait_ge(routes_ready, 1)
                dve.wait_ge(sink_max, 1)
                then(V_.tensor_tensor(cs, colmax[:, 0:B * E3], colmax[:, B * E3:], ALU.max))
                then(V_.reciprocal(colmax[:, 0:B * E3], cs))
                V_.tensor_tensor(cols, cols, over_t(colmax[:, 0:B * E3]), ALU.mult).then_inc(sink_next, 1)
                for r in range(ROUNDS3):
                    dve.wait_ge(sink_sum, r + 1)
                    then(V_.reciprocal(cs, pb[0][:, 0:B * E3]))
                    then(V_.tensor_tensor(cols, cols, over_t(cs), ALU.mult))
                    then(V_.tensor_reduce(rowsum3[:], rows, AX.X, ALU.add))
                    then(V_.reciprocal(best[:], rowsum3[:]))
                    V_.tensor_tensor(rows, rows, over_e(best[:]), ALU.mult).then_inc(sink_next, 1)
                R = B * E3
                gate, work, key, strict, seen, same, run, one = (qT[0:R, i, :] for i in range(8))
                top = small[9][0:R, 0:M3]
                dve.wait_ge(sink_sum, ROUNDS3 + 1)
                then(V_.tensor_copy(gate, pb[1][0:R, 0:S]))
                then(V_.memset(one, 1.0))
                then(V_.memset(strict, 0.0))
                then(V_.memset(seen, 0.0))
                src, other = gate, [work, key]
                for i in range(M3 // 8):
                    then(V_.max(top[:, 8 * i:8 * i + 8], src))
                    then(V_.match_replace(other[i % 2], top[:, 8 * i:8 * i + 8], src, -1.0))
                    src = other[i % 2]
                for m in range(M3):
                    v = top[:, m:m + 1]
                    then(V_.scalar_tensor_tensor(strict, gate, v, strict, ALU.is_lt, ALU.add))
                    then(V_.tensor_scalar(same, gate, v, None, ALU.is_equal))
                    then(V_.tensor_tensor_scan(run, one, same, 0.0, ALU.mult, ALU.add))
                    then(V_.copy_predicated(seen, same.bitcast(I32), run))
                then(V_.tensor_tensor(strict, strict, seen, ALU.add))
                then(V_.tensor_scalar(same, src, 0.0, None, ALU.is_lt))
                then(V_.tensor_scalar(strict, strict, float(E3), -float(E3), ALU.mult, ALU.add))
                V_.scalar_tensor_tensor(key, strict, C("expert1", R), same, ALU.add, ALU.mult).then_inc(sink_next, 1)
                dve.wait_ge(sink_sum, ROUNDS3 + 2)
                keys = masks3[:].rearrange("p t b e -> p (t b) e")
                won = colmax[:].rearrange("p (r e) -> p r e", e=E3)
                then(V_.tensor_copy(masks3[:].rearrange("p t b e -> p (t b e)"), pb[0][:, 0:T * R]))
                then(V_.tensor_reduce(best[:], keys, AX.X, ALU.max))
                then(V_.tensor_tensor(won, keys, over_e(best[:]), ALU.is_equal))
                then(V_.tensor_scalar(keys, keys, 0.0, None, ALU.is_gt))
                then(V_.tensor_tensor(won, won, keys, ALU.mult))
                then(V_.tensor_scalar(rows, rows, 0.5, None, ALU.is_gt))
                then(V_.tensor_tensor(keys, won, rows, ALU.mult))

            def l3_out(p, following, ph="l3_out"):
                count[0] = 0
                dve.wait_ge(pass_done.sem, pass_done(ph, p, 1))
                step(V_.memset(gap[:], 0.0))
                chosen = small[0][:, 0:2 * T * E3].rearrange("p (t b e) -> p t b e", t=T, b=2)
                step(V_.tensor_copy(chosen, masks3[:, :, bass.ds(p * 2, 2), :]))
                settle(ph, p)
                for r in range(2):
                    dve.wait_ge(expert_psum.sem, expert_psum(ph, p, r + 1))
                    for e in range(E3):
                        for t in range(T):
                            o = pb[4 * r + 2 * t + e // 4][:, e % 4 * D:(e % 4 + 1) * D]
                            w, to = chosen[:, t, r, e:e + 1], pair_sum[:, r * T + t, :]
                            if e == 0:
                                step(V_.tensor_scalar(to, o, w, None, ALU.mult))
                            else:
                                step(V_.scalar_tensor_tensor(to, o, w, to, ALU.mult, ALU.add))
                        settle(ph, p)
                    if r == 0:
                        dve.wait_ge(expert_psum.sem, expert_psum(ph, p, 2))
                        step(V_.memset(gap[:], 0.0))
                        if following is not None:
                            take_pair(ph, following)
                end_pair(ph, p)

            V_.memset(ones[:], 1.0).then_inc(fixed_ready, 1)
            V_.memset(ones_e[:], 1.0).then_inc(fixed_ready, 1)
            V_.memset(minus_half[:], -0.5).then_inc(fixed_ready, 1)
            V_.memset(big[:, 0:2 * NG, :], 0.0).then_inc(stacks_clear, 1)
            dve.wait_ge(fixed_ready, 3)
            dve.wait_ge(ali_loaded, 16 * HPG)
            V_.tensor_copy(stack.rearrange("p g side n -> p (g side) n"), big[:, 0:2 * NG, :]).then_inc(stacks_clear, 1)
            dve.wait_ge(stacks_clear, 2)
            dve.wait_ge(x_loaded, 16)
            dve.wait_ge(silu_done, 1)
            dve.wait_ge(const_loaded, 16)
            V_.memset(gap[:], 0.0).then_inc(pass_done.sem, 1)
            dve.wait_ge(loaded[0], 16)
            plain_front(0, "l0_attn")
            with dve.Fori(0, B - 1) as b:
                plain_attn(b, "l0_attn", b + 1)
            plain_attn(B - 1, "l0_attn", None)
            dve.wait_ge(loaded[1], 16)
            dve.wait_ge(pass_done.sem, pass_done("l0_ffn", 0, 1))
            V_.memset(stack, 0.0).then_inc(stacks_clear, 1)
            dve.wait_ge(stacks_clear, 3)
            l0_front(0)
            with dve.Fori(0, B - 1) as b:
                l0_ffn(b, b + 1)
            l0_ffn(B - 1, None)
            dve.wait_ge(loaded[2], 16)
            l1_keep_counts()
            l1_attn_front(0)
            with dve.Fori(0, B - 1) as b:
                l1_attn(b, b + 1)
            l1_attn(B - 1, None)
            dve.wait_ge(loaded[3], 16)
            l1_front()
            with dve.Fori(0, PAIRS - 1) as p:
                l1_ffn(p, p + 1)
            l1_ffn(PAIRS - 1, None)
            dve.wait_ge(loaded[4], 16)
            plain_front(0, "l2_attn")
            with dve.Fori(0, B - 1) as b:
                plain_attn(b, "l2_attn", b + 1)
            plain_attn(B - 1, "l2_attn", None)
            dve.wait_ge(loaded[5], 16)
            l2_front()
            with dve.Fori(0, PAIRS - 1) as p:
                l2_ffn(p, p + 1)
            l2_ffn(PAIRS - 1, None)
            dve.wait_ge(loaded[6], 16)
            l3_front(0)
            with dve.Fori(0, B - 1) as b:
                l3_attn(b, b + 1)
            l3_attn(B - 1, None)
            dve.wait_ge(loaded[7], 16)
            l3_ffn()
            l3_route()
            take_pair_first("l3_ffn")
            with dve.Fori(0, PAIRS - 1) as p:
                l3_out(p, p + 1)
            l3_out(PAIRS - 1, None)

        @block.scalar
        def _(act):
            def wide_front(ph):
                act.wait_ge(wide_scaled.sem, wide_scaled(ph, 0, 1))
                for u in range(PAIRS):
                    act.wait_ge(wide_turned.sem, wide_turned(ph, 0, u + 1))
                    for i in range(2):
                        b = 2 * u + i
                        last = nc.scalar.activation(feats[:, b, :], pb[2 + u][:, i * S:(i + 1) * S], ACT.Identity,
                                                    bias=shift_8[:, b:b + 1], scale=scale_8[:, b:b + 1])
                    last.then_inc(wide_feat.sem, 1)

            def take_front(ph, b, n=1, width=P):
                act.wait_ge(front_turned.sem, front_turned(ph, b, n))
                nc.scalar.activation(next_feat[0:width, :], pb[5][0:width, 0:T * P], ACT.Copy).then_inc(front_feat.sem, 1)

            def take_out(ph, b, n=1):
                act.wait_ge(turned.sem, turned(ph, b, n))
                nc.scalar.activation(feat[:], pb[1][:, 0:T * P], ACT.Copy).then_inc(feat_ready.sem, 1)

            def exp(ph, b, h, blocks, first=False):
                act.wait_ge(max_ready.sem, max_ready(ph, b, h + 1))
                if h >= 3:
                    act.wait_ge(probsT_psum.sem, probsT_psum(ph, b, h - 2))
                elif not first:
                    act.wait_ge(probsT_psum.sem, probsT_psum(ph, b, 0))
                bank = pb[score_banks(ph)[h % len(score_banks(ph))]]
                for t, at, n in blocks:
                    last = nc.scalar.activation(probs[:, h % 3, at:at + n], bank[:, at:at + n], ACT.Exp,
                                                bias=nmax[:, h, t:t + 1], accum_out=rowsum[:, h, t:t + 1])
                last.then_inc(probs_ready.sem, 1)

            def exps(ph, b, blocks, following=None):
                for h in range(len(score_banks(ph)) if early(ph) else 0, H):
                    if following is not None and h == {"l0_ffn": 10, "l3_attn": 11}.get(ph, 5):
                        take_front(ph, following)
                    if following is not None and ph == "l0_ffn" and h == 15:
                        take_front(ph, following, 2, 64)
                    exp(ph, b, h, blocks, ph == "l3_attn" or following is None)

            def first_exps(ph, b, first=False):
                for h in range(len(score_banks(ph))):
                    exp(ph, b, h, CAUSAL, first)

            def plain_front(b, ph):
                take_front(ph, b)
                first_exps(ph, b, True)

            def plain_attn(b, ph, following):
                exps(ph, b, CAUSAL, following)
                take_out(ph, b)
                if following is not None:
                    first_exps(ph, following)

            def l0_front(b, ph="l0_ffn"):
                take_front(ph, b)
                take_front(ph, b, 2, 64)

            def l0_ffn(b, following, ph="l0_ffn"):
                exps(ph, b, CAUSAL, following)
                take_out(ph, b)
                take_out(ph, b, 2)
                for n in range(2 * E0):
                    e, u = n // 2, n % 2
                    act.wait_ge(hid_psum.sem, hid_psum(ph, b, n + 1))
                    if e >= 2:
                        act.wait_ge(expert_psum.sem, expert_psum(ph, b, e - 1))
                    for c in range(2):
                        at = e * C0 + 2 * u + c
                        last = nc.scalar.activation(hid[:, e % 2, 2 * u + c, :], pb[2 + n % 3][:, c * S:(c + 1) * S], ACT.Relu,
                                                    bias=W(ph, "b1")[:, at:at + 1])
                    last.then_inc(hid_ready.sem, 1)

            def l1_exps(ph, b, h):
                act.wait_ge(max_ready.sem, max_ready(ph, b, h + 1))
                bank = pb[score_banks(ph)[h % len(score_banks(ph))]]
                for t in range(T):
                    last = nc.scalar.activation(big[:, h * T + t, :], bank[:, t * S:(t + 1) * S], ACT.Exp,
                                                bias=nmax[:, h, t:t + 1], accum_out=rowsum[:, h, t:t + 1])
                last.then_inc(probs_ready.sem, 1)

            def l1_attn_front(b, ph="l1_attn"):
                take_front(ph, b)
                for h in range(H):
                    l1_exps(ph, b, h)

            def l1_attn(b, following, ph="l1_attn"):
                for it in range(QUICK_STEPS):
                    act.wait_ge(mid_ready.sem, mid_ready(ph, b, 1) + it)
                    for j in range(ROWS_DVE, ROWS1):
                        last = nc.scalar.activation(signs[j - ROWS_DVE], big[:, j, :], ACT.Sign, bias=neg_mid[:, j:j + 1],
                                                    accum_out=tried[:, 1, j:j + 1])
                    last.then_inc(counts_act.sem, 1)
                if following is not None:
                    take_front(ph, following)
                for h in range(H):
                    act.wait_ge(probsT_psum.sem, probsT_psum(ph, b, h + 1))
                    if h >= 2:
                        act.wait_ge(pv_done.sem, pv_done(ph, b, h - 1))
                    nc.scalar.activation(probsT[:, h % 2, :], pb[6 + h % 2][:], ACT.Copy).then_inc(probsT_ready.sem, 1)
                    if following is not None:
                        l1_exps(ph, following, h)
                take_out(ph, b)

            def l1_front(ph="l1_ffn"):
                wide_front(ph)
                act.wait_ge(max_route, 1)
                nc.scalar.activation(rows(10, 2), rows(8, 2), ACT.Exp).then_inc(exp_route, 1)

            def l1_ffn(p, ph="l1_ffn"):
                for e in range(EA):
                    act.wait_ge(hid_psum.sem, hid_psum(ph, p, e + 1))
                    act.wait_ge(hid_ready.sem, hid_ready(ph, p, e - 1))
                    nc.scalar.activation(silus(e), pb[(2, 4, 0)[e % 3]][:], ACT.Silu).then_inc(silu_g.sem, 1)

            def l2_front(ph="l2_ffn"):
                wide_front(ph)
                act.wait_ge(delta_ready, 1)
                nc.scalar.activation(rows(14, 1), rows(13, 1), ACT.Sqrt).then_inc(root_ready, 1)
                for u in range(PAIRS):
                    act.wait_ge(mix_turned, u + 1)
                    nc.scalar.activation(mix_T(u), pb[2 + u][0:E2, :], ACT.Copy).then_inc(mix_feat, 1)
                for u in range(PAIRS):
                    act.wait_ge(ranks_psum, u + 1)
                    nc.scalar.activation(rows(20 + 2 * u, 2), pb[2 + u][:], ACT.Copy).then_inc(ranks_ready, 1)

            def l2_ffn(p, ph="l2_ffn"):
                act.wait_ge(z_psum.sem, z_psum(ph, p, 0))
                for c in range(O2):
                    act.wait_ge(hid_psum.sem, hid_psum(ph, p, c + 1))
                    nc.scalar.activation(gelus(c), pb[2 + c][:], ACT.Gelu).then_inc(hid_ready.sem, 1)

            def l3_values(ph, b):
                for t in range(T):
                    act.wait_ge(v_psum.sem, v_psum(ph, b, t + 1))
                    for j in range(2):
                        last = nc.scalar.activation(V[:, t, j * 512:(j + 1) * 512], pb[6 + j][:], ACT.Copy)
                    last.then_inc(v_ready.sem, 1)

            def l3_front(b, ph="l3_attn"):
                take_front(ph, b)
                l3_values(ph, b)

            def l3_attn(b, following, ph="l3_attn"):
                exps(ph, b, FULL, following)
                for u in range(4):
                    act.wait_ge(o_turned.sem, o_turned(ph, b, u + 1))
                    nc.scalar.activation(feat_o[:, 2 * u:2 * u + 2, :], pb[(6 + u) % 8][:].rearrange("p (c n) -> p c n", c=2), ACT.Copy).then_inc(o_feat.sem, 1)
                if following is not None:
                    l3_values(ph, following)

            act.wait_ge(c_loaded, 16)
            nc.scalar.activation(silu_c[:], silu_c[:], ACT.Silu).then_inc(silu_done, 1)
            plain_front(0, "l0_attn")
            with act.Fori(0, B - 1) as b:
                plain_attn(b, "l0_attn", b + 1)
            plain_attn(B - 1, "l0_attn", None)
            act.wait_ge(loaded[1], 16)
            l0_front(0)
            with act.Fori(0, B - 1) as b:
                l0_ffn(b, b + 1)
            l0_ffn(B - 1, None)
            act.wait_ge(keep_exp, 1)
            nc.scalar.activation(small[1][:, 0:H], small[0][:, 0:H], ACT.Exp, scale=-1.0).then_inc(keep_exped, 1)
            l1_attn_front(0)
            with act.Fori(0, B - 1) as b:
                l1_attn(b, b + 1)
            l1_attn(B - 1, None)
            l1_front()
            with act.Fori(0, PAIRS) as p:
                l1_ffn(p)
            plain_front(0, "l2_attn")
            with act.Fori(0, B - 1) as b:
                plain_attn(b, "l2_attn", b + 1)
            plain_attn(B - 1, "l2_attn", None)
            l2_front()
            with act.Fori(0, PAIRS) as p:
                l2_ffn(p)
            l3_front(0)
            with act.Fori(0, B - 1) as b:
                l3_attn(b, b + 1)
            l3_attn(B - 1, None)
            wide_front("l3_ffn")


def shape_constants():
    out = {"ident": np.eye(P)}
    row = np.arange(P)
    out["first"] = np.tile(np.arange(E0, 0, -1.0), (P, 1))
    out["order8"] = np.tile(np.arange(LEFT), (P, 1))
    k = np.arange(1, E2 + 1)
    out["karange"], out["kinv"] = np.tile(k, (P, 1)), np.tile(1.0 / k, (P, 1))
    out["expert1"] = (row % E3 + 1)[:, None]
    return out


def alibi_rows():
    slope = (2.0 ** (-8.0 / H * (np.arange(H) + 1))).astype(np.float32)
    part = []
    for _ in range(PARTS):
        part.append((slope.view(np.uint32) & np.uint32(0xFFFF0000)).view(np.float32))
        slope = slope - part[-1]
    pos = np.arange(S, dtype=np.float32)
    out = np.zeros((HPG, ALI_ROWS, NG, 2, S), np.float32)
    for u in range(PARTS):
        by_head = part[u].reshape(NG, HPG).T[:, :, None]
        out[:, u, :, 0], out[:, u, :, 1] = by_head, pos
        out[:, PARTS + u, :, 0], out[:, PARTS + u, :, 1] = -pos, by_head
    return out.reshape(HPG, ALI_ROWS, -1)


def rope_tables(angle, dim, half, scale):
    inside = dim >= 0
    sign = np.where(dim % (2 * half) < half, -1.0, 1.0)[:, None]
    cos, sin = np.cos(angle) * inside[:, None], np.sin(angle) * sign * inside[:, None]
    return {"cosq": cos * scale, "sinq": sin * scale, "cosk": cos, "sink": sin}


def rope_small():
    dim = np.arange(P) // HALF % HD
    inv = (1.0 / 10000.0 ** (np.arange(HD // 2, dtype=np.float32) / np.float32(HD // 2))).astype(np.float32)
    angle = (np.arange(S, dtype=np.float32)[None, :] * inv[dim % (HD // 2)][:, None]).astype(np.float64)
    return rope_tables(angle, dim, HD // 2, HD ** -0.5)


def rope_wide():
    dim = np.arange(P) % HD3
    inv = (1.0 / np.float32(10000.0) ** (np.arange(0, HD3, 2, dtype=np.float32) / HD3)).astype(np.float32)
    pos = np.maximum(np.arange(S) - 1, 0).astype(np.float32)
    angle = (pos[None, :] * inv[dim % (HD3 // 2)][:, None]).astype(np.float64)
    return rope_tables(angle, dim, HD3 // 2, HD3 ** -0.5)


def by_dimension(w):
    return w.reshape(-1, 2, HALF, HPG, HD).transpose(0, 3, 1, 4, 2).reshape(w.shape[0], -1)


def column(v):
    return by_dimension(v[None, :]).T


def swap_halves(w, width):
    n = w.shape[0]
    return w.reshape(n, -1, 2, width // 2)[:, :, ::-1].reshape(n, -1)


def everywhere(v):
    return np.broadcast_to(v[None, :], (P, v.shape[0]))


def laid_out(a):
    attn0 = lambda wq, wk, wv, bq, bk, bv, wo, bo: {
        "wq": by_dimension(wq), "wk": by_dimension(wk), "wv": wv, "bq": column(bq), "bk": column(bk),
        "bv": everywhere(bv), "wo": wo, "bo": everywhere(bo)}
    w, b = a["L0_attn_W_qkv"], a["L0_attn_b_qkv"]
    out = {"l0_attn": attn0(w[:, :D], w[:, D:2 * D], w[:, 2 * D:], b[:D], b[D:2 * D], b[2 * D:], a["L0_attn_W_out"], a["L0_attn_b_out"])}
    f = lambda n: a["L0_ffn_" + n]
    out["l0_ffn"] = {
        "n1": everywhere(f("norm1_w")), "n2": everywhere(f("norm2_w")),
        "wq": by_dimension(f("Wq").T), "wqr": by_dimension(swap_halves(f("Wq").T, HD)), "wdkv": f("Wdkv").T,
        "lng": everywhere(f("ln_g")), "lnb": everywhere(f("ln_b")),
        "wuk": by_dimension(f("Wuk").T), "wukr": by_dimension(swap_halves(f("Wuk").T, HD)), "wuv": f("Wuv").T, "wo": f("Wo").T,
        "gate": f("gate_w").T, "gateb": everywhere(f("gate_b")),
        "w1": f("W1").transpose(2, 0, 1).reshape(D, -1), "b1": f("b1").reshape(E0 * C0, P).T,
        "w2": f("W2").reshape(E0, D, C0, P).transpose(3, 0, 2, 1).reshape(P, -1), "b2": f("b2").reshape(1, -1)}
    f = lambda n: a["L1_attn_" + n]
    out["l1_attn"] = attn0(f("Wq").T, f("Wk").T, f("Wv").T, f("bq"), f("bk"), f("bv"), f("Wo").T, f("bo"))
    out["l1_attn"].update(ema=everywhere(f("entropy_ema")), thr=everywhere(f("entropy_threshold")))
    f = lambda n: a["L1_ffn_" + n]
    out["l1_ffn"] = {
        "router": f("router_w").T, "routerb": everywhere(f("router_bias")),
        "gate": np.concatenate([f("gate_w").transpose(2, 0, 1).reshape(D, -1), f("sgate_w").T], 1),
        "up": np.concatenate([f("up_w").transpose(2, 0, 1).reshape(D, -1), f("sup_w").T], 1),
        "down": np.concatenate([f("down_w").transpose(2, 0, 1).reshape(P, -1),
                                f("sdown_w").reshape(D, SH1, P).transpose(2, 1, 0).reshape(P, -1)], 1)}
    f = lambda n: a["L2_attn_" + n]
    out["l2_attn"] = attn0(f("wq"), f("wk"), f("wv"), f("bq"), f("bk"), f("bv"), f("wo"), f("bo"))
    f = lambda n: a["L2_ffn_" + n]
    out["l2_ffn"] = {
        "proj": f("proj"), "c12": np.concatenate([f("C1"), f("C2")], 1), "win1": f("Win1")[:D], "win1b": f("Win1")[D:].T,
        "wout1": f("Wout1").T,
        "win2": second_half(f("Win2")[:O2 * P].reshape(O2, P, R2).transpose(1, 0, 2), 2).reshape(P, -1),
        "win2b": second_half(f("Win2")[O2 * P:].T, 0), "wout2": second_half(f("Wout2").T, 0)}
    w = a["L3_attn_w_qkv"]
    n = H * HD3
    four = [w[:, :n], swap_halves(w[:, :n], HD3), w[:, n:2 * n], swap_halves(w[:, n:2 * n], HD3)]
    out["l3_attn"] = {
        "gamma": everywhere(a["L3_attn_ln_gamma"]), "beta": everywhere(a["L3_attn_ln_beta"]),
        "wqk": np.stack([v.reshape(D, NG3, P) for v in four], 2).reshape(D, -1), "wv": w[:, 2 * n:],
        "wo": a["L3_attn_w_out"].reshape(NG3, P, D).transpose(1, 0, 2).reshape(P, -1)}
    out["l3_ffn"] = {"gate": a["L3_ffn_gate_w"][0], "experts": a["L3_ffn_experts"].transpose(1, 0, 2).reshape(D, -1)}
    for i, ph in enumerate(WEIGHED):
        half = a[f"L{i // 2}_wmod"]
        out[ph]["wmod"] = half[:, :3 * D] if i % 2 == 0 else half[:, 3 * D:]
    out["l0_ffn"].update(rope_small())
    out["l3_attn"].update(rope_wide())
    return out


def second_half(a, axis):
    return np.concatenate([np.zeros_like(a), a], axis)


def side_by_side(cols, parts):
    at, n = offsets(cols)
    out = np.zeros((P, n), np.float32)
    for name, (first, width) in at.items():
        part = parts[name]
        assert part.shape[1] == width, (name, part.shape, width)
        out[:part.shape[0], first:first + width] = part
    return out


def kernel(**inputs):
    import concourse.bacc as bacc
    from concourse.bass_utils import run_bass_kernel_spmd

    a = {k: np.asarray(v) for k, v in inputs.items()}
    arrays = {"x": np.ascontiguousarray(a["L0_attn_x"]),
              "c": np.ascontiguousarray(np.stack([a[f"L{i}_c"] for i in range(4)]).reshape(4 * B, D).T),
              "const": side_by_side(CONSTS, shape_constants())}
    arrays["ali"] = alibi_rows()
    weights = laid_out(a)
    for ph in WEIGHED:
        arrays["weights_" + ph] = side_by_side(COLUMNS[ph], weights[ph])
    nc = bacc.Bacc("TRN2", target_bir_lowering=False, num_devices=1)
    dram = {k: nc.dram_tensor("in_" + k, v.shape, F32, kind="ExternalInput").ap() for k, v in arrays.items()}
    out = nc.dram_tensor("out", (B, S, D), F32, kind="ExternalOutput").ap()
    adaln_program(nc, dram["x"], dram["c"], dram["const"], dram["ali"], {ph: dram["weights_" + ph] for ph in WEIGHED}, out)
    r = run_bass_kernel_spmd(nc, [{"in_" + k: v for k, v in arrays.items()}], core_ids=[0])
    return r.results[0]["out"]
```
